# Optimizing a Trainium2 kernel written in Bass

```python
import numpy as np
import jax
import jax.numpy as jnp

def _softmax(x, axis=-1):
    return jax.nn.softmax(x, axis=axis)

def _gelu(x):
    return jax.nn.gelu(x, approximate=True)

def _silu(x):
    return jax.nn.silu(x)

def _sigmoid(x):
    return jax.nn.sigmoid(x)

def _layernorm(x, axis=-1, eps=1e-05):
    m = jnp.mean(x, axis=axis, keepdims=True)
    v = jnp.var(x, axis=axis, keepdims=True)
    return (x - m) / jnp.sqrt(v + eps)

def _scatter_add(tgt, idx, src, axis=0):
    return tgt.at[idx].add(src)

def _segment_sum(src, seg, n):
    return jax.ops.segment_sum(src, seg, n)
kernel_name = 'mk_gnn_resnorm_d4_gnn_r32_0bece4'

def setup_inputs(seed: int=0):
    np.random.seed(seed)
    _w = jnp.asarray

    def _rec_inputs():
        import jax
        import jax.numpy as jnp
        _gk = jax.random.key(seed)
        x = -0.0001006 + 1 * jax.random.normal(jax.random.fold_in(_gk, 1), (50000, 96), jnp.float32)
        src = jax.random.randint(jax.random.fold_in(_gk, 2), (50000,), 0, 50000, jnp.int32)
        dst = jnp.minimum((50000 * jax.random.uniform(jax.random.fold_in(_gk, 3), (50000,)) ** 2.0).astype(jnp.int32), 49999)
        _o = jnp.argsort(dst, stable=True)
        src = src[_o]
        dst = dst[_o]
        edge_attr_96 = 5.93493e-05 + 1.00006 * jax.random.normal(jax.random.fold_in(_gk, 12), (50000, 96), jnp.float32)
        edge_weight = jax.random.uniform(jax.random.fold_in(_gk, 14), (50000,), jnp.float32, 0.0, 1)
        return (x, src, dst, edge_attr_96, edge_weight)
    x, src, dst, edge_attr_96, edge_weight = _rec_inputs()

    def _L0_gnn_setup():
        import jax, jax.numpy as jnp
        import numpy as np
        N_NODES = 50000
        N_EDGES = 25000
        D = 96

        def _gconv(x, W, W_loop, b, edge_src, edge_dst, edge_weight):
            support = x @ W
            msg = support[edge_src] * edge_weight[:, None]
            agg = jax.ops.segment_sum(msg, edge_dst, num_segments=N_NODES)
            return agg + x @ W_loop + b
        key = jax.random.key(seed)
        ks = jax.random.split(key, 10)
        s = 1.0 / np.sqrt(D)
        x = jax.random.normal(ks[0], (N_NODES, D), dtype=jnp.float32)
        W1 = jax.random.normal(ks[1], (D, D), dtype=jnp.float32) * s
        W1_loop = jax.random.normal(ks[2], (D, D), dtype=jnp.float32) * s
        b1 = jnp.zeros((D,), dtype=jnp.float32)
        W2 = jax.random.normal(ks[3], (D, D), dtype=jnp.float32) * s
        W2_loop = jax.random.normal(ks[4], (D, D), dtype=jnp.float32) * s
        b2 = jnp.zeros((D,), dtype=jnp.float32)
        edge_weight = jax.random.uniform(ks[5], (N_EDGES,), dtype=jnp.float32)
        edge_src = jax.random.randint(ks[6], (N_EDGES,), 0, N_NODES, dtype=jnp.int64 if jax.config.jax_enable_x64 else jnp.int32)
        edge_dst = jax.random.randint(ks[7], (N_EDGES,), 0, N_NODES, dtype=jnp.int64 if jax.config.jax_enable_x64 else jnp.int32)
        return {'x': x, 'W1': W1, 'W1_loop': W1_loop, 'b1': b1, 'W2': W2, 'W2_loop': W2_loop, 'b2': b2, 'edge_weight': edge_weight, 'edge_src': edge_src, 'edge_dst': edge_dst}
    _L0_gnn_all = _L0_gnn_setup()
    _L0_gnn_in = {k: v for k, v in _L0_gnn_all.items() if k in ('W1', 'W1_loop', 'b1', 'W2', 'W2_loop', 'b2')}
    del _L0_gnn_all

    def _L1_gnn_setup():
        import jax, jax.numpy as jnp
        import numpy as np
        N_NODES = 50000
        N_EDGES = 25000
        IN_DIM = 96
        NUM_HEADS = 8
        HEAD_DIM = IN_DIM // NUM_HEADS
        key = jax.random.key(seed)
        ks = jax.random.split(key, 11)
        s = 1.0 / np.sqrt(IN_DIM)
        return {'x': jax.random.normal(ks[0], (N_NODES, IN_DIM), dtype=jnp.float32), 'edge_index': jax.random.randint(ks[1], (2, N_EDGES), 0, N_NODES, dtype=jnp.int64), 'edge_attr': jax.random.normal(ks[2], (N_EDGES, IN_DIM), dtype=jnp.float32), 'Wq': jax.random.normal(ks[3], (IN_DIM, IN_DIM), dtype=jnp.float32) * s, 'bq': jax.random.normal(ks[4], (IN_DIM,), dtype=jnp.float32) * s, 'Wk': jax.random.normal(ks[5], (IN_DIM, IN_DIM), dtype=jnp.float32) * s, 'bk': jax.random.normal(ks[6], (IN_DIM,), dtype=jnp.float32) * s, 'We': jax.random.normal(ks[7], (IN_DIM, IN_DIM), dtype=jnp.float32) * s, 'be': jax.random.normal(ks[8], (IN_DIM,), dtype=jnp.float32) * s, 'Wv': jax.random.normal(ks[9], (IN_DIM, IN_DIM), dtype=jnp.float32) * s, 'bv': jax.random.normal(ks[10], (IN_DIM,), dtype=jnp.float32) * s}
    _L1_gnn_all = _L1_gnn_setup()
    _L1_gnn_in = {k: v for k, v in _L1_gnn_all.items() if k in ('Wq', 'bq', 'Wk', 'bk', 'We', 'be', 'Wv', 'bv')}
    del _L1_gnn_all

    def _L2_gnn_setup():
        import jax, jax.numpy as jnp
        import numpy as np
        N_NODES = 50000
        EPS = 0.0
        key = jax.random.key(seed)
        k1, k2, k3, k4, k5 = jax.random.split(key, 5)
        d = 96
        E = 25000
        feat = jax.random.normal(k1, (N_NODES, d), dtype=jnp.float32)
        W1 = jax.random.normal(k2, (d, d), dtype=jnp.float32) * (1.0 / np.sqrt(d))
        b1 = jnp.zeros((d,), dtype=jnp.float32)
        W2 = jax.random.normal(k3, (d, d), dtype=jnp.float32) * (1.0 / np.sqrt(d))
        b2 = jnp.zeros((d,), dtype=jnp.float32)
        edge_src = jax.random.randint(k4, (E,), 0, N_NODES, dtype=jnp.int64)
        edge_dst = jax.random.randint(k5, (E,), 0, N_NODES, dtype=jnp.int64)
        return {'feat': feat, 'W1': W1, 'b1': b1, 'W2': W2, 'b2': b2, 'edge_src': edge_src, 'edge_dst': edge_dst}
    _L2_gnn_all = _L2_gnn_setup()
    _L2_gnn_in = {k: v for k, v in _L2_gnn_all.items() if k in ('W1', 'b1', 'W2', 'b2')}
    del _L2_gnn_all

    def _L3_gnn_setup():
        import jax, jax.numpy as jnp
        import numpy as np
        N_NODES = 50000
        N_EDGES = 25000
        D_FEAT = 96
        L = 0.5
        key = jax.random.key(seed)
        k1, k2, k3 = jax.random.split(key, 3)
        h = jax.random.normal(k1, (N_NODES, D_FEAT), dtype=jnp.float32)
        src = jax.random.randint(k2, (N_EDGES,), 0, N_NODES, dtype=jnp.int64)
        dst = jax.random.randint(k3, (N_EDGES,), 0, N_NODES, dtype=jnp.int64)
        return {'h': h, 'src': src, 'dst': dst}
    _L3_gnn_all = _L3_gnn_setup()
    _L3_gnn_in = {k: v for k, v in _L3_gnn_all.items() if k in ()}
    del _L3_gnn_all
    return {'x': x, 'src': src, 'dst': dst, 'edge_attr_96': edge_attr_96, 'edge_weight': edge_weight, 'L0_gnn_W1': _L0_gnn_in['W1'], 'L0_gnn_W1_loop': _L0_gnn_in['W1_loop'], 'L0_gnn_b1': _L0_gnn_in['b1'], 'L0_gnn_W2': _L0_gnn_in['W2'], 'L0_gnn_W2_loop': _L0_gnn_in['W2_loop'], 'L0_gnn_b2': _L0_gnn_in['b2'], 'L1_gnn_Wq': _L1_gnn_in['Wq'], 'L1_gnn_bq': _L1_gnn_in['bq'], 'L1_gnn_Wk': _L1_gnn_in['Wk'], 'L1_gnn_bk': _L1_gnn_in['bk'], 'L1_gnn_We': _L1_gnn_in['We'], 'L1_gnn_be': _L1_gnn_in['be'], 'L1_gnn_Wv': _L1_gnn_in['Wv'], 'L1_gnn_bv': _L1_gnn_in['bv'], 'L2_gnn_W1': _L2_gnn_in['W1'], 'L2_gnn_b1': _L2_gnn_in['b1'], 'L2_gnn_W2': _L2_gnn_in['W2'], 'L2_gnn_b2': _L2_gnn_in['b2']}

def reference(x, src, dst, edge_attr_96, edge_weight, L0_gnn_W1, L0_gnn_W1_loop, L0_gnn_b1, L0_gnn_W2, L0_gnn_W2_loop, L0_gnn_b2, L1_gnn_Wq, L1_gnn_bq, L1_gnn_Wk, L1_gnn_bk, L1_gnn_We, L1_gnn_be, L1_gnn_Wv, L1_gnn_bv, L2_gnn_W1, L2_gnn_b1, L2_gnn_W2, L2_gnn_b2):
    import jax
    import jax.numpy as jnp

    def _L0_gnn_ref(x, W1, W1_loop, b1, W2, W2_loop, b2, edge_weight, edge_src, edge_dst):
        import jax, jax.numpy as jnp
        import numpy as np
        N_NODES = 50000
        N_EDGES = 25000
        D = 96

        def _gconv(x, W, W_loop, b, edge_src, edge_dst, edge_weight):
            support = x @ W
            msg = support[edge_src] * edge_weight[:, None]
            agg = jax.ops.segment_sum(msg, edge_dst, num_segments=N_NODES)
            return agg + x @ W_loop + b
        h = jax.nn.relu(_gconv(x, W1, W1_loop, b1, edge_src, edge_dst, edge_weight))
        h = jax.nn.relu(_gconv(h, W2, W2_loop, b2, edge_src, edge_dst, edge_weight))
        return (x + h) * 0.5

    def _L1_gnn_ref(x, edge_index, edge_attr, Wq, bq, Wk, bk, We, be, Wv, bv):
        import jax, jax.numpy as jnp
        import numpy as np
        N_NODES = 50000
        N_EDGES = 25000
        IN_DIM = 96
        NUM_HEADS = 8
        HEAD_DIM = IN_DIM // NUM_HEADS
        N = x.shape[0]
        H, D = (NUM_HEADS, HEAD_DIM)
        Q_h = (x @ Wq + bq).reshape(N, H, D)
        K_h = (x @ Wk + bk).reshape(N, H, D)
        V_h = (x @ Wv + bv).reshape(N, H, D)
        E = (edge_attr @ We + be).reshape(-1, H, D)
        src_idx = edge_index[0]
        dst_idx = edge_index[1]
        src = K_h[src_idx]
        dest = Q_h[dst_idx]
        score = src * dest / jnp.sqrt(jnp.asarray(D, x.dtype))
        score = score * E
        score = jnp.exp(jnp.clip(score.sum(-1, keepdims=True), -5.0, 5.0))
        msg = V_h[src_idx] * score
        wV = jax.ops.segment_sum(msg, dst_idx, num_segments=N)
        Z = jax.ops.segment_sum(score, dst_idx, num_segments=N)
        h_out = wV / (Z + 1e-06)
        return h_out.reshape(N, H * D)

    def _L2_gnn_ref(feat, W1, b1, W2, b2, edge_src, edge_dst):
        import jax, jax.numpy as jnp
        import numpy as np
        N_NODES = 50000
        EPS = 0.0
        msg = feat[edge_src]
        neigh = jax.ops.segment_sum(msg, edge_dst, num_segments=N_NODES)
        rst = (1.0 + EPS) * feat + neigh
        h = jax.nn.relu(rst @ W1 + b1)
        out = h @ W2 + b2
        return out

    def _L3_gnn_ref(h, src, dst):
        import jax, jax.numpy as jnp
        import numpy as np
        N_NODES = 50000
        N_EDGES = 25000
        D_FEAT = 96
        L = 0.5
        N = h.shape[0]
        deg = jax.ops.segment_sum(jnp.ones_like(dst, dtype=h.dtype), dst, num_segments=N)
        inv_deg = (1.0 / jnp.maximum(deg, 1.0))[:, None]

        def mean_agg(x):
            msg_sum = jax.ops.segment_sum(x[src], dst, num_segments=N)
            return msg_sum * inv_deg
        neigh1 = mean_agg(h)
        neigh2 = mean_agg(neigh1)
        return L * neigh1 + (1.0 - L) * neigh2
    edge_index = jnp.stack([src, dst])
    x = _layernorm(x + _L0_gnn_ref(x, L0_gnn_W1, L0_gnn_W1_loop, L0_gnn_b1, L0_gnn_W2, L0_gnn_W2_loop, L0_gnn_b2, edge_weight, src, dst), axis=-1)
    x = _layernorm(x + _L1_gnn_ref(x, edge_index, edge_attr_96, L1_gnn_Wq, L1_gnn_bq, L1_gnn_Wk, L1_gnn_bk, L1_gnn_We, L1_gnn_be, L1_gnn_Wv, L1_gnn_bv), axis=-1)
    x = _layernorm(x + _L2_gnn_ref(x, L2_gnn_W1, L2_gnn_b1, L2_gnn_W2, L2_gnn_b2, src, dst), axis=-1)
    x = _layernorm(x + _L3_gnn_ref(x, src, dst), axis=-1)
    return x

_drawn_inputs = setup_inputs


def setup_inputs(seed=0):
    import zlib

    import numpy as np

    out = dict(_drawn_inputs(seed))
    spreads = {'L0_gnn_b1': (0.0, 0.415),
     'L0_gnn_b2': (0.0, 0.314),
     'L2_gnn_b1': (0.0, 0.1),
     'L2_gnn_b2': (0.0, 0.1)}
    factors = {'L1_gnn_bq': 5.282, 'L1_gnn_bk': 5.422, 'L1_gnn_be': 4.626}
    for name, (base, spread) in spreads.items():
        noise = np.random.default_rng([zlib.crc32(name.encode()), seed]).standard_normal(out[name].shape)
        drawn = base * np.exp(spread * noise) if base else spread * noise
        out[name] = jnp.asarray(drawn.astype(out[name].dtype))
    for name, factor in factors.items():
        out[name] = (out[name] * factor).astype(out[name].dtype)
    return out
```

```python
from contextlib import ExitStack

import concourse.bass as bass
from concourse import mybir

F32 = mybir.dt.float32
I32 = mybir.dt.int32
BF16 = mybir.dt.bfloat16
ALU = mybir.AluOpType
ACT = mybir.ActivationFunctionType
AX = mybir.AxisListType

P = 128
T = 4
GR = P * T
EPS = 1e-5
FAR = 1 << 20
PAD = 1 << 16

SRC, DST, WEIGHT, END_DST, START_DST, SLOT, FIRST, INV_DEG, IS_END, HALF_INV = range(10)
NF = 10

ENGINE_SIGNALS = {
    "A": dict(weighted=1, scanned=1, src_turned=1, own_turned=1, own_cols=1, conv_done=1, conv_out=1,
              x_turned=1, x_cols=1, loop1_done=1, h_rows=1, h_turned=1, h_cols=1, loop2_done=1, y1=2,
              ln1_dve=7, ln1_act=2, ln2_dve=7, ln2_act=3, ln3_dve=7, ln3_act=3, ln4_dve=7, ln4_act=2,
              x2_turned=1, x2_cols=1, mlp1_done=1, mlp_hidden=1, mlp2_done=1, y2=1),
    "B": dict(ids_made=2),
    "C": dict(weighted=1, scanned=1, src_turned=1, own_turned=1, own_cols=1, conv_done=1, y1=2,
              ln1_dve=8, ln1_act=3),
    "D": dict(src_turned=1, own_turned=1, edge_turned=1, src_cols=1, edge_cols=1, filled=1,
              k_done=1, q_done=1, e_done=1, v_done=1, k_cols=1, score=2, sum_done=1, clipped=1,
              exped=1, msg=1, scanned=1, z_scanned=1, attn=4, y_turned=1, ln1_dve=7, ln1_act=3),
    "E": dict(src_turned=1, own_turned=1, scanned=1, rst=1, mlp1_done=1, mlp_hidden=1, mlp2_done=1,
              y2=1, ln1_dve=7, ln1_act=3),
    "F": dict(src_turned=1, scanned=1, y_turned=1, conv_out=1),
    "G": dict(src_turned=1, scanned=1, y_turned=1, y1=1, y2=1, ln1_dve=7, ln1_act=3),
}
DMA_SIGNALS = {
    "A": dict(meta_in=2, x_in=1, ids_out=4, src_in=4, own_in=4, own_out=1, conv_stored=1, h_stored=1,
              x1_stored=1, x2_stored=1, x3_stored=2),
    "B": dict(meta_in=1, src_in=4, ids_stored=1),
    "C": dict(meta_in=3, x_in=2, src_in=4, x1_stored=1),
    "D": dict(meta_in=2, x_in=1, edge_in=1, src_in=4, x1_stored=1),
    "E": dict(meta_in=2, x_in=1, src_in=4, x1_stored=1),
    "F": dict(meta_in=3, src_in=4, x1_stored=1),
    "G": dict(meta_in=3, x_in=2, src_in=4, ids_out=4),
}
PHASES = "ABCDEFG"


class Signal:

    def __init__(self, sem, base):
        self.sem, self.base = sem, base

    def at(self, count):
        return self.base + count


class Step:

    def __init__(self, g, s, h):
        self.g, self.s, self.h = g, s, h
        self.again = not isinstance(g, int) or g >= 2


def after(g, n):
    return not isinstance(g, int) or g >= n


def ticks(eng, groups, delay, body):
    warm = delay + 2 + delay % 2

    def tick(n, u, j):
        def at(k):
            s = (u - k) % 2
            g = n - k
            if isinstance(g, int) and not 0 <= g < groups:
                return None
            return Step(g, s, j + (u - k - s) // 2)

        body(at)

    for n in range(warm):
        tick(n, n % 2, n // 2)
    with eng.Fori(warm // 2, groups // 2 - 1) as j:
        for u in range(2):
            tick(2 * j + u, u, j)
    for n in range(groups - 2, groups + delay):
        tick(n, n % 2, n // 2)


def gnn_kernel(nc, a, out):
    N, D = a["x"].shape
    E = a["src"].shape[0]
    NG = -(-E // GR)
    NG += NG % 2
    EP = NG * GR
    C = EP // P
    NLAST = N - (NG - 1) * GR
    HEADS = 8
    HD = D // HEADS
    CHUNKS = 16
    CH = EP // CHUNKS
    assert N == E and 0 < NLAST <= GR and NLAST % T == 0 and D < P

    def dram(name, shape, dt=F32):
        return nc.dram_tensor(name, shape, dt, kind="Internal").ap()

    edges = dram("edges", (EP + 2, 4), I32)
    dst_list = dram("dst_list", (EP,), I32)
    edges2 = dram("edges2", (EP + 1, D))
    edge_rows = dram("edge_rows", (EP, D))
    meta_t = dram("meta_t", (EP, NF), I32)
    flags_f = dram("flags_f", (EP,), BF16)
    flags_b = dram("flags_b", (EP,), BF16)
    place = dram("place", (EP, 2), I32)
    source = dram("source", (EP, 4), I32)
    x_own = dram("x_own", (EP, D))
    h_t = dram("h_t", (2 * EP, D))
    x1_t = dram("x1_t", (2 * EP, D))
    x2_t = dram("x2_t", (2 * EP, D))
    x3_t = dram("x3_t", (2 * EP, D))
    mean_t = dram("mean_t", (EP + 1, D))

    def groups(t):
        return t.rearrange("(g p t) d -> g p (t d)", p=P, t=T)

    nodes_in = a["x"][0:(NG - 1) * GR, :]
    nodes_out = out[0:(NG - 1) * GR, :]

    with ExitStack() as ctx:
        def sb(name, shape, dt=F32):
            return ctx.enter_context(nc.sbuf_tensor(name, shape, dt))

        def sem(name):
            return ctx.enter_context(nc.semaphore(name))

        row_tiles = [sb(f"rows{i}", [P, 2, T, D]) for i in range(13)]
        col_tiles = [sb(f"cols{i}", [D + 1, 2, GR]) for i in range(9)]
        meta = sb("meta", [P, 2, T, NF], I32)
        srcs = sb("srcs", [P, 2, T, 4], I32)
        ids = sb("ids", [P, 2, T, 2], I32)
        flag = sb("flag", [D, 2, GR], BF16)
        ln_tiles = [(sb(f"ln_st{i}", [P, 2, T, 6]), sb(f"ln_mv{i}", [P, 2, T, 2]), sb(f"ln_s{i}", [P, 2, 7, T]))
                    for i in range(4)]
        ident = sb("ident", [P, P])
        ones = sb("ones", [P, P])
        head_sum = sb("head_sum", [D, D])
        w = {n: sb(n, [D, D]) for n in ("L0_gnn_W1", "L0_gnn_W2")}
        for n in ("L0_gnn_W1_loop", "L0_gnn_W2_loop", "L1_gnn_Wq", "L1_gnn_Wk", "L1_gnn_We", "L1_gnn_Wv",
                  "L2_gnn_W1", "L2_gnn_W2"):
            w[n] = sb(n, [D + 1, D])
        bias_of = {"L0_gnn_W1_loop": "L0_gnn_b1", "L0_gnn_W2_loop": "L0_gnn_b2", "L1_gnn_Wq": "L1_gnn_bq",
                   "L1_gnn_Wk": "L1_gnn_bk", "L1_gnn_We": "L1_gnn_be", "L1_gnn_Wv": "L1_gnn_bv",
                   "L2_gnn_W1": "L2_gnn_b1", "L2_gnn_W2": "L2_gnn_b2"}
        psum = [ctx.enter_context(nc.psum_tensor(f"bank{i}", [P, GR], F32)) for i in range(8)]

        raw = [sb(f"raw{i}", [P, C], I32) for i in range(3)]
        rec = sb("rec", [P, C, 4], I32)
        halo = sb("halo", [P, C + 2, 4], I32)
        slot_no = sb("slot_no", [P, C], I32)
        node_row = sb("node_row", [P, C, 2], I32)
        work = [sb(f"work{i}", [P, C]) for i in range(4)]
        flag_tile = sb("flag_tile", [P, 2, C], BF16)
        meta_all = sb("meta_all", [P, C, NF], I32)
        small = sb("small", [P, 16])
        row1 = sb("row1", [1, 4, P])
        ends = sb("ends", [1, 2, 4], I32)
        zero_row = sb("zero_row", [1, D])
        unsorted = sb("unsorted", [P, 1], I32)
        rank_dst = sb("rank_dst", [P, CH], I32)
        rank_tmp = sb("rank_tmp", [P, CH])
        rank_neg = sb("rank_neg", [P, CH])
        rank_no = sb("rank_no_row", [P, CH])
        rank_sum = sb("rank_sum_col", [P, 1])
        rank_idx = sb("rank_idx", [P, 1], I32)
        rank_rec = sb("rank_rec", [P, 4], I32)
        rank_row = sb("rank_row", [P, D])

        names = []
        for table in (ENGINE_SIGNALS, DMA_SIGNALS):
            for uses in table.values():
                names += [n for n in uses if n not in names]
        engine_sems = {n: sem(n) for n in names if any(n in u for u in ENGINE_SIGNALS.values())}
        dma_sems = {n: [sem(f"{n}{s}") for s in range(2)] for n in names if any(n in u for u in DMA_SIGNALS.values())}

        def signals(phase):
            found = {}
            earlier = PHASES[:PHASES.index(phase)]
            for n in ENGINE_SIGNALS[phase]:
                found[n] = Signal(engine_sems[n], sum(ENGINE_SIGNALS[p].get(n, 0) for p in earlier) * NG)
            for n in DMA_SIGNALS[phase]:
                base = sum(DMA_SIGNALS[p].get(n, 0) for p in earlier) * 16 * NG // 2
                found[n] = [Signal(q, base) for q in dma_sems[n]]
            return found

        s_settled = sem("settled")
        s_phase = sem("phase_done")
        s_weights = sem("weights_in")
        s_raw = sem("raw_in")
        s_edge_copy = sem("edge_copy")
        s_pool_const = sem("pool_const")
        s_pads = sem("pads_set")
        s_prep = sem("prep_dve")
        s_prep_pe = sem("prep_pe")
        s_rec_out = sem("rec_out")
        s_halo = sem("halo_in")
        s_sorted = sem("list_sorted")
        s_tables_out = sem("tables_out")
        s_rank = sem("rank_dve")
        s_disorder = sem("disorder")
        s_rank_no = sem("rank_no")
        s_rank_sum = sem("rank_sum")
        s_rank_in = sem("rank_in")
        s_rank_copy = sem("rank_copy")
        s_rank_row = sem("rank_row_in")
        s_rank_out = sem("rank_out")
        s_rank_done = sem("rank_done")

        block = ctx.enter_context(nc.Block())

        def settle(eng):
            eng.sem_inc(s_settled, 1)

        def f32(tile):
            return tile.bitcast(F32)

        def word(s, f):
            return meta[:, s, :, f]

        def backwards(ap):
            (ps, pn), (fs, fn) = ap.ap
            return bass.AP(ap.tensor, ap.offset + fs * (fn - 1), [[ps, pn], [-fs, fn]])

        def lanes(tile):
            return tile.rearrange("d (p t) -> d p t", t=T)

        def cap(count):
            return min(count, NG) if isinstance(count, int) else count

        def rows_of(bank):
            return psum[bank][:, 0:T * D].rearrange("p (t d) -> p t d", t=T)

        def flat(tile):
            return tile.rearrange("p t d -> p (t d)")

        def turn(pe, bank, rows):
            for t in range(T):
                last = pe.transpose(lanes(psum[bank][0:D, :])[:, :, t], rows[:, t, :], ident[:, :])
            return last

        def turn_back(pe, bank, cols):
            for t in range(T):
                last = pe.transpose(rows_of(bank)[:, t, :], lanes(cols)[:, :, t], ident[0:D, 0:D])
            return last

        def times(pe, bank, *products):
            for t in range(T):
                for i, (cols, weight) in enumerate(products):
                    last = pe.matmul(rows_of(bank)[:, t, :], lanes(cols)[:, :, t], weight,
                                     start=(i == 0), stop=(i == len(products) - 1))
            return last

        def times_cols(pe, bank, cols, weight):
            return pe.matmul(psum[bank][0:D, :], weight, cols, start=True, stop=True)

        def ln_stats(dve, sg, n, st, y, dve_n, act_n):
            stats, mv, sc = ln_tiles[n - 1]
            d, ac = sg[f"ln{n}_dve"], sg[f"ln{n}_act"]
            for t in range(T):
                last = dve.bn_stats(stats[:, st.s, t, :], y[:, t, :])
            last.then_inc(d.sem, 1)
            dve.wait_ge(d.sem, d.at(dve_n * st.g + 1))
            if st.again and act_n == 3:
                dve.wait_ge(ac.sem, ac.at(3 * (st.g - 1)))
            settle(dve)
            for t in range(T):
                last = dve.bn_aggr(mv[:, st.s, t, :], stats[:, st.s, t, :])
            last.then_inc(d.sem, 1)
            dve.wait_ge(d.sem, d.at(dve_n * st.g + 2))
            dve.tensor_scalar(sc[:, st.s, 0, :], mv[:, st.s, :, 1], EPS, None, ALU.add).then_inc(d.sem, 1)

        def ln_root(act, sg, n, st, dve_n, act_n):
            _, _, sc = ln_tiles[n - 1]
            d, ac = sg[f"ln{n}_dve"], sg[f"ln{n}_act"]
            act.wait_ge(d.sem, d.at(dve_n * st.g + 3))
            act.activation(sc[:, st.s, 1, :], sc[:, st.s, 0, :], ACT.Ln).then_inc(ac.sem, 1)
            act.wait_ge(ac.sem, ac.at(act_n * st.g + 1))
            act.activation(sc[:, st.s, 2, :], sc[:, st.s, 1, :], ACT.Exp, scale=-0.5).then_inc(ac.sem, 1)

        def ln_scale(dve, sg, n, st, dve_n, act_n, mask=None):
            _, mv, sc = ln_tiles[n - 1]
            d, ac = sg[f"ln{n}_dve"], sg[f"ln{n}_act"]
            v, r0, t1, t2 = (sc[:, st.s, i, :] for i in (0, 2, 3, 4))
            r, nb = sc[:, st.s, 5, :], sc[:, st.s, 6, :]
            k = dve_n * st.g + 3
            dve.wait_ge(ac.sem, ac.at(act_n * st.g + 2))
            dve.tensor_tensor(t1, v, r0, ALU.mult).then_inc(d.sem, 1)
            dve.wait_ge(d.sem, d.at(k + 1))
            dve.scalar_tensor_tensor(t2, t1, -0.5, r0, ALU.mult, ALU.mult).then_inc(d.sem, 1)
            dve.wait_ge(d.sem, d.at(k + 2))
            dve.scalar_tensor_tensor(r, t2, 1.5, r0, ALU.add, ALU.mult).then_inc(d.sem, 1)
            dve.wait_ge(d.sem, d.at(k + 3))
            if mask is not None:
                dve.tensor_tensor(r, r, mask, ALU.mult).then_inc(d.sem, 1)
                dve.wait_ge(d.sem, d.at(k + 4))
            if act_n == 3:
                dve.scalar_tensor_tensor(nb, mv[:, st.s, :, 0], -1.0, r, ALU.mult, ALU.mult).then_inc(d.sem, 1)

        def ln_apply_dve(dve, sg, n, st, y, result):
            _, mv, sc = ln_tiles[n - 1]
            for t in range(T):
                last = dve.tensor_scalar(result[:, t, :], y[:, t, :], mv[:, st.s, t, 0:1], sc[:, st.s, 5, t:t + 1],
                                         ALU.subtract, ALU.mult)
            last.then_inc(sg[f"ln{n}_dve"].sem, 1)

        def ln_apply_act(act, sg, n, st, y, result, dve_n):
            _, _, sc = ln_tiles[n - 1]
            d = sg[f"ln{n}_dve"]
            act.wait_ge(d.sem, d.at(dve_n * (st.g + 1)))
            for t in range(T):
                last = act.activation(result[:, t, :], y[:, t, :], ACT.Identity,
                                      bias=sc[:, st.s, 6, t:t + 1], scale=sc[:, st.s, 5, t:t + 1])
            last.then_inc(sg[f"ln{n}_act"].sem, 1)

        @block.sync
        def _(sp):
            for n, tile in w.items():
                sp.dma_start(tile[0:D, :], a[n]).then_inc(s_weights, 16)
                if n in bias_of:
                    sp.dma_start(tile[D:D + 1, :], a[bias_of[n]].unsqueeze(0)).then_inc(s_weights, 16)
            sp.wait_ge(s_pads, 5)
            full = E // C
            for i, name in enumerate(("src", "dst", "edge_weight")):
                v = a[name] if name != "edge_weight" else a[name].bitcast(I32)
                sp.dma_start(raw[i][0:full, :], v[0:full * C].rearrange("(p c) -> p c", c=C)).then_inc(s_raw, 16)
                sp.dma_start(raw[i][full:full + 1, 0:E - full * C], v[full * C:E].unsqueeze(0)).then_inc(s_raw, 16)
            body = E // GR * GR
            sp.dma_start(edge_rows[0:body, :].rearrange("(p r) d -> p (r d)", p=P),
                         a["edge_attr_96"][0:body, :].rearrange("(p r) d -> p (r d)", p=P)).then_inc(s_edge_copy, 16)
            sp.dma_start(edge_rows[body:E, :], a["edge_attr_96"][body:E, :]).then_inc(s_edge_copy, 16)
            sp.dma_start(edge_rows[E:EP, :], a["edge_attr_96"][0:EP - E, :]).then_inc(s_edge_copy, 16)
            sp.dma_start(mean_t[EP:EP + 1, :], zero_row[:, :]).then_inc(s_edge_copy, 16)

            sp.wait_ge(s_prep, 4)
            sp.dma_start(edges[0:1, :], ends[:, 0, :]).then_inc(s_rec_out, 16)
            sp.dma_start(edges[EP + 1:EP + 2, :], ends[:, 1, :]).then_inc(s_rec_out, 16)
            sp.dma_start(edges[1:EP + 1, :].rearrange("(p c) f -> p (c f)", p=P),
                         rec[:, :, :].rearrange("p c f -> p (c f)")).then_inc(s_rec_out, 16)
            sp.wait_ge(s_rec_out, 48)
            halo_view = bass.AP(edges.tensor, 0, [[4 * C, P], [1, 4 * (C + 2)]])
            sp.dma_start(halo[:, :, :].rearrange("p c f -> p (c f)"), halo_view).then_inc(s_halo, 16)
            sp.wait_ge(s_edge_copy, 64)
            sp.wait_ge(s_prep, 7)
            disorder = sp.value_load(unsorted[0:1, 0:1])
            with sp.If(disorder > 0):
                sp.dma_start(dst_list.rearrange("(p c) -> p c", p=P), raw[1][:, :]).then_inc(s_rec_out, 16)
                sp.wait_ge(s_rec_out, 64)
                for c in range(CHUNKS):
                    if c:
                        sp.wait_ge(s_rank, 3 * C * c + c)
                    chunk = dst_list[c * CH:(c + 1) * CH]
                    sp.dma_start(rank_dst[:, :], chunk.unsqueeze(0).to_broadcast([P, CH])).then_inc(s_rank_in, 16)
                sp.wait_ge(s_rank_done, 1)
                sp.dma_start(edge_rows.rearrange("(p r) d -> p (r d)", p=P),
                             edges2[1:EP + 1, :].rearrange("(p r) d -> p (r d)", p=P)).then_inc(s_edge_copy, 16)
                sp.wait_ge(s_edge_copy, 80)
                sp.dma_start(halo[:, :, :].rearrange("p c f -> p (c f)"), halo_view).then_inc(s_halo, 16)
                sp.wait_ge(s_halo, 32)
            sp.sem_inc(s_sorted, 1)

            sp.wait_ge(s_pool_const, 6)
            sp.dma_start(place.rearrange("(p c) f -> p (c f)", p=P),
                         node_row[:, :, :].rearrange("p c f -> p (c f)")).then_inc(s_tables_out, 16)
            sp.wait_ge(s_prep, PREP_ALL)
            sp.dma_start(meta_t.rearrange("(p c) f -> p (c f)", p=P),
                         meta_all[:, :, :].rearrange("p c f -> p (c f)")).then_inc(s_tables_out, 16)
            sp.dma_start(flags_f.rearrange("(p c) -> p c", p=P), flag_tile[:, 0, :]).then_inc(s_tables_out, 16)
            sp.dma_start(flags_b.rearrange("(p c) -> p c", p=P), flag_tile[:, 1, :]).then_inc(s_tables_out, 16)
            sp.wait_ge(s_tables_out, 64)
            sp.sem_inc(s_phase, 1)

            meta_g = meta_t.rearrange("(g p t) f -> g p t f", p=P, t=T)
            source_g = source.rearrange("(g p t) f -> g p t f", p=P, t=T)

            def load_meta(st, sig, g):
                settle(sp)
                sp.dma_start(meta[:, st.s, :, :], meta_g[g]).then_inc(sig[st.s].sem, 16)

            def load_flags(st, sig, table, g):
                settle(sp)
                sp.dma_start(flag[:, st.s, :], table[bass.ds(g * GR, GR)].unsqueeze(0).to_broadcast([D, GR]))\
                    .then_inc(sig[st.s].sem, 16)

            def load_rows(st, sig, tile, table, g):
                settle(sp)
                sp.dma_start(flat(tile[:, st.s]), groups(table)[g]).then_inc(sig[st.s].sem, 16)

            def load_source(st, sig, g):
                settle(sp)
                sp.dma_start(srcs[:, st.s, :, :], source_g[g]).then_inc(sig[st.s].sem, 16)

            def store_rows(st, sig, tile, table, g):
                settle(sp)
                sp.dma_start(groups(table)[g], flat(tile[:, st.s])).then_inc(sig[st.s].sem, 16)

            def finish(*sigs):
                for sig, k in sigs:
                    for q in sig:
                        sp.wait_ge(q.sem, q.at(16 * k * NG // 2))
                sp.sem_inc(s_phase, 1)

            sg = signals("A")
            xs, xd, xw, conv, x, h, y1, x1, x2, y2, x3, res = row_tiles[:12]

            def phase_a(at):
                if st := at(0):
                    if st.again:
                        sp.wait_ge(sg["weighted"].sem, sg["weighted"].at(st.g - 1))
                        settle(sp)
                        sp.wait_ge(sg["scanned"].sem, sg["scanned"].at(st.g - 1))
                        settle(sp)
                        sp.wait_ge(sg["own_in"][st.s].sem, sg["own_in"][st.s].at(64 * st.h))
                        settle(sp)
                        sp.wait_ge(sg["ids_out"][st.s].sem, sg["ids_out"][st.s].at(64 * st.h))
                    load_meta(st, sg["meta_in"], st.g)
                    load_flags(st, sg["meta_in"], flags_f, st.g)
                    if st.again:
                        sp.wait_ge(sg["y1"].sem, sg["y1"].at(2 * (st.g - 1)))
                    if isinstance(st.g, int) and st.g == NG - 1:
                        sp.dma_start(flat(x[0:NLAST // T, st.s]),
                                     a["x"][(NG - 1) * GR:N, :].rearrange("(p t) d -> p (t d)", t=T))\
                            .then_inc(sg["x_in"][st.s].sem, 16)
                    else:
                        load_rows(st, sg["x_in"], x, nodes_in, st.g)
                if st := at(1):
                    sp.wait_ge(sg["own_in"][st.s].sem, sg["own_in"][st.s].at(64 * (st.h + 1)))
                    store_rows(st, sg["own_out"], xd, x_own, st.g)
                if st := at(2):
                    sp.wait_ge(sg["ln1_dve"].sem, sg["ln1_dve"].at(7 * (st.g + 1)))
                    store_rows(st, sg["x1_stored"], x1, x1_t, NG + st.g)
                if st := at(3):
                    sp.wait_ge(sg["ln2_act"].sem, sg["ln2_act"].at(3 * (st.g + 1)))
                    store_rows(st, sg["x2_stored"], x2, x2_t, NG + st.g)
                if st := at(4):
                    sp.wait_ge(sg["ln3_act"].sem, sg["ln3_act"].at(3 * (st.g + 1)))
                    store_rows(st, sg["x3_stored"], x3, x3_t, NG + st.g)
                    sp.wait_ge(sg["ln4_dve"].sem, sg["ln4_dve"].at(7 * (st.g + 1)))
                    if isinstance(st.g, int) and st.g == NG - 1:
                        sp.dma_start(out[(NG - 1) * GR:N, :].rearrange("(p t) d -> p (t d)", t=T),
                                     flat(res[0:NLAST // T, st.s])).then_inc(sg["x3_stored"][st.s].sem, 16)
                    else:
                        store_rows(st, sg["x3_stored"], res, nodes_out, st.g)

            ticks(sp, NG, 4, phase_a)
            finish((sg["own_out"], 1), (sg["conv_stored"], 1), (sg["h_stored"], 1), (sg["x1_stored"], 1),
                   (sg["x2_stored"], 1), (sg["x3_stored"], 2), (sg["ids_out"], 4))

            sb_ = signals("B")

            def phase_b(at):
                if st := at(0):
                    if st.again:
                        sp.wait_ge(sb_["src_in"][st.s].sem, sb_["src_in"][st.s].at(64 * st.h))
                    load_meta(st, sb_["meta_in"], st.g)
                if st := at(1):
                    sp.wait_ge(sb_["ids_made"].sem, sb_["ids_made"].at(2 * (st.g + 1)))
                    settle(sp)
                    sp.dma_start(source_g[st.g], srcs[:, st.s, :, :]).then_inc(sb_["ids_stored"][st.s].sem, 16)

            ticks(sp, NG, 1, phase_b)
            finish((sb_["ids_stored"], 1))

            sc = signals("C")
            hs, hown, x, xw, y1, x1 = row_tiles[:6]

            def phase_c(at):
                if st := at(0):
                    if st.again:
                        sp.wait_ge(sc["scanned"].sem, sc["scanned"].at(st.g - 1))
                        settle(sp)
                        sp.wait_ge(sc["src_in"][st.s].sem, sc["src_in"][st.s].at(64 * st.h))
                        settle(sp)
                        sp.wait_ge(sc["ln1_dve"].sem, sc["ln1_dve"].at(8 * (st.g - 1)))
                    load_meta(st, sc["meta_in"], st.g)
                    load_source(st, sc["meta_in"], st.g)
                    load_flags(st, sc["meta_in"], flags_f, st.g)
                    if st.again:
                        sp.wait_ge(sc["own_turned"].sem, sc["own_turned"].at(st.g - 1))
                    load_rows(st, sc["x_in"], hown, h_t, st.g)
                    load_rows(st, sc["x_in"], x, x_own, st.g)
                if st := at(2):
                    sp.wait_ge(sc["ln1_act"].sem, sc["ln1_act"].at(3 * (st.g + 1)))
                    store_rows(st, sc["x1_stored"], x1, x1_t, st.g)

            ticks(sp, NG, 2, phase_c)
            finish((sc["x1_stored"], 1))

            sd = signals("D")
            xs, xo, ea, x2 = row_tiles[:4]

            def phase_d(at):
                if st := at(0):
                    g = NG - 1 - st.g
                    if st.again:
                        sp.wait_ge(sd["scanned"].sem, sd["scanned"].at(st.g - 1))
                        settle(sp)
                        sp.wait_ge(sd["src_in"][st.s].sem, sd["src_in"][st.s].at(64 * st.h))
                    load_source(st, sd["meta_in"], g)
                    load_flags(st, sd["meta_in"], flags_b, g)
                    if st.again:
                        sp.wait_ge(sd["own_turned"].sem, sd["own_turned"].at(st.g - 1))
                    load_rows(st, sd["x_in"], xo, x1_t, g)
                    if st.again:
                        sp.wait_ge(sd["edge_turned"].sem, sd["edge_turned"].at(st.g - 1))
                    load_rows(st, sd["edge_in"], ea, edge_rows, g)
                if st := at(3):
                    sp.wait_ge(sd["ln1_act"].sem, sd["ln1_act"].at(3 * (st.g + 1)))
                    store_rows(st, sd["x1_stored"], x2, x2_t, NG - 1 - st.g)

            ticks(sp, NG, 3, phase_d)
            finish((sd["x1_stored"], 1))

            se = signals("E")
            xs, xo, y2, x3 = row_tiles[:4]

            def phase_e(at):
                if st := at(0):
                    g = NG - 1 - st.g
                    if st.again:
                        sp.wait_ge(se["scanned"].sem, se["scanned"].at(st.g - 1))
                        settle(sp)
                        sp.wait_ge(se["src_in"][st.s].sem, se["src_in"][st.s].at(64 * st.h))
                        settle(sp)
                        sp.wait_ge(se["y2"].sem, se["y2"].at(st.g - 1))
                    load_source(st, se["meta_in"], g)
                    load_flags(st, se["meta_in"], flags_b, g)
                    load_rows(st, se["x_in"], xo, x2_t, g)
                if st := at(2):
                    sp.wait_ge(se["ln1_act"].sem, se["ln1_act"].at(3 * (st.g + 1)))
                    store_rows(st, se["x1_stored"], x3, x3_t, NG - 1 - st.g)

            ticks(sp, NG, 2, phase_e)
            finish((se["x1_stored"], 1))

            sf = signals("F")
            xs, mean = row_tiles[:2]

            def phase_f(at):
                if st := at(0):
                    g = NG - 1 - st.g
                    if st.again:
                        sp.wait_ge(sf["scanned"].sem, sf["scanned"].at(st.g - 1))
                        settle(sp)
                        sp.wait_ge(sf["src_in"][st.s].sem, sf["src_in"][st.s].at(64 * st.h))
                        settle(sp)
                        sp.wait_ge(sf["conv_out"].sem, sf["conv_out"].at(st.g - 1))
                    load_meta(st, sf["meta_in"], g)
                    load_source(st, sf["meta_in"], g)
                    load_flags(st, sf["meta_in"], flags_b, g)
                if st := at(1):
                    sp.wait_ge(sf["conv_out"].sem, sf["conv_out"].at(st.g + 1))
                    store_rows(st, sf["x1_stored"], mean, mean_t[0:EP, :], NG - 1 - st.g)

            ticks(sp, NG, 1, phase_f)
            finish((sf["x1_stored"], 1))

            sh = signals("G")
            xs, xo, mo, t1, y2, res = row_tiles[:6]

            def phase_g(at):
                if st := at(0):
                    g = NG - 1 - st.g
                    if st.again:
                        sp.wait_ge(sh["scanned"].sem, sh["scanned"].at(st.g - 1))
                        settle(sp)
                        sp.wait_ge(sh["ids_out"][st.s].sem, sh["ids_out"][st.s].at(64 * st.h))
                        settle(sp)
                        sp.wait_ge(sh["y2"].sem, sh["y2"].at(st.g - 1))
                    load_meta(st, sh["meta_in"], g)
                    load_source(st, sh["meta_in"], g)
                    load_flags(st, sh["meta_in"], flags_b, g)
                    load_rows(st, sh["x_in"], xo, x3_t, g)
                    load_rows(st, sh["x_in"], mo, mean_t[0:EP, :], g)

            ticks(sp, NG, 0, phase_g)
            finish((sh["ids_out"], 4))

        def gather(pool, tile, table, index, sig):
            pool.indirect_dma_start(out=tile, out_offset=None, in_=table,
                                    in_offset=bass.IndirectOffsetOnAxis(ap=index, axis=0),
                                    bounds_check=table.shape[0] - 1, oob_is_err=False).then_inc(sig.sem, 16)

        def scatter(pool, table, index, tile, sig):
            pool.indirect_dma_start(out=table, out_offset=bass.IndirectOffsetOnAxis(ap=index, axis=0), in_=tile,
                                    in_offset=None, bounds_check=N - 1, oob_is_err=False).then_inc(sig.sem, 16)

        @block.gpsimd
        def _(pool):
            pool.iota(slot_no[:, :], [[1, C]], base=0, channel_multiplier=C).then_inc(s_pool_const, 1)
            pool.iota(node_row[:, :, :], [[1, C], [0, 2]], base=EP, channel_multiplier=C).then_inc(s_pool_const, 1)
            pool.memset(ident[:, :], 0.0).then_inc(s_pool_const, 1)
            pool.memset(head_sum[:, :], float(HD) ** -0.5).then_inc(s_pool_const, 1)
            pool.wait_ge(s_pool_const, 4)
            pool.affine_select(out=ident[:, :], in_=ident[:, :], compare_op=ALU.not_equal, fill=1.0, base=0,
                               pattern=[[-1, P]], channel_multiplier=1).then_inc(s_pool_const, 1)
            blocks = head_sum[:, :].rearrange("p (h c) -> p h c", c=HD)
            pool.affine_select(out=blocks, in_=blocks, compare_op=ALU.is_ge, fill=0.0, base=0,
                               pattern=[[-HD, HEADS], [0, HD]], channel_multiplier=1).then_inc(s_pool_const, 1)
            pool.wait_ge(s_pool_const, 6)
            pool.affine_select(out=blocks, in_=blocks, compare_op=ALU.is_ge, fill=0.0, base=HD - 1,
                               pattern=[[HD, HEADS], [0, HD]], channel_multiplier=-1).then_inc(s_pool_const, 1)

            pool.wait_ge(s_prep, 7)
            pool.wait_ge(s_edge_copy, 64)
            disorder = pool.value_load(unsorted[0:1, 0:1])
            with pool.If(disorder > 0):
                pool.wait_ge(s_rank, CHUNKS * (3 * C + 1))
                unsorted_rows = edge_rows.rearrange("(p c) d -> p c d", p=P)

                def move(c, first):
                    if not first:
                        pool.wait_ge(s_rank_out, 32 * c)
                    pool.dma_start(rank_row[:, :], unsorted_rows[:, bass.ds(c, 1), :].rearrange("p c d -> p (c d)"))\
                        .then_inc(s_rank_row, 16)
                    pool.tensor_copy(rank_idx[:, :], work[0][:, bass.ds(c, 1)]).then_inc(s_rank_copy, 1)
                    pool.tensor_copy(rank_rec[:, :], rec[:, bass.ds(c, 1), :].rearrange("p c f -> p (c f)"))\
                        .then_inc(s_rank_copy, 1)
                    pool.wait_ge(s_rank_copy, 2 * c + 2)
                    pool.wait_ge(s_rank_row, 16 * c + 16)
                    settle(pool)
                    for table, tile in ((edges2, rank_row), (edges, rank_rec)):
                        pool.indirect_dma_start(out=table, out_offset=bass.IndirectOffsetOnAxis(
                            ap=rank_idx[:, 0:1], axis=0), in_=tile[:, :], in_offset=None,
                            bounds_check=EP, oob_is_err=False).then_inc(s_rank_out, 16)

                move(0, True)
                with pool.Fori(1, C) as c:
                    move(c, False)
                pool.wait_ge(s_rank_out, 32 * C)
                pool.sem_inc(s_rank_done, 1)

            sg = signals("A")
            xs, xd = row_tiles[0:2]
            pool.wait_ge(s_phase, 1)

            def phase_a(at):
                st = at(0)
                pool.wait_ge(sg["meta_in"][st.s].sem, sg["meta_in"][st.s].at(32 * (st.h + 1)))
                settle(pool)
                for t in range(T):
                    scatter(pool, place, meta[:, st.s, t, END_DST:END_DST + 1], meta[:, st.s, t, SLOT:SLOT + 2],
                            sg["ids_out"][st.s])
                if st.again:
                    pool.wait_ge(sg["weighted"].sem, sg["weighted"].at(st.g - 1))
                settle(pool)
                for t in range(T):
                    gather(pool, xs[:, st.s, t, :], a["x"], meta[:, st.s, t, SRC:SRC + 1], sg["src_in"][st.s])
                if st.again:
                    pool.wait_ge(sg["own_turned"].sem, sg["own_turned"].at(st.g - 1))
                    pool.wait_ge(sg["own_out"][st.s].sem, sg["own_out"][st.s].at(16 * st.h))
                settle(pool)
                for t in range(T):
                    gather(pool, xd[:, st.s, t, :], a["x"], meta[:, st.s, t, DST:DST + 1], sg["own_in"][st.s])

            ticks(pool, NG, 0, phase_a)

            sb_ = signals("B")
            pool.wait_ge(s_phase, 2)

            def phase_b(at):
                st = at(0)
                pool.wait_ge(sb_["meta_in"][st.s].sem, sb_["meta_in"][st.s].at(16 * (st.h + 1)))
                if st.again:
                    pool.wait_ge(sb_["ids_made"].sem, sb_["ids_made"].at(2 * (st.g - 1)))
                settle(pool)
                for t in range(T):
                    gather(pool, ids[:, st.s, t, :], place, meta[:, st.s, t, SRC:SRC + 1], sb_["src_in"][st.s])

            ticks(pool, NG, 0, phase_b)

            def sources(phase, table, field, metas, reader, extra=0, more=None):
                s = signals(phase)
                xs = row_tiles[0]
                pool.wait_ge(s_phase, PHASES.index(phase) + 1)

                def body(at):
                    if st := at(0):
                        pool.wait_ge(s["meta_in"][st.s].sem, s["meta_in"][st.s].at(16 * metas * (st.h + 1)))
                        if st.again:
                            pool.wait_ge(s[reader].sem, s[reader].at(st.g - 1))
                        settle(pool)
                        for t in range(T):
                            gather(pool, xs[:, st.s, t, :], table, srcs[:, st.s, t, field:field + 1],
                                   s["src_in"][st.s])
                    if more:
                        more(s, at)

                ticks(pool, NG, extra, body)

            sources("C", h_t, 0, 3, "weighted")
            sources("D", x1_t, 0, 2, "src_turned")
            sources("E", x2_t, 1, 2, "src_turned")
            sources("F", x3_t, 1, 3, "src_turned")

            def results(s, at):
                if st := at(1):
                    pool.wait_ge(s["ln1_act"].sem, s["ln1_act"].at(3 * (st.g + 1)))
                    settle(pool)
                    for t in range(T):
                        scatter(pool, out, meta[:, st.s, t, START_DST:START_DST + 1], row_tiles[5][:, st.s, t, :],
                                s["ids_out"][st.s])

            sources("G", mean_t, 2, 3, "src_turned", 1, results)

        @block.tensor
        def _(pe):
            pe.wait_ge(s_pads, 5)
            pe.wait_ge(s_prep, 5)
            pe.matmul(psum[0][:, 0:1], ones[:, :], small[:, 0:1], start=True, stop=True).then_inc(s_prep_pe, 1)
            pe.wait_ge(s_pool_const, 7)
            pe.wait_ge(s_prep, 16)
            pe.transpose(psum[1][0:1, 0:P], small[:, 2:3], ident[:, :]).then_inc(s_prep_pe, 1)
            pe.transpose(psum[2][0:1, 0:P], small[:, 3:4], ident[:, :]).then_inc(s_prep_pe, 1)
            pe.wait_ge(s_prep, 20)
            pe.matmul(psum[3][:, 0:1], row1[0:1, 2, :], ones[0:1, 0:1], start=True, stop=True).then_inc(s_prep_pe, 1)
            pe.matmul(psum[4][:, 0:1], row1[0:1, 3, :], ones[0:1, 0:1], start=True, stop=True).then_inc(s_prep_pe, 1)
            pe.wait_ge(s_weights, 16 * (len(w) + len(bias_of)))

            sg = signals("A")
            xs, xd, xw, conv, x, h, y1, x1, x2 = row_tiles[:9]
            seg, xd_c, x_c, h_c, x2_c, g_c = col_tiles[:6]
            pe.wait_ge(s_phase, 1)

            def phase_a(at):
                if st := at(0):
                    pe.wait_ge(sg["x_in"][st.s].sem, sg["x_in"][st.s].at(16 * (st.h + 1)))
                    if after(st.g, 3):
                        pe.wait_ge(sg["x2_cols"].sem, sg["x2_cols"].at(st.g - 2))
                    turn(pe, 3, x[:, st.s]).then_inc(sg["x_turned"].sem, 1)
                if st := at(1):
                    pe.wait_ge(sg["h_rows"].sem, sg["h_rows"].at(st.g + 1))
                    if st.again:
                        pe.wait_ge(sg["mlp_hidden"].sem, sg["mlp_hidden"].at(st.g - 1))
                    turn(pe, 4, h[:, st.s]).then_inc(sg["h_turned"].sem, 1)
                if st := at(0):
                    pe.wait_ge(sg["weighted"].sem, sg["weighted"].at(st.g + 1))
                    if after(st.g, 1):
                        pe.wait_ge(sg["scanned"].sem, sg["scanned"].at(st.g))
                    turn(pe, 0, xw[:, st.s]).then_inc(sg["src_turned"].sem, 1)
                    pe.wait_ge(sg["own_in"][st.s].sem, sg["own_in"][st.s].at(64 * (st.h + 1)))
                    if after(st.g, 1):
                        pe.wait_ge(sg["own_cols"].sem, sg["own_cols"].at(st.g))
                    turn(pe, 1, xd[:, st.s]).then_inc(sg["own_turned"].sem, 1)
                    pe.wait_ge(sg["x_cols"].sem, sg["x_cols"].at(st.g + 1))
                    if after(st.g, 3):
                        pe.wait_ge(sg["y2"].sem, sg["y2"].at(st.g - 2))
                    times(pe, 5, (x_c[:, st.s], w["L0_gnn_W1_loop"][:, :])).then_inc(sg["loop1_done"].sem, 1)
                if st := at(1):
                    pe.wait_ge(sg["h_cols"].sem, sg["h_cols"].at(st.g + 1))
                    if after(st.g, 1):
                        pe.wait_ge(sg["y1"].sem, sg["y1"].at(2 * st.g))
                    times(pe, 6, (h_c[:, st.s], w["L0_gnn_W2_loop"][:, :])).then_inc(sg["loop2_done"].sem, 1)
                if st := at(0):
                    pe.wait_ge(sg["scanned"].sem, sg["scanned"].at(st.g + 1))
                    pe.wait_ge(sg["own_cols"].sem, sg["own_cols"].at(st.g + 1))
                    if after(st.g, 1):
                        pe.wait_ge(sg["conv_out"].sem, sg["conv_out"].at(st.g))
                    times(pe, 2, (seg[0:D, st.s], w["L0_gnn_W1"][:, :]), (xd_c[:, st.s], w["L0_gnn_W1_loop"][:, :]))\
                        .then_inc(sg["conv_done"].sem, 1)
                if st := at(2):
                    pe.wait_ge(sg["ln2_act"].sem, sg["ln2_act"].at(3 * (st.g + 1)))
                    pe.wait_ge(sg["x_cols"].sem, sg["x_cols"].at(cap(st.g + 3)))
                    turn(pe, 3, x2[:, st.s]).then_inc(sg["x2_turned"].sem, 1)
                    pe.wait_ge(sg["x2_cols"].sem, sg["x2_cols"].at(st.g + 1))
                    pe.wait_ge(sg["h_cols"].sem, sg["h_cols"].at(cap(st.g + 2)))
                    times_cols(pe, 4, x2_c[:, st.s], w["L2_gnn_W1"][:, :]).then_inc(sg["mlp1_done"].sem, 1)
                    pe.wait_ge(sg["mlp_hidden"].sem, sg["mlp_hidden"].at(st.g + 1))
                    pe.wait_ge(sg["h_rows"].sem, sg["h_rows"].at(cap(st.g + 3)))
                    times(pe, 5, (g_c[:, st.s], w["L2_gnn_W2"][:, :])).then_inc(sg["mlp2_done"].sem, 1)

            ticks(pe, NG, 2, phase_a)

            sc = signals("C")
            hs, hown, x, xw = row_tiles[:4]
            seg, h_c = col_tiles[:2]
            pe.wait_ge(s_phase, 3)

            def phase_c(at):
                st = at(0)
                pe.wait_ge(sc["x_in"][st.s].sem, sc["x_in"][st.s].at(32 * (st.h + 1)))
                if after(st.g, 1):
                    pe.wait_ge(sc["own_cols"].sem, sc["own_cols"].at(st.g))
                turn(pe, 1, hown[:, st.s]).then_inc(sc["own_turned"].sem, 1)
                pe.wait_ge(sc["weighted"].sem, sc["weighted"].at(st.g + 1))
                if after(st.g, 1):
                    pe.wait_ge(sc["scanned"].sem, sc["scanned"].at(st.g))
                turn(pe, 0, xw[:, st.s]).then_inc(sc["src_turned"].sem, 1)
                pe.wait_ge(sc["scanned"].sem, sc["scanned"].at(st.g + 1))
                pe.wait_ge(sc["own_cols"].sem, sc["own_cols"].at(st.g + 1))
                if after(st.g, 1):
                    pe.wait_ge(sc["y1"].sem, sc["y1"].at(2 * st.g))
                times(pe, 2, (seg[0:D, st.s], w["L0_gnn_W2"][:, :]), (h_c[:, st.s], w["L0_gnn_W2_loop"][:, :]))\
                    .then_inc(sc["conv_done"].sem, 1)

            ticks(pe, NG, 0, phase_c)

            sd = signals("D")
            xs, xo, ea = row_tiles[:3]
            xs_c, xf_c, ea_c, k_c, sc_c, ex_c, wv_c, z_c, y_c = col_tiles
            pe.wait_ge(s_phase, 4)

            def phase_d(at):
                if st := at(0):
                    pe.wait_ge(sd["x_in"][st.s].sem, sd["x_in"][st.s].at(16 * (st.h + 1)))
                    if after(st.g, 1):
                        pe.wait_ge(sd["filled"].sem, sd["filled"].at(st.g))
                    turn(pe, 1, xo[:, st.s]).then_inc(sd["own_turned"].sem, 1)
                    pe.wait_ge(sd["edge_in"][st.s].sem, sd["edge_in"][st.s].at(16 * (st.h + 1)))
                    if after(st.g, 1):
                        pe.wait_ge(sd["edge_cols"].sem, sd["edge_cols"].at(st.g))
                    turn(pe, 2, ea[:, st.s]).then_inc(sd["edge_turned"].sem, 1)
                    pe.wait_ge(sd["src_in"][st.s].sem, sd["src_in"][st.s].at(64 * (st.h + 1)))
                    if after(st.g, 1):
                        pe.wait_ge(sd["src_cols"].sem, sd["src_cols"].at(st.g))
                    turn(pe, 0, xs[:, st.s]).then_inc(sd["src_turned"].sem, 1)
                if st := at(1):
                    pe.wait_ge(sd["score"].sem, sd["score"].at(2 * (st.g + 1)))
                    pe.wait_ge(sd["k_cols"].sem, sd["k_cols"].at(st.g + 1))
                    times_cols(pe, 3, sc_c[0:D, st.s], head_sum[:, :]).then_inc(sd["sum_done"].sem, 1)
                if st := at(0):
                    pe.wait_ge(sd["filled"].sem, sd["filled"].at(st.g + 1))
                    if after(st.g, 1):
                        pe.wait_ge(sd["score"].sem, sd["score"].at(2 * st.g))
                    times_cols(pe, 5, xf_c[:, st.s], w["L1_gnn_Wq"][:, :]).then_inc(sd["q_done"].sem, 1)
                    pe.wait_ge(sd["edge_cols"].sem, sd["edge_cols"].at(st.g + 1))
                    times_cols(pe, 6, ea_c[:, st.s], w["L1_gnn_We"][:, :]).then_inc(sd["e_done"].sem, 1)
                    pe.wait_ge(sd["src_cols"].sem, sd["src_cols"].at(st.g + 1))
                    if after(st.g, 1):
                        pe.wait_ge(sd["clipped"].sem, sd["clipped"].at(st.g))
                    times_cols(pe, 3, xs_c[:, st.s], w["L1_gnn_Wk"][:, :]).then_inc(sd["k_done"].sem, 1)
                if st := at(2):
                    pe.wait_ge(sd["attn"].sem, sd["attn"].at(4 * (st.g + 1)))
                    if after(st.g, 1):
                        pe.wait_ge(sd["ln1_act"].sem, sd["ln1_act"].at(3 * st.g))
                    turn_back(pe, 7, y_c[0:D, st.s]).then_inc(sd["y_turned"].sem, 1)
                if st := at(0):
                    if after(st.g, 1):
                        pe.wait_ge(sd["msg"].sem, sd["msg"].at(st.g))
                    times_cols(pe, 4, xs_c[:, st.s], w["L1_gnn_Wv"][:, :]).then_inc(sd["v_done"].sem, 1)

            ticks(pe, NG, 2, phase_d)

            se = signals("E")
            xs, xo = row_tiles[:2]
            seg, rst, g_c = col_tiles[:3]
            pe.wait_ge(s_phase, 5)

            def phase_e(at):
                if st := at(0):
                    pe.wait_ge(se["x_in"][st.s].sem, se["x_in"][st.s].at(16 * (st.h + 1)))
                    if after(st.g, 1):
                        pe.wait_ge(se["rst"].sem, se["rst"].at(st.g))
                    turn(pe, 1, xo[:, st.s]).then_inc(se["own_turned"].sem, 1)
                    pe.wait_ge(se["src_in"][st.s].sem, se["src_in"][st.s].at(64 * (st.h + 1)))
                    turn(pe, 0, xs[:, st.s]).then_inc(se["src_turned"].sem, 1)
                if st := at(1):
                    pe.wait_ge(se["rst"].sem, se["rst"].at(st.g + 1))
                    if after(st.g, 1):
                        pe.wait_ge(se["mlp_hidden"].sem, se["mlp_hidden"].at(st.g))
                    times_cols(pe, 2, rst[:, st.s], w["L2_gnn_W1"][:, :]).then_inc(se["mlp1_done"].sem, 1)
                    pe.wait_ge(se["mlp_hidden"].sem, se["mlp_hidden"].at(st.g + 1))
                    if after(st.g, 1):
                        pe.wait_ge(se["y2"].sem, se["y2"].at(st.g))
                    times(pe, 3, (g_c[:, st.s], w["L2_gnn_W2"][:, :])).then_inc(se["mlp2_done"].sem, 1)

            ticks(pe, NG, 1, phase_e)

            for phase, reader in (("F", "conv_out"), ("G", "y2")):
                s = signals(phase)
                xs, seg = row_tiles[0], col_tiles[0]
                pe.wait_ge(s_phase, PHASES.index(phase) + 1)

                def phase_fg(at):
                    if st := at(0):
                        pe.wait_ge(s["src_in"][st.s].sem, s["src_in"][st.s].at(64 * (st.h + 1)))
                        if after(st.g, 1):
                            pe.wait_ge(s["scanned"].sem, s["scanned"].at(st.g))
                        turn(pe, 0, xs[:, st.s]).then_inc(s["src_turned"].sem, 1)
                        pe.wait_ge(s["scanned"].sem, s["scanned"].at(st.g + 1))
                        if after(st.g, 1):
                            pe.wait_ge(s[reader].sem, s[reader].at(st.g))
                        turn_back(pe, 1, seg[0:D, st.s]).then_inc(s["y_turned"].sem, 1)

                ticks(pe, NG, 0, phase_fg)

        @block.scalar
        def _(act):
            act.preload_act_table_set("natural_log_exp_and_others")

            sg = signals("A")
            xs, xd, xw, conv, x, h, y1, x1, x2, y2, x3, res = row_tiles[:12]
            seg, xd_c, x_c, h_c, x2_c, g_c = col_tiles[:6]
            act.wait_ge(s_phase, 1)
            act.wait_ge(s_pads, 5)

            def phase_a(at):
                if st := at(0):
                    act.wait_ge(sg["x_turned"].sem, sg["x_turned"].at(st.g + 1))
                    if st.again:
                        act.wait_ge(sg["loop1_done"].sem, sg["loop1_done"].at(st.g - 1))
                    act.activation(x_c[0:D, st.s], psum[3][0:D, :], ACT.Copy).then_inc(sg["x_cols"].sem, 1)
                if st := at(1):
                    act.wait_ge(sg["h_turned"].sem, sg["h_turned"].at(st.g + 1))
                    if st.again:
                        act.wait_ge(sg["loop2_done"].sem, sg["loop2_done"].at(st.g - 1))
                    act.activation(h_c[0:D, st.s], psum[4][0:D, :], ACT.Copy).then_inc(sg["h_cols"].sem, 1)
                if st := at(2):
                    ln_root(act, sg, 2, st, 7, 3)
                if st := at(3):
                    ln_root(act, sg, 3, st, 7, 3)
                if st := at(0):
                    act.wait_ge(sg["own_turned"].sem, sg["own_turned"].at(st.g + 1))
                    if st.again:
                        act.wait_ge(sg["conv_done"].sem, sg["conv_done"].at(st.g - 1))
                    act.activation(xd_c[0:D, st.s], psum[1][0:D, :], ACT.Copy).then_inc(sg["own_cols"].sem, 1)
                    act.wait_ge(sg["loop1_done"].sem, sg["loop1_done"].at(st.g + 1))
                    if st.again:
                        act.wait_ge(sg["h_turned"].sem, sg["h_turned"].at(st.g - 1))
                        act.wait_ge(sg["h_stored"][st.s].sem, sg["h_stored"][st.s].at(16 * st.h))
                    act.activation(h[:, st.s], rows_of(5), ACT.Relu).then_inc(sg["h_rows"].sem, 1)
                    act.wait_ge(sg["h_rows"].sem, sg["h_rows"].at(st.g + 1))
                    act.dma_start(groups(h_t)[NG + st.g], flat(h[:, st.s])).then_inc(sg["h_stored"][st.s].sem, 16)
                if st := at(2):
                    if st.again:
                        act.wait_ge(sg["y2"].sem, sg["y2"].at(st.g - 1))
                        act.wait_ge(sg["x2_stored"][st.s].sem, sg["x2_stored"][st.s].at(16 * st.h))
                    ln_apply_act(act, sg, 2, st, x1[:, st.s], x2[:, st.s], 7)
                if st := at(1):
                    ln_root(act, sg, 1, st, 7, 2)
                if st := at(3):
                    if st.again:
                        act.wait_ge(sg["x3_stored"][st.s].sem, sg["x3_stored"][st.s].at(32 * st.h))
                        act.wait_ge(sg["ln4_dve"].sem, sg["ln4_dve"].at(7 * (st.g - 1)))
                    ln_apply_act(act, sg, 3, st, y2[:, st.s], x3[:, st.s], 7)
                if st := at(2):
                    act.wait_ge(sg["x2_turned"].sem, sg["x2_turned"].at(st.g + 1))
                    if st.again:
                        act.wait_ge(sg["mlp1_done"].sem, sg["mlp1_done"].at(st.g - 1))
                    act.activation(x2_c[0:D, st.s], psum[3][0:D, :], ACT.Copy).then_inc(sg["x2_cols"].sem, 1)
                if st := at(0):
                    act.wait_ge(sg["conv_done"].sem, sg["conv_done"].at(st.g + 1))
                    if st.again:
                        act.wait_ge(sg["conv_stored"][st.s].sem, sg["conv_stored"][st.s].at(16 * st.h))
                    act.activation(conv[:, st.s], rows_of(2), ACT.Relu).then_inc(sg["conv_out"].sem, 1)
                    act.wait_ge(sg["conv_out"].sem, sg["conv_out"].at(st.g + 1))
                    act.dma_start(groups(h_t)[st.g], flat(conv[:, st.s])).then_inc(sg["conv_stored"][st.s].sem, 16)
                if st := at(2):
                    act.wait_ge(sg["mlp1_done"].sem, sg["mlp1_done"].at(st.g + 1))
                    if st.again:
                        act.wait_ge(sg["mlp2_done"].sem, sg["mlp2_done"].at(st.g - 1))
                    act.activation(g_c[0:D, st.s], psum[4][0:D, :], ACT.Relu).then_inc(sg["mlp_hidden"].sem, 1)
                if st := at(3):
                    ln_root(act, sg, 4, st, 7, 2)

            ticks(act, NG, 3, phase_a)

            sc = signals("C")
            hs, hown, x, xw, y1, x1 = row_tiles[:6]
            seg, h_c = col_tiles[:2]
            act.wait_ge(s_phase, 3)

            def phase_c(at):
                if st := at(0):
                    act.wait_ge(sc["own_turned"].sem, sc["own_turned"].at(st.g + 1))
                    if st.again:
                        act.wait_ge(sc["conv_done"].sem, sc["conv_done"].at(st.g - 1))
                    act.activation(h_c[0:D, st.s], psum[1][0:D, :], ACT.Copy).then_inc(sc["own_cols"].sem, 1)
                if st := at(1):
                    ln_root(act, sc, 1, st, 8, 3)
                    if st.again:
                        act.wait_ge(sc["x1_stored"][st.s].sem, sc["x1_stored"][st.s].at(16 * st.h))
                    ln_apply_act(act, sc, 1, st, y1[:, st.s], x1[:, st.s], 8)

            ticks(act, NG, 1, phase_c)

            sd = signals("D")
            x2 = row_tiles[3]
            xs_c, xf_c, ea_c, k_c, sc_c, ex_c, wv_c, z_c, y_c = col_tiles
            act.wait_ge(s_phase, 4)

            def phase_d(at):
                if st := at(1):
                    act.wait_ge(sd["k_done"].sem, sd["k_done"].at(st.g + 1))
                    if st.again:
                        act.wait_ge(sd["score"].sem, sd["score"].at(2 * (st.g - 1)))
                    act.activation(k_c[0:D, st.s], psum[3][0:D, :], ACT.Copy).then_inc(sd["k_cols"].sem, 1)
                if st := at(0):
                    act.wait_ge(sd["edge_turned"].sem, sd["edge_turned"].at(st.g + 1))
                    if st.again:
                        act.wait_ge(sd["e_done"].sem, sd["e_done"].at(st.g - 1))
                    act.activation(ea_c[0:D, st.s], psum[2][0:D, :], ACT.Copy).then_inc(sd["edge_cols"].sem, 1)
                    act.wait_ge(sd["src_turned"].sem, sd["src_turned"].at(st.g + 1))
                    if st.again:
                        act.wait_ge(sd["v_done"].sem, sd["v_done"].at(st.g - 1))
                    act.activation(xs_c[0:D, st.s], psum[0][0:D, :], ACT.Copy).then_inc(sd["src_cols"].sem, 1)
                if st := at(1):
                    act.wait_ge(sd["clipped"].sem, sd["clipped"].at(st.g + 1))
                    if st.again:
                        act.wait_ge(sd["z_scanned"].sem, sd["z_scanned"].at(st.g - 1))
                    act.activation(ex_c[0:D, st.s], k_c[0:D, st.s], ACT.Exp).then_inc(sd["exped"].sem, 1)
                if st := at(2):
                    ln_root(act, sd, 1, st, 7, 3)
                    if st.again:
                        act.wait_ge(sd["x1_stored"][st.s].sem, sd["x1_stored"][st.s].at(16 * st.h))
                    ln_apply_act(act, sd, 1, st, rows_of(7), x2[:, st.s], 7)

            ticks(act, NG, 2, phase_d)

            se = signals("E")
            xs, xo, y2, x3 = row_tiles[:4]
            seg, rst, g_c = col_tiles[:3]
            act.wait_ge(s_phase, 5)

            def phase_e(at):
                if st := at(1):
                    act.wait_ge(se["mlp1_done"].sem, se["mlp1_done"].at(st.g + 1))
                    if st.again:
                        act.wait_ge(se["mlp2_done"].sem, se["mlp2_done"].at(st.g - 1))
                    act.activation(g_c[0:D, st.s], psum[2][0:D, :], ACT.Relu).then_inc(se["mlp_hidden"].sem, 1)
                    ln_root(act, se, 1, st, 7, 3)
                    if st.again:
                        act.wait_ge(se["x1_stored"][st.s].sem, se["x1_stored"][st.s].at(16 * st.h))
                    ln_apply_act(act, se, 1, st, y2[:, st.s], x3[:, st.s], 7)

            ticks(act, NG, 1, phase_e)

            sf = signals("F")
            mean = row_tiles[1]
            act.wait_ge(s_phase, 6)

            def phase_f(at):
                st = at(0)
                act.wait_ge(sf["y_turned"].sem, sf["y_turned"].at(st.g + 1))
                if st.again:
                    act.wait_ge(sf["x1_stored"][st.s].sem, sf["x1_stored"][st.s].at(16 * st.h))
                for t in range(T):
                    last = act.activation(mean[:, st.s, t, :], rows_of(1)[:, t, :], ACT.Copy,
                                          scale=f32(meta[:, st.s, t, INV_DEG:INV_DEG + 1]))
                last.then_inc(sf["conv_out"].sem, 1)

            ticks(act, NG, 0, phase_f)

            sh = signals("G")
            y2, res = row_tiles[4:6]
            act.wait_ge(s_phase, 7)

            def phase_g(at):
                if st := at(0):
                    ln_root(act, sh, 1, st, 7, 3)
                    if st.again:
                        act.wait_ge(sh["ids_out"][st.s].sem, sh["ids_out"][st.s].at(64 * st.h))
                    ln_apply_act(act, sh, 1, st, y2[:, st.s], res[:, st.s], 7)

            ticks(act, NG, 0, phase_g)

        @block.vector
        def _(dve):
            dve.memset(ones[:, :], 1.0).then_inc(s_pads, 1)
            dve.memset(raw[0][:, :], 0).then_inc(s_pads, 1)
            dve.memset(raw[1][:, :], PAD).then_inc(s_pads, 1)
            dve.memset(raw[2][:, :], 0).then_inc(s_pads, 1)
            dve.memset(zero_row[:, :], 0.0)
            dve.memset(ends[:, 0, :], -1)
            dve.memset(ends[:, 1, :], FAR)
            for tile in col_tiles:
                last = dve.memset(tile[D:D + 1, :, :], 1.0)
            last.then_inc(s_pads, 1)

            done = [0]

            def step(ins):
                done[0] += 1
                ins.then_inc(s_prep, 1)
                dve.wait_ge(s_prep, done[0])

            dve.wait_ge(s_raw, 96)
            dve.wait_ge(s_pool_const, 2)
            for i in range(3):
                step(dve.tensor_copy(rec[:, :, i], raw[i][:, :]))
            step(dve.tensor_copy(rec[:, :, 3], slot_no[:, :]))
            cur, before, behind = halo[:, 1:C + 1, 1], halo[:, 0:C, 1], halo[:, 2:C + 2, 1]
            dve.wait_ge(s_halo, 16)
            dve.tensor_tensor(work[0][:, :], cur, before, ALU.is_lt).then_inc(s_disorder, 1)
            dve.wait_ge(s_disorder, 1)
            step(dve.tensor_reduce(small[:, 0:1], work[0][:, :], AX.X, ALU.add))
            dve.wait_ge(s_prep_pe, 1)
            step(dve.tensor_copy(small[:, 1:2], psum[0][:, 0:1]))
            step(dve.tensor_copy(unsorted[:, :], small[:, 1:2]))

            disorder = dve.value_load(unsorted[0:1, 0:1])
            with dve.If(disorder > 0):
                dve.tensor_copy(work[1][:, :], slot_no[:, :])
                dve.memset(work[0][:, :], 1.0)
                dve.tensor_copy(work[2][:, :], raw[1][:, :])
                for chunk in range(CHUNKS):
                    dve.wait_ge(s_rank_in, 16 * (chunk + 1))
                    base = (3 * C + 1) * chunk
                    dve.memset(rank_neg[:, :], -1.0)
                    dve.memset(rank_tmp[:, :], 1.0).then_inc(s_rank, 1)
                    dve.wait_ge(s_rank, base + 1)
                    dve.tensor_tensor_scan(rank_no[:, :], rank_tmp[:, :], rank_neg[:, :],
                                           initial=float(1 - chunk * CH), op0=ALU.mult, op1=ALU.add)\
                        .then_inc(s_rank_no, 1)
                    dve.wait_ge(s_rank_no, chunk + 1)

                    def rank_column(c):
                        k = base + 1 + 3 * c
                        dve.tensor_scalar(rank_tmp[:, :], rank_dst[:, :], work[2][:, bass.ds(c, 1)], float(PAD),
                                          ALU.subtract, ALU.mult).then_inc(s_rank, 1)
                        dve.wait_ge(s_rank, k + 1)
                        dve.scalar_tensor_tensor(rank_tmp[:, :], rank_tmp[:, :], work[1][:, bass.ds(c, 1)],
                                                 rank_no[:, :], ALU.subtract, ALU.is_lt).then_inc(s_rank, 1)
                        dve.wait_ge(s_rank, k + 2)
                        dve.tensor_reduce(rank_sum[:, :], rank_tmp[:, :], AX.X, ALU.add).then_inc(s_rank_sum, 1)
                        dve.wait_ge(s_rank_sum, C * chunk + c + 1)
                        dve.tensor_tensor(work[0][:, bass.ds(c, 1)], work[0][:, bass.ds(c, 1)], rank_sum[:, :],
                                          ALU.add).then_inc(s_rank, 1)
                        dve.wait_ge(s_rank, k + 3)

                    with dve.Fori(0, C) as c:
                        rank_column(c)
                dve.wait_ge(s_rank_done, 1)

            dve.wait_ge(s_sorted, 1)
            same_before, same_behind, first_slot, last_slot = (t[:, :] for t in work)
            m = meta_all
            mf = f32(m[:, :, :])
            no = slot_no[:, :]
            dve.tensor_copy(m[:, :, SRC], halo[:, 1:C + 1, 0])
            dve.tensor_copy(m[:, :, WEIGHT], halo[:, 1:C + 1, 2])
            dve.tensor_scalar(m[:, :, DST], cur, float(N - 1), None, ALU.min)
            dve.tensor_copy(m[:, :, SLOT], no)
            dve.tensor_tensor(mf[:, :, IS_END], cur, behind, ALU.not_equal)
            dve.tensor_tensor(same_before, cur, before, ALU.is_equal)
            step(dve.tensor_tensor(same_behind, cur, behind, ALU.is_equal))
            dve.tensor_copy(flag_tile[:, 0, :], same_before)
            dve.tensor_copy(flag_tile[:, 1, :], same_behind)
            dve.tensor_scalar(first_slot, same_before, -1.0, 1.0, ALU.mult, ALU.add)
            step(dve.tensor_scalar(last_slot, same_behind, -1.0, 1.0, ALU.mult, ALU.add))
            dve.scalar_tensor_tensor(m[:, :, START_DST], cur, float(-FAR), first_slot, ALU.add, ALU.mult)
            step(dve.scalar_tensor_tensor(m[:, :, END_DST], cur, float(-FAR), last_slot, ALU.add, ALU.mult))
            dve.tensor_scalar(m[:, :, START_DST], m[:, :, START_DST], float(FAR), None, ALU.add)
            step(dve.tensor_scalar(m[:, :, END_DST], m[:, :, END_DST], float(FAR), None, ALU.add))
            dve.tensor_tensor(same_before, first_slot, no, ALU.mult)
            step(dve.scalar_tensor_tensor(same_behind, no, float(-FAR), last_slot, ALU.add, ALU.mult))
            step(dve.tensor_scalar(same_behind, same_behind, float(FAR), None, ALU.add))
            dve.tensor_tensor_scan(first_slot, same_before, same_before, initial=0.0, op0=ALU.max, op1=ALU.max)
            step(dve.tensor_tensor_scan(backwards(last_slot), backwards(same_behind), backwards(same_behind),
                                        initial=float(FAR), op0=ALU.min, op1=ALU.min))
            step(dve.tensor_copy(small[:, 2:3], first_slot[:, C - 1:C]))
            step(dve.tensor_copy(small[:, 3:4], last_slot[:, 0:1]))
            dve.wait_ge(s_prep_pe, 3)
            dve.tensor_copy(row1[0:1, 0, :], psum[1][0:1, 0:P])
            dve.memset(row1[0:1, 2, 0:1], 0.0)
            dve.memset(row1[0:1, 3, P - 1:P], float(FAR))
            step(dve.tensor_copy(row1[0:1, 1, :], psum[2][0:1, 0:P]))
            step(dve.tensor_tensor_scan(row1[0:1, 2, 1:P], row1[0:1, 0, 0:P - 1], row1[0:1, 0, 0:P - 1],
                                        initial=0.0, op0=ALU.max, op1=ALU.max))
            step(dve.tensor_tensor_scan(backwards(row1[0:1, 3, 0:P - 1]), backwards(row1[0:1, 1, 1:P]),
                                        backwards(row1[0:1, 1, 1:P]), initial=float(FAR), op0=ALU.min,
                                        op1=ALU.min))
            step(dve.memset(small[:, 6:7], 0.0))
            dve.wait_ge(s_prep_pe, 5)
            dve.tensor_copy(small[:, 4:5], psum[3][:, 0:1])
            step(dve.tensor_copy(small[:, 5:6], psum[4][:, 0:1]))
            dve.tensor_scalar(first_slot, first_slot, small[:, 4:5], None, ALU.max)
            step(dve.tensor_scalar(last_slot, last_slot, small[:, 5:6], None, ALU.min))
            dve.tensor_copy(m[:, :, FIRST], first_slot)
            step(dve.scalar_tensor_tensor(same_before, last_slot, 1.0, no, ALU.add, ALU.subtract))
            step(dve.reciprocal(mf[:, :, INV_DEG], same_before))
            step(dve.tensor_scalar(mf[:, :, HALF_INV], mf[:, :, INV_DEG], 0.5, None, ALU.mult))
            assert done[0] == PREP_ALL

            def weigh(s, st, rows, result, readers_done):
                dve.wait_ge(s["src_in"][st.s].sem, s["src_in"][st.s].at(64 * (st.h + 1)))
                if st.again:
                    dve.wait_ge(s[readers_done].sem, s[readers_done].at(st.g - 1))
                weight = f32(meta[:, st.s, :, WEIGHT:WEIGHT + 1]).to_broadcast([P, T, D])
                dve.tensor_tensor(result[:, st.s], rows[:, st.s], weight, ALU.mult).then_inc(s["weighted"].sem, 1)

            def scan(s, st, name, result, data, backward, free):
                order = backwards if backward else (lambda ap: ap)
                carry = 0 if backward else GR - 1
                q = s[name]
                if after(st.g, 1):
                    dve.wait_ge(q.sem, q.at(st.g))
                if st.again and free:
                    dve.wait_ge(s[free[0]].sem, s[free[0]].at(free[1] * (st.g - 1)))
                initial = result[0:D, 1 - st.s, carry:carry + 1] if after(st.g, 1) else 0.0
                dve.tensor_tensor_scan(order(result[0:D, st.s, :]), order(flag[:, st.s, :]), order(data),
                                       initial=initial, op0=ALU.mult, op1=ALU.add).then_inc(q.sem, 1)

            sg = signals("A")
            xs, xd, xw, conv, x, h, y1, x1, x2, y2, x3, res = row_tiles[:12]
            tmp = row_tiles[12]
            seg = col_tiles[0]
            dve.wait_ge(s_phase, 1)

            def mix(s, st, bank, own, tmp, y):
                q = s["y1"]
                dve.scalar_tensor_tensor(tmp[:, st.s], rows_of(bank), 0.0, own[:, st.s], ALU.max, ALU.add)\
                    .then_inc(q.sem, 1)
                dve.wait_ge(q.sem, q.at(2 * st.g + 1))
                dve.scalar_tensor_tensor(y[:, st.s], tmp[:, st.s], 0.5, own[:, st.s], ALU.mult, ALU.add)\
                    .then_inc(q.sem, 1)
                dve.wait_ge(q.sem, q.at(2 * st.g + 2))

            def phase_a(at):
                if st := at(0):
                    dve.wait_ge(sg["meta_in"][st.s].sem, sg["meta_in"][st.s].at(32 * (st.h + 1)))
                    weigh(sg, st, xs, xw, "src_turned")
                if st := at(2):
                    dve.wait_ge(sg["ln1_dve"].sem, sg["ln1_dve"].at(7 * (st.g + 1)))
                    ln_stats(dve, sg, 2, st, x1[:, st.s], 7, 3)
                if st := at(3):
                    ln_stats(dve, sg, 3, st, y2[:, st.s], 7, 3)
                if st := at(0):
                    dve.wait_ge(sg["src_turned"].sem, sg["src_turned"].at(st.g + 1))
                    scan(sg, st, "scanned", seg, psum[0][0:D, :], False, ("conv_done", 1))
                if st := at(1):
                    dve.wait_ge(sg["loop2_done"].sem, sg["loop2_done"].at(st.g + 1))
                    mix(sg, st, 6, x, tmp, y1)
                    ln_stats(dve, sg, 1, st, y1[:, st.s], 7, 2)
                if st := at(2):
                    ln_scale(dve, sg, 2, st, 7, 3)
                if st := at(3):
                    ln_scale(dve, sg, 3, st, 7, 3)
                if st := at(1):
                    ln_scale(dve, sg, 1, st, 7, 2)
                    if st.again:
                        dve.wait_ge(sg["x1_stored"][st.s].sem, sg["x1_stored"][st.s].at(16 * st.h))
                        dve.wait_ge(sg["ln2_act"].sem, sg["ln2_act"].at(3 * (st.g - 1)))
                    ln_apply_dve(dve, sg, 1, st, y1[:, st.s], x1[:, st.s])
                if st := at(3):
                    dve.wait_ge(sg["ln3_act"].sem, sg["ln3_act"].at(3 * (st.g + 1)))
                    ln_stats(dve, sg, 4, st, x3[:, st.s], 7, 2)
                if st := at(2):
                    dve.wait_ge(sg["mlp2_done"].sem, sg["mlp2_done"].at(st.g + 1))
                    if st.again:
                        dve.wait_ge(sg["ln3_act"].sem, sg["ln3_act"].at(3 * (st.g - 1)))
                    dve.tensor_tensor(y2[:, st.s], rows_of(5), x2[:, st.s], ALU.add).then_inc(sg["y2"].sem, 1)
                    dve.wait_ge(sg["y2"].sem, sg["y2"].at(st.g + 1))
                if st := at(3):
                    ln_scale(dve, sg, 4, st, 7, 2)
                    if st.again:
                        dve.wait_ge(sg["x3_stored"][st.s].sem, sg["x3_stored"][st.s].at(32 * st.h))
                    ln_apply_dve(dve, sg, 4, st, x3[:, st.s], res[:, st.s])

            ticks(dve, NG, 3, phase_a)

            sb_ = signals("B")
            dve.wait_ge(s_phase, 2)

            def phase_b(at):
                st = at(0)
                q = sb_["ids_made"]
                dve.wait_ge(sb_["src_in"][st.s].sem, sb_["src_in"][st.s].at(64 * (st.h + 1)))
                if st.again:
                    dve.wait_ge(sb_["ids_stored"][st.s].sem, sb_["ids_stored"][st.s].at(16 * st.h))
                dve.tensor_copy(srcs[:, st.s, :, 0:2], ids[:, st.s, :, :]).then_inc(q.sem, 1)
                dve.tensor_scalar(srcs[:, st.s, :, 2:4], ids[:, st.s, :, 1:2].to_broadcast([P, T, 2]), float(EP), None, ALU.min).then_inc(q.sem, 1)

            ticks(dve, NG, 0, phase_b)

            sc = signals("C")
            hs, hown, x, xw, y1, x1, tmp = row_tiles[:7]
            dve.wait_ge(s_phase, 3)

            def phase_c(at):
                if st := at(0):
                    dve.wait_ge(sc["meta_in"][st.s].sem, sc["meta_in"][st.s].at(48 * (st.h + 1)))
                    weigh(sc, st, hs, xw, "src_turned")
                if st := at(1):
                    dve.wait_ge(sc["x_in"][st.s].sem, sc["x_in"][st.s].at(32 * (st.h + 1)))
                    dve.wait_ge(sc["conv_done"].sem, sc["conv_done"].at(st.g + 1))
                    if st.again:
                        dve.wait_ge(sc["ln1_act"].sem, sc["ln1_act"].at(3 * (st.g - 1)))
                    mix(sc, st, 2, x, tmp, y1)
                    ln_stats(dve, sc, 1, st, y1[:, st.s], 8, 3)
                if st := at(0):
                    dve.wait_ge(sc["src_turned"].sem, sc["src_turned"].at(st.g + 1))
                    scan(sc, st, "scanned", seg, psum[0][0:D, :], False, ("conv_done", 1))
                if st := at(1):
                    ln_scale(dve, sc, 1, st, 8, 3, f32(word(st.s, IS_END)))

            ticks(dve, NG, 1, phase_c)

            sd = signals("D")
            xs_c, xf_c, ea_c, k_c, sc_c, ex_c, wv_c, z_c, y_c = col_tiles
            dve.wait_ge(s_phase, 4)

            def phase_d(at):
                if st := at(1):
                    q = sd["score"]
                    dve.wait_ge(sd["k_cols"].sem, sd["k_cols"].at(st.g + 1))
                    dve.wait_ge(sd["q_done"].sem, sd["q_done"].at(st.g + 1))
                    if st.again:
                        dve.wait_ge(sd["sum_done"].sem, sd["sum_done"].at(st.g - 1))
                    dve.tensor_tensor(sc_c[0:D, st.s], k_c[0:D, st.s], psum[5][0:D, :], ALU.mult).then_inc(q.sem, 1)
                    dve.wait_ge(q.sem, q.at(2 * st.g + 1))
                    dve.wait_ge(sd["e_done"].sem, sd["e_done"].at(st.g + 1))
                    dve.tensor_tensor(sc_c[0:D, st.s], sc_c[0:D, st.s], psum[6][0:D, :], ALU.mult).then_inc(q.sem, 1)
                if st := at(0):
                    dve.wait_ge(sd["meta_in"][st.s].sem, sd["meta_in"][st.s].at(32 * (st.h + 1)))
                    dve.wait_ge(sd["own_turned"].sem, sd["own_turned"].at(st.g + 1))
                    if st.again:
                        dve.wait_ge(sd["q_done"].sem, sd["q_done"].at(st.g - 1))
                    scan(sd, st, "filled", xf_c, psum[1][0:D, :], True, ("attn", 4))
                if st := at(1):
                    dve.wait_ge(sd["sum_done"].sem, sd["sum_done"].at(st.g + 1))
                    dve.wait_ge(sd["score"].sem, sd["score"].at(2 * (st.g + 1)))
                    dve.tensor_scalar(k_c[0:D, st.s], psum[3][0:D, :], -5.0, 5.0, ALU.max, ALU.min)\
                        .then_inc(sd["clipped"].sem, 1)
                if st := at(2):
                    dve.wait_ge(sd["y_turned"].sem, sd["y_turned"].at(st.g + 1))
                    ln_stats(dve, sd, 1, st, rows_of(7), 7, 3)
                if st := at(1):
                    dve.wait_ge(sd["exped"].sem, sd["exped"].at(st.g + 1))
                    dve.wait_ge(sd["v_done"].sem, sd["v_done"].at(st.g + 1))
                    dve.tensor_tensor(sc_c[0:D, st.s], psum[4][0:D, :], ex_c[0:D, st.s], ALU.mult)\
                        .then_inc(sd["msg"].sem, 1)
                    scan(sd, st, "z_scanned", z_c, ex_c[0:D, st.s], True, None)
                    dve.wait_ge(sd["msg"].sem, sd["msg"].at(st.g + 1))
                    scan(sd, st, "scanned", wv_c, sc_c[0:D, st.s], True, None)
                if st := at(2):
                    ln_scale(dve, sd, 1, st, 7, 3)
                if st := at(1):
                    q = sd["attn"]
                    k = 4 * st.g
                    if st.again:
                        dve.wait_ge(sd["y_turned"].sem, sd["y_turned"].at(st.g - 1))
                    y = y_c[0:D, st.s]
                    dve.wait_ge(sd["z_scanned"].sem, sd["z_scanned"].at(st.g + 1))
                    dve.tensor_scalar(y, z_c[0:D, st.s], 1e-6, None, ALU.add).then_inc(q.sem, 1)
                    dve.wait_ge(q.sem, q.at(k + 1))
                    dve.reciprocal(y, y).then_inc(q.sem, 1)
                    dve.wait_ge(q.sem, q.at(k + 2))
                    dve.wait_ge(sd["scanned"].sem, sd["scanned"].at(st.g + 1))
                    dve.tensor_tensor(y, y, wv_c[0:D, st.s], ALU.mult).then_inc(q.sem, 1)
                    dve.wait_ge(q.sem, q.at(k + 3))
                    dve.wait_ge(sd["filled"].sem, sd["filled"].at(st.g + 1))
                    dve.tensor_tensor(y, y, xf_c[0:D, st.s], ALU.add).then_inc(q.sem, 1)

            ticks(dve, NG, 2, phase_d)

            se = signals("E")
            xs, xo, y2, x3 = row_tiles[:4]
            seg, rst, g_c = col_tiles[:3]
            dve.wait_ge(s_phase, 5)

            def phase_e(at):
                if st := at(0):
                    dve.wait_ge(se["meta_in"][st.s].sem, se["meta_in"][st.s].at(32 * (st.h + 1)))
                    dve.wait_ge(se["src_turned"].sem, se["src_turned"].at(st.g + 1))
                    scan(se, st, "scanned", seg, psum[0][0:D, :], True, ("rst", 1))
                    dve.wait_ge(se["scanned"].sem, se["scanned"].at(st.g + 1))
                    if st.again:
                        dve.wait_ge(se["mlp1_done"].sem, se["mlp1_done"].at(st.g - 1))
                    dve.wait_ge(se["own_turned"].sem, se["own_turned"].at(st.g + 1))
                    dve.tensor_tensor(rst[0:D, st.s], psum[1][0:D, :], seg[0:D, st.s], ALU.add)\
                        .then_inc(se["rst"].sem, 1)
                if st := at(1):
                    dve.wait_ge(se["mlp2_done"].sem, se["mlp2_done"].at(st.g + 1))
                    dve.wait_ge(se["x_in"][st.s].sem, se["x_in"][st.s].at(16 * (st.h + 1)))
                    if st.again:
                        dve.wait_ge(se["ln1_act"].sem, se["ln1_act"].at(3 * (st.g - 1)))
                    dve.tensor_tensor(y2[:, st.s], rows_of(3), xo[:, st.s], ALU.add).then_inc(se["y2"].sem, 1)
                    dve.wait_ge(se["y2"].sem, se["y2"].at(st.g + 1))
                    ln_stats(dve, se, 1, st, y2[:, st.s], 7, 3)
                    ln_scale(dve, se, 1, st, 7, 3)

            ticks(dve, NG, 1, phase_e)

            sf = signals("F")
            dve.wait_ge(s_phase, 6)

            def phase_f(at):
                st = at(0)
                dve.wait_ge(sf["meta_in"][st.s].sem, sf["meta_in"][st.s].at(48 * (st.h + 1)))
                dve.wait_ge(sf["src_turned"].sem, sf["src_turned"].at(st.g + 1))
                scan(sf, st, "scanned", seg, psum[0][0:D, :], True, ("y_turned", 1))

            ticks(dve, NG, 0, phase_f)

            sh = signals("G")
            xs, xo, mo, t1, y2, res = row_tiles[:6]
            dve.wait_ge(s_phase, 7)

            def phase_g(at):
                st = at(0)
                dve.wait_ge(sh["meta_in"][st.s].sem, sh["meta_in"][st.s].at(48 * (st.h + 1)))
                dve.wait_ge(sh["x_in"][st.s].sem, sh["x_in"][st.s].at(32 * (st.h + 1)))
                dve.scalar_tensor_tensor(t1[:, st.s], mo[:, st.s], 0.5, xo[:, st.s], ALU.mult, ALU.add)\
                    .then_inc(sh["y1"].sem, 1)
                dve.wait_ge(sh["src_turned"].sem, sh["src_turned"].at(st.g + 1))
                scan(sh, st, "scanned", seg, psum[0][0:D, :], True, ("y_turned", 1))
                dve.wait_ge(sh["y1"].sem, sh["y1"].at(st.g + 1))
                dve.wait_ge(sh["y_turned"].sem, sh["y_turned"].at(st.g + 1))
                if st.again:
                    dve.wait_ge(sh["ln1_act"].sem, sh["ln1_act"].at(3 * (st.g - 1)))
                for t in range(T):
                    last = dve.scalar_tensor_tensor(y2[:, st.s, t, :], rows_of(1)[:, t, :],
                                                    f32(meta[:, st.s, t, HALF_INV:HALF_INV + 1]),
                                                    t1[:, st.s, t, :], ALU.mult, ALU.add)
                last.then_inc(sh["y2"].sem, 1)
                dve.wait_ge(sh["y2"].sem, sh["y2"].at(st.g + 1))
                ln_stats(dve, sh, 1, st, y2[:, st.s], 7, 3)
                ln_scale(dve, sh, 1, st, 7, 3)

            ticks(dve, NG, 0, phase_g)


PREP_ALL = 25

_INS = ["x", "src", "dst", "edge_attr_96", "edge_weight", "L0_gnn_W1", "L0_gnn_W1_loop", "L0_gnn_b1", "L0_gnn_W2",
        "L0_gnn_W2_loop", "L0_gnn_b2", "L1_gnn_Wq", "L1_gnn_bq", "L1_gnn_Wk", "L1_gnn_bk", "L1_gnn_We",
        "L1_gnn_be", "L1_gnn_Wv", "L1_gnn_bv", "L2_gnn_W1", "L2_gnn_b1", "L2_gnn_W2", "L2_gnn_b2"]


def kernel(**inputs):
    import numpy as _np
    import concourse.bacc as _bacc
    from concourse import mybir as _mybir
    from concourse.bass_utils import run_bass_kernel_spmd as _run

    nc = _bacc.Bacc("TRN2", target_bir_lowering=False, num_devices=1)
    arrays, args = {}, {}
    for name in _INS:
        v = _np.ascontiguousarray(inputs[name])
        arrays[f"in_{name}_dram"] = v
        args[name] = nc.dram_tensor(f"in_{name}_dram", v.shape, _mybir.dt.from_np(v.dtype), kind="ExternalInput").ap()
    out = nc.dram_tensor("out_0_dram", inputs["x"].shape, _mybir.dt.float32, kind="ExternalOutput").ap()
    gnn_kernel(nc, args, out)
    r = _run(nc, [arrays], core_ids=[0])
    return r.results[0]["out_0_dram"]
```

```python
import math
from contextlib import ExitStack

import concourse.bass as bass
from concourse import mybir

F32 = mybir.dt.float32
I32 = mybir.dt.int32
BF16 = mybir.dt.bfloat16
ALU = mybir.AluOpType
ACT = mybir.ActivationFunctionType
AX = mybir.AxisListType

P = 128
T = 4
GR = P * T
EPS = 1e-5
FAR = 1 << 20
PAD = 1 << 16

SRC, DST, WEIGHT, END_DST, START_DST, SLOT, FIRST, INV_DEG, IS_END, HALF_INV = range(10)
NF = 10

DEPTH = 4

ENGINE_SIGNALS = {
    "A": dict(weighted=1, scanned=1, src_turned=1, own_turned=1, own_cols=1, conv_done=1, conv_out=1,
              x_turned=1, x_cols=1, loop1_done=1, h_rows=1, h_turned=1, h_cols=1, loop2_done=1, y1=2,
              ln1_dve=7, ln1_act=2, ln2_dve=7, ln2_act=3, ln3_dve=7, ln3_act=3,
              x2_turned=1, x2_cols=1, mlp1_done=1, mlp_hidden=1, mlp2_done=1, y2=1),
    "B": dict(ids_made=2, ln1_dve=7, ln1_act=3),
    "C": dict(weighted=1, scanned=1, src_turned=1, own_turned=1, own_cols=1, conv_done=1, y1=2,
              ln1_dve=8, ln1_act=3),
    "D": dict(src_turned=1, own_turned=1, edge_turned=1, src_cols=1, edge_cols=1, k_cols=1, filled=1,
              k_done=1, q_done=1, e_done=1, v_done=1, score=2, sum_done=1, exped=1, clipped=1,
              msg=1, scanned=1, z_scanned=1, z_guarded=1, attn=2, y_turned=1, divided=3, ln1_dve=7,
              ln1_act=3),
    "E": dict(src_turned=1, own_turned=1, scanned=1, rst=1, mlp1_done=1, mlp_hidden=1, mlp2_done=1,
              y2=1, ln1_dve=7, ln1_act=3),
    "F": dict(src_turned=1, scanned=1, y_turned=1, conv_out=1),
    "G": dict(src_turned=1, scanned=1, y_turned=1, y1=1, y2=1, ln1_dve=7, ln1_act=3),
}
DMA_SIGNALS = {
    "A": dict(meta_in=2, x_in=1, ids_out=4, src_in=4, own_in=4, own_out=1, conv_stored=1, h_stored=1,
              x1_stored=1, x2_stored=1, x3_stored=1),
    "B": dict(meta_in=1, x_in=1, src_in=4, ids_stored=1, x1_stored=1),
    "C": dict(source_in=1, meta_in=2, x_in=2, src_in=4, x1_stored=1),
    "D": dict(source_in=1, meta_in=1, x_in=1, edge_in=1, src_in=4, x1_stored=1),
    "E": dict(source_in=1, meta_in=1, x_in=1, src_in=4, x1_stored=1),
    "F": dict(source_in=1, meta_in=2, src_in=4, x1_stored=1),
    "G": dict(source_in=1, meta_in=1, index_in=1, x_in=2, src_in=4, ids_out=4),
}
PHASES = "ABCDEFG"


class Step:

    def __init__(self, g, s, h, groups):
        self.g, self.s, self.h, self.groups = g, s, h, groups
        self.s2 = s % 2

    def back(self, n):
        if isinstance(self.g, int) and self.g < n:
            return None
        s = (self.s - n) % DEPTH
        return Step(self.g - n, s, self.h + (self.s - n - s) // DEPTH, self.groups)

    def ahead(self, n):
        if isinstance(self.g, int):
            n = min(n, self.groups - 1 - self.g)
        s = (self.s + n) % DEPTH
        return Step(self.g + n, s, self.h + (self.s + n - s) // DEPTH, self.groups)


class Signal:

    def __init__(self, sem, base, per):
        self.sem, self.base, self.per = sem, base, per

    def of(self, st, part=None):
        return self.sem, self.base + self.per * st.g + (self.per if part is None else part)


class DmaSignal:

    def __init__(self, sems, bases, per):
        self.sems, self.bases, self.per = sems, bases, per

    def of(self, st):
        return self.sems[st.s], self.bases[st.s] + 16 * self.per * (st.h + 1)


def ticks(eng, groups, delay, body):
    warm = -(-(delay + DEPTH) // DEPTH)

    def tick(n, u, j):
        def at(k):
            s = (u - k) % DEPTH
            g = n - k
            if isinstance(g, int) and not 0 <= g < groups:
                return None
            return Step(g, s, j + (u - k - s) // DEPTH, groups)

        body(at)

    for n in range(DEPTH * warm):
        tick(n, n % DEPTH, n // DEPTH)
    rounds = (groups - 1) // DEPTH
    assert rounds > warm
    with eng.Fori(warm, rounds) as j:
        for u in range(DEPTH):
            tick(DEPTH * j + u, u, j)
    for n in range(DEPTH * rounds, groups + delay):
        tick(n, n % DEPTH, n // DEPTH)


def gnn_kernel(nc, a, out):
    N, D = a["x"].shape
    E = a["src"].shape[0]
    NG = -(-E // GR)
    NG += NG % 2
    EP = NG * GR
    C = EP // P
    NLAST = N - (NG - 1) * GR
    HEADS = 8
    HD = D // HEADS
    CHUNKS = 32
    CH = EP // CHUNKS
    assert N == E and 0 < NLAST <= GR and NLAST % T == 0 and D < P

    def dram(name, shape, dt=F32):
        return nc.dram_tensor(name, shape, dt, kind="Internal").ap()

    edges = dram("edges", (EP + 2, 4), I32)
    dst_list = dram("dst_list", (EP,), I32)
    edges2 = dram("edges2", (EP + 1, D))
    edge_rows = dram("edge_rows", (EP, D))
    meta_t = dram("meta_t", (EP, NF), I32)
    flags_f = dram("flags_f", (EP,), BF16)
    flags_b = dram("flags_b", (EP,), BF16)
    place = dram("place", (EP, 2), I32)
    source = dram("source", (EP, 4), I32)
    x_own = dram("x_own", (EP, D))
    h_t = dram("h_t", (2 * EP, D))
    x1_t = dram("x1_t", (2 * EP, D))
    x2_t = dram("x2_t", (2 * EP, D))
    x3_t = dram("x3_t", (2 * EP, D))
    mean_t = dram("mean_t", (EP + 1, D))

    def groups(t):
        return t.rearrange("(g p t) d -> g p (t d)", p=P, t=T)

    nodes_in = a["x"][0:(NG - 1) * GR, :]
    nodes_out = out[0:(NG - 1) * GR, :]

    with ExitStack() as ctx:
        def sb(name, shape, dt=F32):
            return ctx.enter_context(nc.sbuf_tensor(name, shape, dt))

        def sem(name):
            return ctx.enter_context(nc.semaphore(name))

        deep_rows = [sb(f"deep_rows{i}", [P, DEPTH, T, D]) for i in range(3)]
        row_tiles = [sb(f"rows{i}", [P, 2, T, D]) for i in range(9)]
        deep_cols = sb("deep_cols", [D + 1, DEPTH, GR])
        col_tiles = [sb(f"cols{i}", [D + 1, 2, GR]) for i in range(8)]
        meta = sb("meta", [P, DEPTH, T, NF], I32)
        srcs = sb("srcs", [P, DEPTH, T, 4], I32)
        ids = sb("ids", [P, 2, T, 2], I32)
        flag = sb("flag", [D, DEPTH, GR], BF16)
        ln_tiles = [(sb(f"ln_st{i}", [P, 2, T, 6]), sb(f"ln_mv{i}", [P, 2, T, 2]), sb(f"ln_s{i}", [P, 2, 7, T]))
                    for i in range(3)]
        z_r = sb("z_rows", [P, 2, 2, T, HEADS])
        ident = sb("ident", [P, P])
        ones = sb("ones", [P, P])
        head_sum = sb("head_sum", [D, D])
        w = {n: sb(n, [D, D]) for n in ("L0_gnn_W1", "L0_gnn_W2")}
        for n in ("L0_gnn_W1_loop", "L0_gnn_W2_loop", "L1_gnn_Wq", "L1_gnn_Wk", "L1_gnn_We", "L1_gnn_Wv",
                  "L2_gnn_W1", "L2_gnn_W2"):
            w[n] = sb(n, [D + 1, D])
        bias_of = {"L0_gnn_W1_loop": "L0_gnn_b1", "L0_gnn_W2_loop": "L0_gnn_b2", "L1_gnn_Wq": "L1_gnn_bq",
                   "L1_gnn_Wk": "L1_gnn_bk", "L1_gnn_We": "L1_gnn_be", "L1_gnn_Wv": "L1_gnn_bv",
                   "L2_gnn_W1": "L2_gnn_b1", "L2_gnn_W2": "L2_gnn_b2"}
        psum = [ctx.enter_context(nc.psum_tensor(f"bank{i}", [P, GR], F32)) for i in range(8)]

        raw = [sb(f"raw{i}", [P, C], I32) for i in range(3)]
        rec = sb("rec", [P, C, 4], I32)
        halo = sb("halo", [P, C + 2, 4], I32)
        slot_no = sb("slot_no", [P, C], I32)
        node_row = sb("node_row", [P, C, 2], I32)
        work = [sb(f"work{i}", [P, C]) for i in range(4)]
        flag_tile = sb("flag_tile", [P, 2, C], BF16)
        meta_all = sb("meta_all", [P, C, NF], I32)
        small = sb("small", [P, 16])
        row1 = sb("row1", [1, 4, P])
        ends = sb("ends", [1, 2, 4], I32)
        zero_row = sb("zero_row", [1, D])
        unsorted = sb("unsorted", [P, 1], I32)
        rank_dst = sb("rank_dst", [P, CH], I32)
        rank_tmp = sb("rank_tmp", [P, CH])
        rank_neg = sb("rank_neg", [P, CH])
        rank_no = sb("rank_no_row", [P, CH])
        rank_sum = sb("rank_sum_col", [P, 1])
        rank_idx = sb("rank_idx", [P, 1], I32)
        rank_rec = sb("rank_rec", [P, 4], I32)
        rank_row = sb("rank_row", [P, D])

        names = []
        for table in (ENGINE_SIGNALS, DMA_SIGNALS):
            for uses in table.values():
                names += [n for n in uses if n not in names]
        engine_sems = {n: sem(n) for n in names if any(n in u for u in ENGINE_SIGNALS.values())}
        dma_sems = {n: [sem(f"{n}{s}") for s in range(DEPTH)] for n in names
                    if any(n in u for u in DMA_SIGNALS.values())}
        in_slot = [len(range(s, NG, DEPTH)) for s in range(DEPTH)]

        def signals(phase):
            found = {}
            earlier = PHASES[:PHASES.index(phase)]
            for n, per in ENGINE_SIGNALS[phase].items():
                found[n] = Signal(engine_sems[n], sum(ENGINE_SIGNALS[p].get(n, 0) for p in earlier) * NG, per)
            for n, per in DMA_SIGNALS[phase].items():
                dmas = sum(DMA_SIGNALS[p].get(n, 0) for p in earlier)
                found[n] = DmaSignal(dma_sems[n], [16 * dmas * c for c in in_slot], per)
            return found

        s_settled = sem("settled")
        s_phase = sem("phase_done")
        s_weights = sem("weights_in")
        s_raw = sem("raw_in")
        s_edge_copy = sem("edge_copy")
        s_pool_const = sem("pool_const")
        s_pads = sem("pads_set")
        s_prep = sem("prep_dve")
        s_prep_pe = sem("prep_pe")
        s_rec_out = sem("rec_out")
        s_halo = sem("halo_in")
        s_sorted = sem("list_sorted")
        s_tables_out = sem("tables_out")
        s_rank = sem("rank_dve")
        s_disorder = sem("disorder")
        s_rank_no = sem("rank_no")
        s_rank_sum = sem("rank_sum")
        s_rank_in = sem("rank_in")
        s_rank_copy = sem("rank_copy")
        s_rank_row = sem("rank_row_in")
        s_rank_out = sem("rank_out")
        s_rank_done = sem("rank_done")

        block = ctx.enter_context(nc.Block())

        def settle(eng):
            eng.sem_inc(s_settled, 1)

        def f32(tile):
            return tile.bitcast(F32)

        def word(st, f):
            return meta[:, st.s, :, f]

        def backwards(ap):
            (ps, pn), (fs, fn) = ap.ap
            return bass.AP(ap.tensor, ap.offset + fs * (fn - 1), [[ps, pn], [-fs, fn]])

        def lanes(tile):
            return tile.rearrange("d (p t) -> d p t", t=T)

        def rows_of(bank):
            return psum[bank][:, 0:T * D].rearrange("p (t d) -> p t d", t=T)

        def head_rows(bank):
            return psum[bank][:, T * D:T * D + T * HEADS].rearrange("p (t h) -> p t h", t=T)

        def flat(tile):
            return tile.rearrange("p t d -> p (t d)")

        def turn(pe, bank, rows):
            for t in range(T):
                last = pe.transpose(lanes(psum[bank][0:D, :])[:, :, t], rows[:, t, :], ident[:, :])
            return last

        def turn_back(pe, bank, cols):
            for t in range(T):
                last = pe.transpose(rows_of(bank)[:, t, :], lanes(cols)[:, :, t], ident[0:D, 0:D])
            return last

        def times(pe, bank, *products):
            for t in range(T):
                for i, (cols, weight) in enumerate(products):
                    last = pe.matmul(rows_of(bank)[:, t, :], lanes(cols)[:, :, t], weight,
                                     start=(i == 0), stop=(i == len(products) - 1))
            return last

        def times_cols(pe, bank, cols, weight):
            return pe.matmul(psum[bank][0:D, :], weight, cols, start=True, stop=True)

        def ln_stats(dve, sg, n, st, y):
            stats, mv, sc = ln_tiles[n - 1]
            d, ac = sg[f"ln{n}_dve"], sg[f"ln{n}_act"]
            for t in range(T):
                last = dve.bn_stats(stats[:, st.s2, t, :], y[:, t, :])
            last.then_inc(d.sem, 1)
            dve.wait_ge(*d.of(st, 1))
            if ac.per == 3 and (old := st.back(2)):
                dve.wait_ge(*ac.of(old))
            settle(dve)
            for t in range(T):
                last = dve.bn_aggr(mv[:, st.s2, t, :], stats[:, st.s2, t, :])
            last.then_inc(d.sem, 1)
            dve.wait_ge(*d.of(st, 2))
            dve.tensor_scalar(sc[:, st.s2, 0, :], mv[:, st.s2, :, 1], EPS, None, ALU.add).then_inc(d.sem, 1)

        def ln_root(act, sg, n, st):
            _, _, sc = ln_tiles[n - 1]
            d, ac = sg[f"ln{n}_dve"], sg[f"ln{n}_act"]
            act.wait_ge(*d.of(st, 3))
            act.activation(sc[:, st.s2, 1, :], sc[:, st.s2, 0, :], ACT.Ln).then_inc(ac.sem, 1)
            act.wait_ge(*ac.of(st, 1))
            act.activation(sc[:, st.s2, 2, :], sc[:, st.s2, 1, :], ACT.Exp, scale=-0.5).then_inc(ac.sem, 1)

        def ln_scale(dve, sg, n, st, mask=None):
            _, mv, sc = ln_tiles[n - 1]
            d, ac = sg[f"ln{n}_dve"], sg[f"ln{n}_act"]
            v, r0, t1, t2 = (sc[:, st.s2, i, :] for i in (0, 2, 3, 4))
            r, nb = sc[:, st.s2, 5, :], sc[:, st.s2, 6, :]
            dve.wait_ge(*ac.of(st, 2))
            dve.tensor_tensor(t1, v, r0, ALU.mult).then_inc(d.sem, 1)
            dve.wait_ge(*d.of(st, 4))
            dve.scalar_tensor_tensor(t2, t1, -0.5, r0, ALU.mult, ALU.mult).then_inc(d.sem, 1)
            dve.wait_ge(*d.of(st, 5))
            dve.scalar_tensor_tensor(r, t2, 1.5, r0, ALU.add, ALU.mult).then_inc(d.sem, 1)
            dve.wait_ge(*d.of(st, 6))
            if mask is not None:
                dve.tensor_tensor(r, r, mask, ALU.mult).then_inc(d.sem, 1)
                dve.wait_ge(*d.of(st, 7))
            if ac.per == 3:
                dve.scalar_tensor_tensor(nb, mv[:, st.s2, :, 0], -1.0, r, ALU.mult, ALU.mult).then_inc(d.sem, 1)

        def ln_apply_dve(dve, sg, n, st, y, result):
            _, mv, sc = ln_tiles[n - 1]
            for t in range(T):
                last = dve.tensor_scalar(result[:, t, :], y[:, t, :], mv[:, st.s2, t, 0:1],
                                         sc[:, st.s2, 5, t:t + 1], ALU.subtract, ALU.mult)
            last.then_inc(sg[f"ln{n}_dve"].sem, 1)

        def ln_apply_act(act, sg, n, st, y, result):
            _, _, sc = ln_tiles[n - 1]
            act.wait_ge(*sg[f"ln{n}_dve"].of(st))
            for t in range(T):
                last = act.activation(result[:, t, :], y[:, t, :], ACT.Identity,
                                      bias=sc[:, st.s2, 6, t:t + 1], scale=sc[:, st.s2, 5, t:t + 1])
            last.then_inc(sg[f"ln{n}_act"].sem, 1)

        @block.sync
        def _(sp):
            for n, tile in w.items():
                sp.dma_start(tile[0:D, :], a[n]).then_inc(s_weights, 16)
                if n in bias_of:
                    sp.dma_start(tile[D:D + 1, :], a[bias_of[n]].unsqueeze(0)).then_inc(s_weights, 16)
            sp.wait_ge(s_pads, 5)
            full = E // C
            for i, name in enumerate(("src", "dst", "edge_weight")):
                v = a[name] if name != "edge_weight" else a[name].bitcast(I32)
                sp.dma_start(raw[i][0:full, :], v[0:full * C].rearrange("(p c) -> p c", c=C)).then_inc(s_raw, 16)
                sp.dma_start(raw[i][full:full + 1, 0:E - full * C], v[full * C:E].unsqueeze(0)).then_inc(s_raw, 16)
            body = E // GR * GR
            sp.dma_start(edge_rows[0:body, :].rearrange("(p r) d -> p (r d)", p=P),
                         a["edge_attr_96"][0:body, :].rearrange("(p r) d -> p (r d)", p=P)).then_inc(s_edge_copy, 16)
            sp.dma_start(edge_rows[body:E, :], a["edge_attr_96"][body:E, :]).then_inc(s_edge_copy, 16)
            sp.dma_start(edge_rows[E:EP, :], a["edge_attr_96"][0:EP - E, :]).then_inc(s_edge_copy, 16)
            sp.dma_start(mean_t[EP:EP + 1, :], zero_row[:, :]).then_inc(s_edge_copy, 16)

            sp.wait_ge(s_prep, 4)
            sp.dma_start(edges[0:1, :], ends[:, 0, :]).then_inc(s_rec_out, 16)
            sp.dma_start(edges[EP + 1:EP + 2, :], ends[:, 1, :]).then_inc(s_rec_out, 16)
            sp.dma_start(edges[1:EP + 1, :].rearrange("(p c) f -> p (c f)", p=P),
                         rec[:, :, :].rearrange("p c f -> p (c f)")).then_inc(s_rec_out, 16)
            sp.wait_ge(s_rec_out, 48)
            halo_view = bass.AP(edges.tensor, 0, [[4 * C, P], [1, 4 * (C + 2)]])
            sp.dma_start(halo[:, :, :].rearrange("p c f -> p (c f)"), halo_view).then_inc(s_halo, 16)
            sp.wait_ge(s_edge_copy, 64)
            sp.wait_ge(s_prep, 7)
            disorder = sp.value_load(unsorted[0:1, 0:1])
            with sp.If(disorder > 0):
                sp.dma_start(dst_list.rearrange("(p c) -> p c", p=P), raw[1][:, :]).then_inc(s_rec_out, 16)
                sp.wait_ge(s_rec_out, 64)
                for c in range(CHUNKS):
                    if c:
                        sp.wait_ge(s_rank, 3 * C * c + c)
                    chunk = dst_list[c * CH:(c + 1) * CH]
                    sp.dma_start(rank_dst[:, :], chunk.unsqueeze(0).to_broadcast([P, CH])).then_inc(s_rank_in, 16)
                sp.wait_ge(s_rank_done, 1)
                sp.dma_start(edge_rows.rearrange("(p r) d -> p (r d)", p=P),
                             edges2[1:EP + 1, :].rearrange("(p r) d -> p (r d)", p=P)).then_inc(s_edge_copy, 16)
                sp.wait_ge(s_edge_copy, 80)
                sp.dma_start(halo[:, :, :].rearrange("p c f -> p (c f)"), halo_view).then_inc(s_halo, 16)
                sp.wait_ge(s_halo, 32)
            sp.sem_inc(s_sorted, 1)

            sp.wait_ge(s_pool_const, 6)
            sp.dma_start(place.rearrange("(p c) f -> p (c f)", p=P),
                         node_row[:, :, :].rearrange("p c f -> p (c f)")).then_inc(s_tables_out, 16)
            sp.wait_ge(s_prep, PREP_ALL)
            sp.dma_start(meta_t.rearrange("(p c) f -> p (c f)", p=P),
                         meta_all[:, :, :].rearrange("p c f -> p (c f)")).then_inc(s_tables_out, 16)
            sp.dma_start(flags_f.rearrange("(p c) -> p c", p=P), flag_tile[:, 0, :]).then_inc(s_tables_out, 16)
            sp.dma_start(flags_b.rearrange("(p c) -> p c", p=P), flag_tile[:, 1, :]).then_inc(s_tables_out, 16)
            sp.wait_ge(s_tables_out, 64)
            sp.sem_inc(s_phase, 1)

            meta_g = meta_t.rearrange("(g p t) f -> g p t f", p=P, t=T)
            source_g = source.rearrange("(g p t) f -> g p t f", p=P, t=T)

            def free(*signals_of_old):
                for sig, old in signals_of_old:
                    if old:
                        sp.wait_ge(*sig.of(old))
                        settle(sp)

            def load_meta(st, sig, g):
                sp.dma_start(meta[:, st.s, :, :], meta_g[g]).then_inc(sig.sems[st.s], 16)

            def load_flags(st, sig, table, g):
                sp.dma_start(flag[:, st.s, :], table[bass.ds(g * GR, GR)].unsqueeze(0).to_broadcast([D, GR]))\
                    .then_inc(sig.sems[st.s], 16)

            def load_rows(st, sig, tile, table, g):
                sp.dma_start(flat(tile[:, st.s]), groups(table)[g]).then_inc(sig.sems[st.s], 16)

            def load_source(st, sig, g):
                sp.dma_start(srcs[:, st.s, :, :], source_g[g]).then_inc(sig.sems[st.s], 16)

            def finish(sg, *names):
                for n in names:
                    for s in range(DEPTH):
                        sp.wait_ge(sg[n].sems[s], sg[n].bases[s] + 16 * sg[n].per * in_slot[s])
                sp.sem_inc(s_phase, 1)

            sg = signals("A")
            xs, xd, x = deep_rows

            def phase_a(at):
                if st := at(0):
                    old = st.back(DEPTH)
                    free((sg["weighted"], old), (sg["scanned"], old), (sg["own_in"], old), (sg["ids_out"], old))
                    load_meta(st, sg["meta_in"], st.g)
                    load_flags(st, sg["meta_in"], flags_f, st.g)
                    free((sg["y1"], old))
                    if isinstance(st.g, int) and st.g == NG - 1:
                        sp.dma_start(flat(x[0:NLAST // T, st.s]),
                                     a["x"][(NG - 1) * GR:N, :].rearrange("(p t) d -> p (t d)", t=T))\
                            .then_inc(sg["x_in"].sems[st.s], 16)
                    else:
                        load_rows(st, sg["x_in"], x, nodes_in, st.g)

            ticks(sp, NG, 0, phase_a)
            finish(sg, "own_out", "conv_stored", "h_stored", "x1_stored", "x2_stored", "x3_stored", "ids_out")

            sb_ = signals("B")
            x3 = deep_rows[0]

            def phase_b(at):
                if st := at(0):
                    old = st.back(DEPTH)
                    free((sb_["src_in"], old))
                    load_meta(st, sb_["meta_in"], st.g)
                    free((sb_["ln1_act"], old))
                    load_rows(st, sb_["x_in"], x3, x3_t, NG + st.g)

            ticks(sp, NG, 0, phase_b)
            finish(sb_, "ids_stored", "x1_stored")

            sc = signals("C")
            hs, hown, x = deep_rows

            def phase_c(at):
                if st := at(0):
                    old = st.back(DEPTH)
                    free((sc["src_in"], old))
                    load_source(st, sc["source_in"], st.g)
                    free((sc["scanned"], old), (sc["ln1_dve"], old))
                    load_meta(st, sc["meta_in"], st.g)
                    load_flags(st, sc["meta_in"], flags_f, st.g)
                    free((sc["own_turned"], old))
                    load_rows(st, sc["x_in"], hown, h_t, st.g)
                    load_rows(st, sc["x_in"], x, x_own, st.g)

            ticks(sp, NG, 0, phase_c)
            finish(sc, "x1_stored")

            sd = signals("D")
            xs, xo, ea = deep_rows

            def phase_d(at):
                if st := at(0):
                    g = NG - 1 - st.g
                    old = st.back(DEPTH)
                    free((sd["src_in"], old))
                    load_source(st, sd["source_in"], g)
                    free((sd["scanned"], old))
                    load_flags(st, sd["meta_in"], flags_b, g)
                    free((sd["own_turned"], old))
                    load_rows(st, sd["x_in"], xo, x1_t, g)
                    free((sd["edge_turned"], old))
                    load_rows(st, sd["edge_in"], ea, edge_rows, g)

            ticks(sp, NG, 0, phase_d)
            finish(sd, "x1_stored")

            se = signals("E")
            xs, xo = deep_rows[:2]

            def phase_e(at):
                if st := at(0):
                    g = NG - 1 - st.g
                    old = st.back(DEPTH)
                    free((se["src_in"], old))
                    load_source(st, se["source_in"], g)
                    free((se["scanned"], old))
                    load_flags(st, se["meta_in"], flags_b, g)
                    free((se["y2"], old))
                    load_rows(st, se["x_in"], xo, x2_t, g)

            ticks(sp, NG, 0, phase_e)
            finish(se, "x1_stored")

            sf = signals("F")

            def phase_f(at):
                if st := at(0):
                    g = NG - 1 - st.g
                    old = st.back(DEPTH)
                    free((sf["src_in"], old))
                    load_source(st, sf["source_in"], g)
                    free((sf["scanned"], old), (sf["conv_out"], old))
                    load_flags(st, sf["meta_in"], flags_b, g)
                    load_meta(st, sf["meta_in"], g)

            ticks(sp, NG, 0, phase_f)
            finish(sf, "x1_stored")

            sh = signals("G")
            xs, xo, mo = deep_rows

            def phase_g(at):
                if st := at(0):
                    g = NG - 1 - st.g
                    old = st.back(DEPTH)
                    free((sh["src_in"], old))
                    load_source(st, sh["source_in"], g)
                    free((sh["scanned"], old))
                    load_flags(st, sh["meta_in"], flags_b, g)
                    free((sh["y1"], old))
                    load_rows(st, sh["x_in"], xo, x3_t, g)
                    load_rows(st, sh["x_in"], mo, mean_t[0:EP, :], g)
                    free((sh["ids_out"], old))
                    load_meta(st, sh["index_in"], g)

            ticks(sp, NG, 0, phase_g)
            finish(sh, "ids_out")

        def gather(pool, tile, table, index, sig, st):
            pool.indirect_dma_start(out=tile, out_offset=None, in_=table,
                                    in_offset=bass.IndirectOffsetOnAxis(ap=index, axis=0),
                                    bounds_check=table.shape[0] - 1, oob_is_err=False).then_inc(sig.sems[st.s], 16)

        def scatter(pool, table, index, tile, sig, st):
            pool.indirect_dma_start(out=table, out_offset=bass.IndirectOffsetOnAxis(ap=index, axis=0), in_=tile,
                                    in_offset=None, bounds_check=N - 1, oob_is_err=False)\
                .then_inc(sig.sems[st.s], 16)

        @block.gpsimd
        def _(pool):
            pool.iota(slot_no[:, :], [[1, C]], base=0, channel_multiplier=C).then_inc(s_pool_const, 1)
            pool.iota(node_row[:, :, :], [[1, C], [0, 2]], base=EP, channel_multiplier=C).then_inc(s_pool_const, 1)
            pool.memset(ident[:, :], 0.0).then_inc(s_pool_const, 1)
            pool.memset(head_sum[:, :], float(HD) ** -0.5).then_inc(s_pool_const, 1)
            pool.wait_ge(s_pool_const, 4)
            pool.affine_select(out=ident[:, :], in_=ident[:, :], compare_op=ALU.not_equal, fill=1.0, base=0,
                               pattern=[[-1, P]], channel_multiplier=1).then_inc(s_pool_const, 1)
            blocks = head_sum[:, :].rearrange("p (h c) -> p h c", c=HD)
            pool.affine_select(out=blocks, in_=blocks, compare_op=ALU.is_ge, fill=0.0, base=0,
                               pattern=[[-HD, HEADS], [0, HD]], channel_multiplier=1).then_inc(s_pool_const, 1)
            pool.wait_ge(s_pool_const, 6)
            pool.affine_select(out=blocks, in_=blocks, compare_op=ALU.is_ge, fill=0.0, base=HD - 1,
                               pattern=[[HD, HEADS], [0, HD]], channel_multiplier=-1).then_inc(s_pool_const, 1)

            pool.wait_ge(s_prep, 7)
            pool.wait_ge(s_edge_copy, 64)
            disorder = pool.value_load(unsorted[0:1, 0:1])
            with pool.If(disorder > 0):
                pool.wait_ge(s_rank, CHUNKS * (3 * C + 1))
                unsorted_rows = edge_rows.rearrange("(p c) d -> p c d", p=P)

                def move(c, first):
                    if not first:
                        pool.wait_ge(s_rank_out, 32 * c)
                    pool.dma_start(rank_row[:, :], unsorted_rows[:, bass.ds(c, 1), :].rearrange("p c d -> p (c d)"))\
                        .then_inc(s_rank_row, 16)
                    pool.tensor_copy(rank_idx[:, :], work[0][:, bass.ds(c, 1)]).then_inc(s_rank_copy, 1)
                    pool.tensor_copy(rank_rec[:, :], rec[:, bass.ds(c, 1), :].rearrange("p c f -> p (c f)"))\
                        .then_inc(s_rank_copy, 1)
                    pool.wait_ge(s_rank_copy, 2 * c + 2)
                    pool.wait_ge(s_rank_row, 16 * c + 16)
                    settle(pool)
                    for table, tile in ((edges2, rank_row), (edges, rank_rec)):
                        pool.indirect_dma_start(out=table, out_offset=bass.IndirectOffsetOnAxis(
                            ap=rank_idx[:, 0:1], axis=0), in_=tile[:, :], in_offset=None,
                            bounds_check=EP, oob_is_err=False).then_inc(s_rank_out, 16)

                move(0, True)
                with pool.Fori(1, C) as c:
                    move(c, False)
                pool.wait_ge(s_rank_out, 32 * C)
                pool.sem_inc(s_rank_done, 1)

            sg = signals("A")
            xs, xd, x = deep_rows
            pool.wait_ge(s_phase, 1)

            def phase_a(at):
                st = at(0)
                old = st.back(DEPTH)
                pool.wait_ge(*sg["meta_in"].of(st))
                settle(pool)
                for t in range(T):
                    gather(pool, xs[:, st.s, t, :], a["x"], meta[:, st.s, t, SRC:SRC + 1], sg["src_in"], st)
                if old:
                    pool.wait_ge(*sg["own_turned"].of(old))
                    pool.wait_ge(*sg["own_out"].of(old))
                    settle(pool)
                for t in range(T):
                    gather(pool, xd[:, st.s, t, :], a["x"], meta[:, st.s, t, DST:DST + 1], sg["own_in"], st)
                for t in range(T):
                    scatter(pool, place, meta[:, st.s, t, END_DST:END_DST + 1], meta[:, st.s, t, SLOT:SLOT + 2],
                            sg["ids_out"], st)

            ticks(pool, NG, 0, phase_a)

            sb_ = signals("B")
            pool.wait_ge(s_phase, 2)

            def phase_b(at):
                st = at(0)
                pool.wait_ge(*sb_["meta_in"].of(st))
                if old := st.back(2):
                    pool.wait_ge(*sb_["ids_made"].of(old))
                settle(pool)
                for t in range(T):
                    gather(pool, ids[:, st.s2, t, :], place, meta[:, st.s, t, SRC:SRC + 1], sb_["src_in"], st)

            ticks(pool, NG, 0, phase_b)

            def sources(phase, table, field, reader, extra=0, more=None):
                s = signals(phase)
                xs = deep_rows[0]
                pool.wait_ge(s_phase, PHASES.index(phase) + 1)

                def body(at):
                    if st := at(0):
                        pool.wait_ge(*s["source_in"].of(st))
                        if old := st.back(DEPTH):
                            pool.wait_ge(*s[reader].of(old))
                        settle(pool)
                        for t in range(T):
                            gather(pool, xs[:, st.s, t, :], table, srcs[:, st.s, t, field:field + 1],
                                   s["src_in"], st)
                    if more:
                        more(s, at)

                ticks(pool, NG, extra, body)

            def attend(s, at):
                xs_c, ea_c, sc_c, ex_c, wv_c, z_c, y_c, zg_c = col_tiles
                if st := at(3):
                    pool.wait_ge(*s["z_guarded"].of(st))
                    if old := st.back(2):
                        pool.wait_ge(*s["y_turned"].of(old))
                    y = y_c[0:D, st.s2, :]
                    pool.tensor_tensor(y, zg_c[0:D, st.s2, :], deep_cols[0:D, st.s, :], ALU.mult)\
                        .then_inc(s["attn"].sem, 1)
                    pool.wait_ge(*s["attn"].of(st, 1))
                    pool.wait_ge(*s["scanned"].of(st))
                    pool.tensor_tensor(y, y, wv_c[0:D, st.s2, :], ALU.add).then_inc(s["attn"].sem, 1)

            def results(s, at):
                if st := at(3):
                    pool.wait_ge(*s["ln1_act"].of(st))
                    pool.wait_ge(*s["index_in"].of(st))
                    settle(pool)
                    for t in range(T):
                        scatter(pool, out, meta[:, st.s, t, START_DST:START_DST + 1], row_tiles[2][:, st.s2, t, :],
                                s["ids_out"], st)

            sources("C", h_t, 0, "weighted")
            sources("D", x1_t, 0, "src_turned", 3, attend)
            sources("E", x2_t, 1, "src_turned")
            sources("F", x3_t, 1, "src_turned")
            sources("G", mean_t, 2, "src_turned", 3, results)

        @block.tensor
        def _(pe):
            pe.wait_ge(s_pads, 5)
            pe.wait_ge(s_prep, 5)
            pe.matmul(psum[0][:, 0:1], ones[:, :], small[:, 0:1], start=True, stop=True).then_inc(s_prep_pe, 1)
            pe.wait_ge(s_pool_const, 7)
            pe.wait_ge(s_prep, 16)
            pe.transpose(psum[1][0:1, 0:P], small[:, 2:3], ident[:, :]).then_inc(s_prep_pe, 1)
            pe.transpose(psum[2][0:1, 0:P], small[:, 3:4], ident[:, :]).then_inc(s_prep_pe, 1)
            pe.wait_ge(s_prep, 20)
            pe.matmul(psum[3][:, 0:1], row1[0:1, 2, :], ones[0:1, 0:1], start=True, stop=True).then_inc(s_prep_pe, 1)
            pe.matmul(psum[4][:, 0:1], row1[0:1, 3, :], ones[0:1, 0:1], start=True, stop=True).then_inc(s_prep_pe, 1)
            pe.wait_ge(s_weights, 16 * (len(w) + len(bias_of)))

            sg = signals("A")
            xs, xd, x = deep_rows
            xw, conv, h, y1, x1, x2, y2, x3, tmp = row_tiles
            seg, xd_c, x_c, h_c, x2_c, g_c = col_tiles[:6]
            pe.wait_ge(s_phase, 1)

            def phase_a(at):
                if st := at(0):
                    pe.wait_ge(*sg["x_in"].of(st))
                    if old := st.back(1):
                        pe.wait_ge(*sg["x_cols"].of(old))
                    turn(pe, 3, x[:, st.s]).then_inc(sg["x_turned"].sem, 1)
                if st := at(1):
                    pe.wait_ge(*sg["h_rows"].of(st))
                    if old := st.back(4):
                        pe.wait_ge(*sg["mlp_hidden"].of(old))
                    turn(pe, 4, h[:, st.s2]).then_inc(sg["h_turned"].sem, 1)
                if st := at(4):
                    pe.wait_ge(*sg["ln2_act"].of(st))
                    if old := st.back(1):
                        pe.wait_ge(*sg["x2_cols"].of(old))
                    turn(pe, 7, x2[:, st.s2]).then_inc(sg["x2_turned"].sem, 1)
                if st := at(0):
                    pe.wait_ge(*sg["weighted"].of(st))
                    if old := st.back(1):
                        pe.wait_ge(*sg["scanned"].of(old))
                    turn(pe, 0, xw[:, st.s2]).then_inc(sg["src_turned"].sem, 1)
                    pe.wait_ge(*sg["own_in"].of(st))
                    if old := st.back(1):
                        pe.wait_ge(*sg["own_cols"].of(old))
                    turn(pe, 1, xd[:, st.s]).then_inc(sg["own_turned"].sem, 1)
                    pe.wait_ge(*sg["x_cols"].of(st))
                    if old := st.back(5):
                        pe.wait_ge(*sg["y2"].of(old))
                    times(pe, 5, (x_c[:, st.s2], w["L0_gnn_W1_loop"][:, :])).then_inc(sg["loop1_done"].sem, 1)
                if st := at(1):
                    pe.wait_ge(*sg["h_cols"].of(st))
                    if old := st.back(1):
                        pe.wait_ge(*sg["y1"].of(old))
                    times(pe, 6, (h_c[:, st.s2], w["L0_gnn_W2_loop"][:, :])).then_inc(sg["loop2_done"].sem, 1)
                if st := at(4):
                    pe.wait_ge(*sg["x2_cols"].of(st))
                    pe.wait_ge(*sg["h_cols"].of(st.ahead(3)))
                    times_cols(pe, 4, x2_c[:, st.s2], w["L2_gnn_W1"][:, :]).then_inc(sg["mlp1_done"].sem, 1)
                if st := at(0):
                    pe.wait_ge(*sg["scanned"].of(st))
                    pe.wait_ge(*sg["own_cols"].of(st))
                    if old := st.back(1):
                        pe.wait_ge(*sg["conv_out"].of(old))
                    times(pe, 2, (seg[0:D, st.s2], w["L0_gnn_W1"][:, :]),
                          (xd_c[:, st.s2], w["L0_gnn_W1_loop"][:, :])).then_inc(sg["conv_done"].sem, 1)
                if st := at(4):
                    pe.wait_ge(*sg["mlp_hidden"].of(st))
                    pe.wait_ge(*sg["h_rows"].of(st.ahead(4)))
                    times(pe, 5, (g_c[:, st.s2], w["L2_gnn_W2"][:, :])).then_inc(sg["mlp2_done"].sem, 1)

            ticks(pe, NG, 4, phase_a)

            sc = signals("C")
            hs, hown, x = deep_rows
            xw = row_tiles[0]
            seg, h_c = col_tiles[:2]
            pe.wait_ge(s_phase, 3)

            def phase_c(at):
                if st := at(0):
                    pe.wait_ge(*sc["x_in"].of(st))
                    if old := st.back(2):
                        pe.wait_ge(*sc["own_cols"].of(old))
                    turn(pe, 2 + st.s2, hown[:, st.s]).then_inc(sc["own_turned"].sem, 1)
                    pe.wait_ge(*sc["weighted"].of(st))
                    if old := st.back(2):
                        pe.wait_ge(*sc["scanned"].of(old))
                    turn(pe, st.s2, xw[:, st.s2]).then_inc(sc["src_turned"].sem, 1)
                if st := at(1):
                    pe.wait_ge(*sc["scanned"].of(st))
                    pe.wait_ge(*sc["own_cols"].of(st))
                    if old := st.back(2):
                        pe.wait_ge(*sc["y1"].of(old))
                    times(pe, 4 + st.s2, (seg[0:D, st.s2], w["L0_gnn_W2"][:, :]),
                          (h_c[:, st.s2], w["L0_gnn_W2_loop"][:, :])).then_inc(sc["conv_done"].sem, 1)

            ticks(pe, NG, 1, phase_c)

            sd = signals("D")
            xs, xo, ea = deep_rows
            xs_c, ea_c, sc_c, ex_c, wv_c, z_c, y_c, zg_c = col_tiles
            xf_c = deep_cols
            pe.wait_ge(s_phase, 4)

            def phase_d(at):
                if st := at(4):
                    pe.wait_ge(*sd["attn"].of(st))
                    if old := st.back(1):
                        pe.wait_ge(*sd["divided"].of(old))
                    for t in range(T):
                        pe.matmul(head_rows(7)[:, t, :], lanes(z_c[0:D, st.s2])[:, :, t],
                                  ident[0:D, 0:D].rearrange("p (h c) -> p h c", c=HD)[:, :, 0],
                                  start=True, stop=True)
                    turn_back(pe, 7, y_c[0:D, st.s2]).then_inc(sd["y_turned"].sem, 1)
                if st := at(0):
                    pe.wait_ge(*sd["x_in"].of(st))
                    if old := st.back(1):
                        pe.wait_ge(*sd["filled"].of(old))
                    turn(pe, 1, xo[:, st.s]).then_inc(sd["own_turned"].sem, 1)
                    pe.wait_ge(*sd["edge_in"].of(st))
                    if old := st.back(1):
                        pe.wait_ge(*sd["edge_cols"].of(old))
                    turn(pe, 2, ea[:, st.s]).then_inc(sd["edge_turned"].sem, 1)
                if st := at(2):
                    pe.wait_ge(*sd["score"].of(st))
                    times_cols(pe, 3, sc_c[0:D, st.s2], head_sum[:, :]).then_inc(sd["sum_done"].sem, 1)
                if st := at(1):
                    pe.wait_ge(*sd["filled"].of(st))
                    if old := st.back(1):
                        pe.wait_ge(*sd["score"].of(old))
                    times_cols(pe, 5, xf_c[:, st.s], w["L1_gnn_Wq"][:, :]).then_inc(sd["q_done"].sem, 1)
                    pe.wait_ge(*sd["edge_cols"].of(st))
                    times_cols(pe, 6, ea_c[:, st.s2], w["L1_gnn_We"][:, :]).then_inc(sd["e_done"].sem, 1)
                if st := at(0):
                    pe.wait_ge(*sd["src_in"].of(st))
                    if old := st.back(1):
                        pe.wait_ge(*sd["src_cols"].of(old))
                    turn(pe, 0, xs[:, st.s]).then_inc(sd["src_turned"].sem, 1)
                if st := at(1):
                    pe.wait_ge(*sd["src_cols"].of(st))
                    if old := st.back(1):
                        pe.wait_ge(*sd["exped"].of(old))
                    times_cols(pe, 3, xs_c[:, st.s2], w["L1_gnn_Wk"][:, :]).then_inc(sd["k_done"].sem, 1)
                    if old := st.back(1):
                        pe.wait_ge(*sd["msg"].of(old))
                    times_cols(pe, 4, xs_c[:, st.s2], w["L1_gnn_Wv"][:, :]).then_inc(sd["v_done"].sem, 1)

            ticks(pe, NG, 4, phase_d)

            se = signals("E")
            xs, xo = deep_rows[:2]
            seg, rst, g_c = col_tiles[:3]
            pe.wait_ge(s_phase, 5)

            def phase_e(at):
                if st := at(0):
                    pe.wait_ge(*se["x_in"].of(st))
                    if old := st.back(2):
                        pe.wait_ge(*se["rst"].of(old))
                    turn(pe, 2 + st.s2, xo[:, st.s]).then_inc(se["own_turned"].sem, 1)
                    pe.wait_ge(*se["src_in"].of(st))
                    turn(pe, st.s2, xs[:, st.s]).then_inc(se["src_turned"].sem, 1)
                if st := at(2):
                    pe.wait_ge(*se["mlp_hidden"].of(st))
                    if old := st.back(2):
                        pe.wait_ge(*se["y2"].of(old))
                    times(pe, 6 + st.s2, (g_c[:, st.s2], w["L2_gnn_W2"][:, :])).then_inc(se["mlp2_done"].sem, 1)
                if st := at(1):
                    pe.wait_ge(*se["rst"].of(st))
                    if old := st.back(2):
                        pe.wait_ge(*se["mlp_hidden"].of(old))
                    times_cols(pe, 4 + st.s2, rst[:, st.s2], w["L2_gnn_W1"][:, :]).then_inc(se["mlp1_done"].sem, 1)

            ticks(pe, NG, 2, phase_e)

            for phase, reader in (("F", "conv_out"), ("G", "y2")):
                s = signals(phase)
                xs, seg = deep_rows[0], col_tiles[0]
                pe.wait_ge(s_phase, PHASES.index(phase) + 1)

                def phase_fg(at):
                    if st := at(0):
                        pe.wait_ge(*s["src_in"].of(st))
                        if old := st.back(2):
                            pe.wait_ge(*s["scanned"].of(old))
                        turn(pe, st.s2, xs[:, st.s]).then_inc(s["src_turned"].sem, 1)
                    if st := at(1):
                        pe.wait_ge(*s["scanned"].of(st))
                        if old := st.back(2):
                            pe.wait_ge(*s[reader].of(old))
                        turn_back(pe, 2 + st.s2, seg[0:D, st.s2]).then_inc(s["y_turned"].sem, 1)

                ticks(pe, NG, 1, phase_fg)

        @block.scalar
        def _(act):
            act.preload_act_table_set("natural_log_exp_and_others")

            def store(st, sig, made, tile, table, g):
                act.wait_ge(*made.of(st))
                act.dma_start(groups(table)[g], tile).then_inc(sig.sems[st.s], 16)

            sg = signals("A")
            xs, xd, x = deep_rows
            xw, conv, h, y1, x1, x2, y2, x3, tmp = row_tiles
            seg, xd_c, x_c, h_c, x2_c, g_c = col_tiles[:6]
            act.wait_ge(s_phase, 1)
            act.wait_ge(s_pads, 5)

            def phase_a(at):
                if st := at(0):
                    act.wait_ge(*sg["x_turned"].of(st))
                    if old := st.back(2):
                        act.wait_ge(*sg["loop1_done"].of(old))
                    act.activation(x_c[0:D, st.s2], psum[3][0:D, :], ACT.Copy).then_inc(sg["x_cols"].sem, 1)
                if st := at(1):
                    store(st, sg["own_out"], sg["own_in"], flat(xd[:, st.s]), x_own, st.g)
                    store(st, sg["h_stored"], sg["h_rows"], flat(h[:, st.s2]), h_t, NG + st.g)
                    store(st, sg["conv_stored"], sg["conv_out"], flat(conv[:, st.s2]), h_t, st.g)
                    act.wait_ge(*sg["h_turned"].of(st))
                    if old := st.back(2):
                        act.wait_ge(*sg["loop2_done"].of(old))
                    act.activation(h_c[0:D, st.s2], psum[4][0:D, :], ACT.Copy).then_inc(sg["h_cols"].sem, 1)
                if st := at(3):
                    store(st, sg["x1_stored"], sg["ln1_dve"], flat(x1[:, st.s2]), x1_t, NG + st.g)
                if st := at(4):
                    store(st, sg["x2_stored"], sg["ln2_act"], flat(x2[:, st.s2]), x2_t, NG + st.g)
                    act.wait_ge(*sg["x2_turned"].of(st))
                    if old := st.back(2):
                        act.wait_ge(*sg["mlp1_done"].of(old))
                    act.activation(x2_c[0:D, st.s2], psum[7][0:D, :], ACT.Copy).then_inc(sg["x2_cols"].sem, 1)
                if st := at(6):
                    store(st, sg["x3_stored"], sg["ln3_act"], flat(x3[:, st.s2]), x3_t, NG + st.g)
                if st := at(5):
                    ln_root(act, sg, 3, st)
                if st := at(0):
                    act.wait_ge(*sg["own_turned"].of(st))
                    if old := st.back(2):
                        act.wait_ge(*sg["conv_done"].of(old))
                    act.activation(xd_c[0:D, st.s2], psum[1][0:D, :], ACT.Copy).then_inc(sg["own_cols"].sem, 1)
                if st := at(2):
                    ln_root(act, sg, 1, st)
                if st := at(0):
                    act.wait_ge(*sg["loop1_done"].of(st))
                    if old := st.back(2):
                        act.wait_ge(*sg["h_turned"].of(old))
                        act.wait_ge(*sg["h_stored"].of(old))
                    act.activation(h[:, st.s2], rows_of(5), ACT.Relu).then_inc(sg["h_rows"].sem, 1)
                if st := at(5):
                    if old := st.back(2):
                        act.wait_ge(*sg["x3_stored"].of(old))
                    ln_apply_act(act, sg, 3, st, y2[:, st.s2], x3[:, st.s2])
                if st := at(3):
                    ln_root(act, sg, 2, st)
                if st := at(4):
                    act.wait_ge(*sg["mlp1_done"].of(st))
                    if old := st.back(2):
                        act.wait_ge(*sg["mlp2_done"].of(old))
                    act.activation(g_c[0:D, st.s2], psum[4][0:D, :], ACT.Relu).then_inc(sg["mlp_hidden"].sem, 1)
                if st := at(0):
                    act.wait_ge(*sg["conv_done"].of(st))
                    if old := st.back(2):
                        act.wait_ge(*sg["conv_stored"].of(old))
                    act.activation(conv[:, st.s2], rows_of(2), ACT.Relu).then_inc(sg["conv_out"].sem, 1)
                if st := at(3):
                    if old := st.back(2):
                        act.wait_ge(*sg["y2"].of(old))
                        act.wait_ge(*sg["x2_turned"].of(old))
                        act.wait_ge(*sg["x2_stored"].of(old))
                    ln_apply_act(act, sg, 2, st, x1[:, st.s2], x2[:, st.s2])

            ticks(act, NG, 6, phase_a)

            sb_ = signals("B")
            x3 = deep_rows[0]
            res = row_tiles[0]
            act.wait_ge(s_phase, 2)

            def phase_b(at):
                if st := at(1):
                    act.wait_ge(*sb_["ln1_act"].of(st))
                    if isinstance(st.g, int) and st.g == NG - 1:
                        act.dma_start(out[(NG - 1) * GR:N, :].rearrange("(p t) d -> p (t d)", t=T),
                                      flat(res[0:NLAST // T, st.s2])).then_inc(sb_["x1_stored"].sems[st.s], 16)
                    else:
                        act.dma_start(groups(nodes_out)[st.g], flat(res[:, st.s2]))\
                            .then_inc(sb_["x1_stored"].sems[st.s], 16)
                    act.wait_ge(*sb_["ids_made"].of(st))
                    act.dma_start(source.rearrange("(g p t) f -> g p t f", p=P, t=T)[st.g], srcs[:, st.s, :, :])\
                        .then_inc(sb_["ids_stored"].sems[st.s], 16)
                if st := at(0):
                    ln_root(act, sb_, 1, st)
                    if old := st.back(2):
                        act.wait_ge(*sb_["x1_stored"].of(old))
                    ln_apply_act(act, sb_, 1, st, x3[:, st.s], res[:, st.s2])

            ticks(act, NG, 1, phase_b)

            sc = signals("C")
            xw, y1, x1 = row_tiles[:3]
            seg, h_c = col_tiles[:2]
            act.wait_ge(s_phase, 3)

            def phase_c(at):
                if st := at(3):
                    store(st, sc["x1_stored"], sc["ln1_act"], flat(x1[:, st.s2]), x1_t, st.g)
                if st := at(0):
                    act.wait_ge(*sc["own_turned"].of(st))
                    if old := st.back(2):
                        act.wait_ge(*sc["conv_done"].of(old))
                    act.activation(h_c[0:D, st.s2], psum[2 + st.s2][0:D, :], ACT.Copy)\
                        .then_inc(sc["own_cols"].sem, 1)
                if st := at(2):
                    ln_root(act, sc, 1, st)
                    if old := st.back(2):
                        act.wait_ge(*sc["x1_stored"].of(old))
                    ln_apply_act(act, sc, 1, st, y1[:, st.s2], x1[:, st.s2])

            ticks(act, NG, 3, phase_c)

            sd = signals("D")
            x2, y_r = row_tiles[:2]
            xs_c, ea_c, sc_c, ex_c, wv_c, z_c, y_c, zg_c = col_tiles
            act.wait_ge(s_phase, 4)

            def phase_d(at):
                if st := at(5):
                    store(st, sd["x1_stored"], sd["ln1_act"], flat(x2[:, st.s2]), x2_t, NG - 1 - st.g)
                if st := at(0):
                    act.wait_ge(*sd["edge_turned"].of(st))
                    if old := st.back(2):
                        act.wait_ge(*sd["e_done"].of(old))
                    act.activation(ea_c[0:D, st.s2], psum[2][0:D, :], ACT.Copy).then_inc(sd["edge_cols"].sem, 1)
                if st := at(2):
                    act.wait_ge(*sd["sum_done"].of(st))
                    if old := st.back(2):
                        act.wait_ge(*sd["z_scanned"].of(old))
                    act.activation(ex_c[0:D, st.s2], psum[3][0:D, :], ACT.Exp).then_inc(sd["exped"].sem, 1)
                if st := at(4):
                    ln_root(act, sd, 1, st)
                if st := at(0):
                    act.wait_ge(*sd["src_turned"].of(st))
                    if old := st.back(2):
                        act.wait_ge(*sd["v_done"].of(old))
                    act.activation(xs_c[0:D, st.s2], psum[0][0:D, :], ACT.Copy).then_inc(sd["src_cols"].sem, 1)
                if st := at(4):
                    if old := st.back(2):
                        act.wait_ge(*sd["x1_stored"].of(old))
                    ln_apply_act(act, sd, 1, st, y_r[:, st.s2], x2[:, st.s2])
                if st := at(1):
                    act.wait_ge(*sd["k_done"].of(st))
                    if old := st.back(2):
                        act.wait_ge(*sd["msg"].of(old))
                        act.wait_ge(*sd["z_scanned"].of(old))
                    act.activation(ex_c[0:D, st.s2], psum[3][0:D, :], ACT.Copy).then_inc(sd["k_cols"].sem, 1)
                if st := at(2):
                    act.wait_ge(*sd["z_scanned"].of(st))
                    if old := st.back(2):
                        act.wait_ge(*sd["attn"].of(old))
                    act.activation(zg_c[0:D, st.s2], z_c[0:D, st.s2], ACT.Copy, bias=1e-6)\
                        .then_inc(sd["z_guarded"].sem, 1)

            ticks(act, NG, 5, phase_d)

            se = signals("E")
            y2, x3 = row_tiles[:2]
            seg, rst, g_c = col_tiles[:3]
            act.wait_ge(s_phase, 5)

            def phase_e(at):
                if st := at(4):
                    store(st, se["x1_stored"], se["ln1_act"], flat(x3[:, st.s2]), x3_t, NG - 1 - st.g)
                if st := at(3):
                    ln_root(act, se, 1, st)
                    if old := st.back(2):
                        act.wait_ge(*se["x1_stored"].of(old))
                    ln_apply_act(act, se, 1, st, y2[:, st.s2], x3[:, st.s2])
                if st := at(1):
                    act.wait_ge(*se["mlp1_done"].of(st))
                    if old := st.back(2):
                        act.wait_ge(*se["mlp2_done"].of(old))
                    act.activation(g_c[0:D, st.s2], psum[4 + st.s2][0:D, :], ACT.Relu)\
                        .then_inc(se["mlp_hidden"].sem, 1)

            ticks(act, NG, 4, phase_e)

            sf = signals("F")
            mean = row_tiles[0]
            act.wait_ge(s_phase, 6)

            def phase_f(at):
                if st := at(2):
                    store(st, sf["x1_stored"], sf["conv_out"], flat(mean[:, st.s2]), mean_t[0:EP, :],
                          NG - 1 - st.g)
                if st := at(1):
                    act.wait_ge(*sf["y_turned"].of(st))
                    if old := st.back(2):
                        act.wait_ge(*sf["x1_stored"].of(old))
                    for t in range(T):
                        last = act.activation(mean[:, st.s2, t, :], rows_of(2 + st.s2)[:, t, :], ACT.Copy,
                                              scale=f32(meta[:, st.s, t, INV_DEG:INV_DEG + 1]))
                    last.then_inc(sf["conv_out"].sem, 1)

            ticks(act, NG, 2, phase_f)

            sh = signals("G")
            t1, y2, res = row_tiles[:3]
            act.wait_ge(s_phase, 7)

            def phase_g(at):
                if st := at(2):
                    ln_root(act, sh, 1, st)
                    if old := st.back(2):
                        act.wait_ge(*sh["ids_out"].of(old))
                    ln_apply_act(act, sh, 1, st, y2[:, st.s2], res[:, st.s2])

            ticks(act, NG, 2, phase_g)

        @block.vector
        def _(dve):
            dve.memset(ones[:, :], 1.0).then_inc(s_pads, 1)
            dve.memset(raw[0][:, :], 0).then_inc(s_pads, 1)
            dve.memset(raw[1][:, :], PAD).then_inc(s_pads, 1)
            dve.memset(raw[2][:, :], 0).then_inc(s_pads, 1)
            dve.memset(zero_row[:, :], 0.0)
            dve.memset(ends[:, 0, :], -1)
            dve.memset(ends[:, 1, :], FAR)
            for tile in (deep_cols, *col_tiles):
                last = dve.memset(tile[D:D + 1, :, :], 1.0)
            last.then_inc(s_pads, 1)

            done = [0]

            def step(ins):
                done[0] += 1
                ins.then_inc(s_prep, 1)
                dve.wait_ge(s_prep, done[0])

            dve.wait_ge(s_raw, 96)
            dve.wait_ge(s_pool_const, 2)
            for i in range(3):
                step(dve.tensor_copy(rec[:, :, i], raw[i][:, :]))
            step(dve.tensor_copy(rec[:, :, 3], slot_no[:, :]))
            cur, before, behind = halo[:, 1:C + 1, 1], halo[:, 0:C, 1], halo[:, 2:C + 2, 1]
            dve.wait_ge(s_halo, 16)
            dve.tensor_tensor(work[0][:, :], cur, before, ALU.is_lt).then_inc(s_disorder, 1)
            dve.wait_ge(s_disorder, 1)
            step(dve.tensor_reduce(small[:, 0:1], work[0][:, :], AX.X, ALU.add))
            dve.wait_ge(s_prep_pe, 1)
            step(dve.tensor_copy(small[:, 1:2], psum[0][:, 0:1]))
            step(dve.tensor_copy(unsorted[:, :], small[:, 1:2]))

            disorder = dve.value_load(unsorted[0:1, 0:1])
            with dve.If(disorder > 0):
                dve.tensor_copy(work[1][:, :], slot_no[:, :])
                dve.memset(work[0][:, :], 1.0)
                dve.tensor_copy(work[2][:, :], raw[1][:, :])
                for chunk in range(CHUNKS):
                    dve.wait_ge(s_rank_in, 16 * (chunk + 1))
                    base = (3 * C + 1) * chunk
                    dve.memset(rank_neg[:, :], -1.0)
                    dve.memset(rank_tmp[:, :], 1.0).then_inc(s_rank, 1)
                    dve.wait_ge(s_rank, base + 1)
                    dve.tensor_tensor_scan(rank_no[:, :], rank_tmp[:, :], rank_neg[:, :],
                                           initial=float(1 - chunk * CH), op0=ALU.mult, op1=ALU.add)\
                        .then_inc(s_rank_no, 1)
                    dve.wait_ge(s_rank_no, chunk + 1)

                    def rank_column(c):
                        k = base + 1 + 3 * c
                        dve.tensor_scalar(rank_tmp[:, :], rank_dst[:, :], work[2][:, bass.ds(c, 1)], float(PAD),
                                          ALU.subtract, ALU.mult).then_inc(s_rank, 1)
                        dve.wait_ge(s_rank, k + 1)
                        dve.scalar_tensor_tensor(rank_tmp[:, :], rank_tmp[:, :], work[1][:, bass.ds(c, 1)],
                                                 rank_no[:, :], ALU.subtract, ALU.is_lt).then_inc(s_rank, 1)
                        dve.wait_ge(s_rank, k + 2)
                        dve.tensor_reduce(rank_sum[:, :], rank_tmp[:, :], AX.X, ALU.add).then_inc(s_rank_sum, 1)
                        dve.wait_ge(s_rank_sum, C * chunk + c + 1)
                        dve.tensor_tensor(work[0][:, bass.ds(c, 1)], work[0][:, bass.ds(c, 1)], rank_sum[:, :],
                                          ALU.add).then_inc(s_rank, 1)
                        dve.wait_ge(s_rank, k + 3)

                    with dve.Fori(0, C) as c:
                        rank_column(c)
                dve.wait_ge(s_rank_done, 1)

            dve.wait_ge(s_sorted, 1)
            same_before, same_behind, first_slot, last_slot = (t[:, :] for t in work)
            m = meta_all
            mf = f32(m[:, :, :])
            no = slot_no[:, :]
            dve.tensor_copy(m[:, :, SRC], halo[:, 1:C + 1, 0])
            dve.tensor_copy(m[:, :, WEIGHT], halo[:, 1:C + 1, 2])
            dve.tensor_scalar(m[:, :, DST], cur, float(N - 1), None, ALU.min)
            dve.tensor_copy(m[:, :, SLOT], no)
            dve.tensor_tensor(mf[:, :, IS_END], cur, behind, ALU.not_equal)
            dve.tensor_tensor(same_before, cur, before, ALU.is_equal)
            step(dve.tensor_tensor(same_behind, cur, behind, ALU.is_equal))
            dve.tensor_copy(flag_tile[:, 0, :], same_before)
            dve.tensor_copy(flag_tile[:, 1, :], same_behind)
            dve.tensor_scalar(first_slot, same_before, -1.0, 1.0, ALU.mult, ALU.add)
            step(dve.tensor_scalar(last_slot, same_behind, -1.0, 1.0, ALU.mult, ALU.add))
            dve.scalar_tensor_tensor(m[:, :, START_DST], cur, float(-FAR), first_slot, ALU.add, ALU.mult)
            step(dve.scalar_tensor_tensor(m[:, :, END_DST], cur, float(-FAR), last_slot, ALU.add, ALU.mult))
            dve.tensor_scalar(m[:, :, START_DST], m[:, :, START_DST], float(FAR), None, ALU.add)
            step(dve.tensor_scalar(m[:, :, END_DST], m[:, :, END_DST], float(FAR), None, ALU.add))
            dve.tensor_tensor(same_before, first_slot, no, ALU.mult)
            step(dve.scalar_tensor_tensor(same_behind, no, float(-FAR), last_slot, ALU.add, ALU.mult))
            step(dve.tensor_scalar(same_behind, same_behind, float(FAR), None, ALU.add))
            dve.tensor_tensor_scan(first_slot, same_before, same_before, initial=0.0, op0=ALU.max, op1=ALU.max)
            step(dve.tensor_tensor_scan(backwards(last_slot), backwards(same_behind), backwards(same_behind),
                                        initial=float(FAR), op0=ALU.min, op1=ALU.min))
            step(dve.tensor_copy(small[:, 2:3], first_slot[:, C - 1:C]))
            step(dve.tensor_copy(small[:, 3:4], last_slot[:, 0:1]))
            dve.wait_ge(s_prep_pe, 3)
            dve.tensor_copy(row1[0:1, 0, :], psum[1][0:1, 0:P])
            dve.memset(row1[0:1, 2, 0:1], 0.0)
            dve.memset(row1[0:1, 3, P - 1:P], float(FAR))
            step(dve.tensor_copy(row1[0:1, 1, :], psum[2][0:1, 0:P]))
            step(dve.tensor_tensor_scan(row1[0:1, 2, 1:P], row1[0:1, 0, 0:P - 1], row1[0:1, 0, 0:P - 1],
                                        initial=0.0, op0=ALU.max, op1=ALU.max))
            step(dve.tensor_tensor_scan(backwards(row1[0:1, 3, 0:P - 1]), backwards(row1[0:1, 1, 1:P]),
                                        backwards(row1[0:1, 1, 1:P]), initial=float(FAR), op0=ALU.min,
                                        op1=ALU.min))
            step(dve.memset(small[:, 6:7], 0.0))
            dve.wait_ge(s_prep_pe, 5)
            dve.tensor_copy(small[:, 4:5], psum[3][:, 0:1])
            step(dve.tensor_copy(small[:, 5:6], psum[4][:, 0:1]))
            dve.tensor_scalar(first_slot, first_slot, small[:, 4:5], None, ALU.max)
            step(dve.tensor_scalar(last_slot, last_slot, small[:, 5:6], None, ALU.min))
            dve.tensor_copy(m[:, :, FIRST], first_slot)
            step(dve.scalar_tensor_tensor(same_before, last_slot, 1.0, no, ALU.add, ALU.subtract))
            step(dve.reciprocal(mf[:, :, INV_DEG], same_before))
            step(dve.tensor_scalar(mf[:, :, HALF_INV], mf[:, :, INV_DEG], 0.5, None, ALU.mult))
            assert done[0] == PREP_ALL

            def weigh(s, st, rows, result):
                dve.wait_ge(*s["src_in"].of(st))
                if old := st.back(2):
                    dve.wait_ge(*s["src_turned"].of(old))
                weight = f32(meta[:, st.s, :, WEIGHT:WEIGHT + 1]).to_broadcast([P, T, D])
                dve.tensor_tensor(result[:, st.s2], rows[:, st.s], weight, ALU.mult).then_inc(s["weighted"].sem, 1)

            def scan(s, st, name, result, slot, data, backward, used=None):
                order = backwards if backward else (lambda ap: ap)
                carry = 0 if backward else GR - 1
                initial = 0.0
                if old := st.back(1):
                    dve.wait_ge(*s[name].of(old))
                    initial = result[0:D, slot(old), carry:carry + 1]
                if used:
                    dve.wait_ge(*used)
                dve.tensor_tensor_scan(order(result[0:D, slot(st), :]), order(flag[:, st.s, :]), order(data),
                                       initial=initial, op0=ALU.mult, op1=ALU.add).then_inc(s[name].sem, 1)

            def s2(st):
                return st.s2

            def mix(s, st, bank, own, tmp, y):
                q = s["y1"]
                dve.scalar_tensor_tensor(tmp[:, st.s2], rows_of(bank), 0.0, own[:, st.s], ALU.max, ALU.add)\
                    .then_inc(q.sem, 1)
                dve.wait_ge(*q.of(st, 1))
                dve.scalar_tensor_tensor(y[:, st.s2], tmp[:, st.s2], 0.5, own[:, st.s], ALU.mult, ALU.add)\
                    .then_inc(q.sem, 1)
                dve.wait_ge(*q.of(st))

            sg = signals("A")
            xs, xd, x = deep_rows
            xw, conv, h, y1, x1, x2, y2, x3, tmp = row_tiles
            seg = col_tiles[0]
            dve.wait_ge(s_phase, 1)

            def phase_a(at):
                if st := at(5):
                    dve.wait_ge(*sg["mlp2_done"].of(st))
                    if old := st.back(2):
                        dve.wait_ge(*sg["ln3_act"].of(old))
                    dve.tensor_tensor(y2[:, st.s2], rows_of(5), x2[:, st.s2], ALU.add).then_inc(sg["y2"].sem, 1)
                    dve.wait_ge(*sg["y2"].of(st))
                    ln_stats(dve, sg, 3, st, y2[:, st.s2])
                if st := at(0):
                    dve.wait_ge(*sg["meta_in"].of(st))
                    weigh(sg, st, xs, xw)
                if st := at(2):
                    dve.wait_ge(*sg["loop2_done"].of(st))
                    mix(sg, st, 6, x, tmp, y1)
                    ln_stats(dve, sg, 1, st, y1[:, st.s2])
                if st := at(0):
                    dve.wait_ge(*sg["src_turned"].of(st))
                    old = st.back(2)
                    scan(sg, st, "scanned", seg, s2, psum[0][0:D, :], False, old and sg["conv_done"].of(old))
                if st := at(5):
                    ln_scale(dve, sg, 3, st)
                if st := at(3):
                    dve.wait_ge(*sg["ln1_dve"].of(st))
                    ln_stats(dve, sg, 2, st, x1[:, st.s2])
                if st := at(2):
                    ln_scale(dve, sg, 1, st)
                    if old := st.back(2):
                        dve.wait_ge(*sg["x1_stored"].of(old))
                        dve.wait_ge(*sg["ln2_act"].of(old))
                    ln_apply_dve(dve, sg, 1, st, y1[:, st.s2], x1[:, st.s2])
                if st := at(3):
                    ln_scale(dve, sg, 2, st)

            ticks(dve, NG, 5, phase_a)

            sb_ = signals("B")
            x3 = deep_rows[0]
            dve.wait_ge(s_phase, 2)

            def phase_b(at):
                st = at(0)
                q = sb_["ids_made"]
                dve.wait_ge(*sb_["x_in"].of(st))
                ln_stats(dve, sb_, 1, st, x3[:, st.s])
                dve.wait_ge(*sb_["src_in"].of(st))
                if old := st.back(DEPTH):
                    dve.wait_ge(*sb_["ids_stored"].of(old))
                dve.tensor_copy(srcs[:, st.s, :, 0:2], ids[:, st.s2, :, :]).then_inc(q.sem, 1)
                dve.tensor_scalar(srcs[:, st.s, :, 2:4], ids[:, st.s2, :, 1:2].to_broadcast([P, T, 2]),
                                  float(EP), None, ALU.min).then_inc(q.sem, 1)
                ln_scale(dve, sb_, 1, st)

            ticks(dve, NG, 0, phase_b)

            sc = signals("C")
            hs, hown, x = deep_rows
            xw, y1, x1, tmp = row_tiles[:4]
            dve.wait_ge(s_phase, 3)

            def phase_c(at):
                if st := at(2):
                    dve.wait_ge(*sc["conv_done"].of(st))
                    if old := st.back(2):
                        dve.wait_ge(*sc["ln1_act"].of(old))
                    mix(sc, st, 4 + st.s2, x, tmp, y1)
                    ln_stats(dve, sc, 1, st, y1[:, st.s2])
                if st := at(0):
                    dve.wait_ge(*sc["meta_in"].of(st))
                    weigh(sc, st, hs, xw)
                if st := at(1):
                    dve.wait_ge(*sc["src_turned"].of(st))
                    old = st.back(2)
                    scan(sc, st, "scanned", seg, s2, psum[st.s2][0:D, :], False, old and sc["conv_done"].of(old))
                if st := at(2):
                    ln_scale(dve, sc, 1, st, f32(word(st, IS_END)))

            ticks(dve, NG, 2, phase_c)

            sd = signals("D")
            xs_c, ea_c, sc_c, ex_c, wv_c, z_c, y_c, zg_c = col_tiles
            xf_c = deep_cols
            y_r = row_tiles[1]
            dve.wait_ge(s_phase, 4)

            def phase_d(at):
                if st := at(2):
                    q = sd["score"]
                    dve.wait_ge(*sd["q_done"].of(st))
                    dve.wait_ge(*sd["k_cols"].of(st))
                    if old := st.back(2):
                        dve.wait_ge(*sd["msg"].of(old))
                    dve.tensor_tensor(sc_c[0:D, st.s2], ex_c[0:D, st.s2], psum[5][0:D, :], ALU.mult)\
                        .then_inc(q.sem, 1)
                    dve.wait_ge(*q.of(st, 1))
                    dve.wait_ge(*sd["e_done"].of(st))
                    dve.tensor_tensor(sc_c[0:D, st.s2], sc_c[0:D, st.s2], psum[6][0:D, :], ALU.mult)\
                        .then_inc(q.sem, 1)
                if st := at(0):
                    dve.wait_ge(*sd["meta_in"].of(st))
                    dve.wait_ge(*sd["own_turned"].of(st))
                    old = st.back(DEPTH)
                    if old:
                        dve.wait_ge(*sd["q_done"].of(old))
                    scan(sd, st, "filled", xf_c, lambda q: q.s, psum[1][0:D, :], True, old and sd["attn"].of(old))
                if st := at(4):
                    q = sd["divided"]
                    dve.wait_ge(*sd["y_turned"].of(st))
                    dve.tensor_scalar(z_r[:, st.s2, 0], head_rows(7), 1e-6, None, ALU.add).then_inc(q.sem, 1)
                    dve.wait_ge(*q.of(st, 1))
                    dve.reciprocal(z_r[:, st.s2, 1], z_r[:, st.s2, 0]).then_inc(q.sem, 1)
                    dve.wait_ge(*q.of(st, 2))
                    if old := st.back(2):
                        dve.wait_ge(*sd["ln1_act"].of(old))
                    dve.tensor_tensor(y_r[:, st.s2].rearrange("p t (h c) -> p (t h) c", c=HD),
                                      psum[7][:, 0:T * D].rearrange("p (n c) -> p n c", c=HD),
                                      z_r[:, st.s2, 1].rearrange("p t h -> p (t h)").unsqueeze(2)
                                      .to_broadcast([P, T * HEADS, HD]), ALU.mult).then_inc(q.sem, 1)
                    dve.wait_ge(*q.of(st))
                    ln_stats(dve, sd, 1, st, y_r[:, st.s2])
                if st := at(2):
                    dve.wait_ge(*sd["exped"].of(st))
                    dve.tensor_scalar(ex_c[0:D, st.s2], ex_c[0:D, st.s2], math.exp(-5.0), math.exp(5.0), ALU.max,
                                      ALU.min).then_inc(sd["clipped"].sem, 1)
                    dve.wait_ge(*sd["clipped"].of(st))
                    old = st.back(2)
                    scan(sd, st, "z_scanned", z_c, s2, ex_c[0:D, st.s2], True, old and sd["y_turned"].of(old))
                    dve.wait_ge(*sd["v_done"].of(st))
                    dve.wait_ge(*sd["sum_done"].of(st))
                    dve.tensor_tensor(sc_c[0:D, st.s2], psum[4][0:D, :], ex_c[0:D, st.s2], ALU.mult)\
                        .then_inc(sd["msg"].sem, 1)
                    dve.wait_ge(*sd["msg"].of(st))
                    scan(sd, st, "scanned", wv_c, s2, sc_c[0:D, st.s2], True, old and sd["attn"].of(old))
                if st := at(4):
                    ln_scale(dve, sd, 1, st)

            ticks(dve, NG, 4, phase_d)

            se = signals("E")
            xs, xo = deep_rows[:2]
            y2, x3 = row_tiles[:2]
            seg, rst, g_c = col_tiles[:3]
            dve.wait_ge(s_phase, 5)

            def phase_e(at):
                if st := at(3):
                    dve.wait_ge(*se["mlp2_done"].of(st))
                    if old := st.back(2):
                        dve.wait_ge(*se["ln1_act"].of(old))
                    dve.tensor_tensor(y2[:, st.s2], rows_of(6 + st.s2), xo[:, st.s], ALU.add)\
                        .then_inc(se["y2"].sem, 1)
                    dve.wait_ge(*se["y2"].of(st))
                    ln_stats(dve, se, 1, st, y2[:, st.s2])
                if st := at(1):
                    dve.wait_ge(*se["meta_in"].of(st))
                    dve.wait_ge(*se["src_turned"].of(st))
                    old = st.back(2)
                    scan(se, st, "scanned", seg, s2, psum[st.s2][0:D, :], True, old and se["rst"].of(old))
                    dve.wait_ge(*se["scanned"].of(st))
                    if old:
                        dve.wait_ge(*se["mlp1_done"].of(old))
                    dve.tensor_tensor(rst[0:D, st.s2], psum[2 + st.s2][0:D, :], seg[0:D, st.s2], ALU.add)\
                        .then_inc(se["rst"].sem, 1)
                if st := at(3):
                    ln_scale(dve, se, 1, st)

            ticks(dve, NG, 3, phase_e)

            sf = signals("F")
            dve.wait_ge(s_phase, 6)

            def phase_f(at):
                st = at(0)
                dve.wait_ge(*sf["meta_in"].of(st))
                dve.wait_ge(*sf["src_turned"].of(st))
                old = st.back(2)
                scan(sf, st, "scanned", seg, s2, psum[st.s2][0:D, :], True, old and sf["y_turned"].of(old))

            ticks(dve, NG, 0, phase_f)

            sh = signals("G")
            xs, xo, mo = deep_rows
            t1, y2, res = row_tiles[:3]
            dve.wait_ge(s_phase, 7)

            def phase_g(at):
                if st := at(2):
                    dve.wait_ge(*sh["y_turned"].of(st))
                    dve.wait_ge(*sh["index_in"].of(st))
                    if old := st.back(2):
                        dve.wait_ge(*sh["ln1_act"].of(old))
                    dve.wait_ge(*sh["x_in"].of(st))
                    dve.scalar_tensor_tensor(t1[:, st.s2], mo[:, st.s], 0.5, xo[:, st.s], ALU.mult, ALU.add)\
                        .then_inc(sh["y1"].sem, 1)
                    dve.wait_ge(*sh["y1"].of(st))
                    for t in range(T):
                        last = dve.scalar_tensor_tensor(y2[:, st.s2, t, :], rows_of(2 + st.s2)[:, t, :],
                                                        f32(meta[:, st.s, t, HALF_INV:HALF_INV + 1]),
                                                        t1[:, st.s2, t, :], ALU.mult, ALU.add)
                    last.then_inc(sh["y2"].sem, 1)
                    dve.wait_ge(*sh["y2"].of(st))
                    ln_stats(dve, sh, 1, st, y2[:, st.s2])
                if st := at(0):
                    dve.wait_ge(*sh["meta_in"].of(st))
                    dve.wait_ge(*sh["src_turned"].of(st))
                    old = st.back(2)
                    scan(sh, st, "scanned", seg, s2, psum[st.s2][0:D, :], True, old and sh["y_turned"].of(old))
                if st := at(2):
                    ln_scale(dve, sh, 1, st)

            ticks(dve, NG, 2, phase_g)


PREP_ALL = 25

_INS = ["x", "src", "dst", "edge_attr_96", "edge_weight", "L0_gnn_W1", "L0_gnn_W1_loop", "L0_gnn_b1", "L0_gnn_W2",
        "L0_gnn_W2_loop", "L0_gnn_b2", "L1_gnn_Wq", "L1_gnn_bq", "L1_gnn_Wk", "L1_gnn_bk", "L1_gnn_We",
        "L1_gnn_be", "L1_gnn_Wv", "L1_gnn_bv", "L2_gnn_W1", "L2_gnn_b1", "L2_gnn_W2", "L2_gnn_b2"]


def kernel(**inputs):
    import numpy as _np
    import concourse.bacc as _bacc
    from concourse import mybir as _mybir
    from concourse.bass_utils import run_bass_kernel_spmd as _run

    nc = _bacc.Bacc("TRN2", target_bir_lowering=False, num_devices=1)
    arrays, args = {}, {}
    for name in _INS:
        v = _np.ascontiguousarray(inputs[name])
        arrays[f"in_{name}_dram"] = v
        args[name] = nc.dram_tensor(f"in_{name}_dram", v.shape, _mybir.dt.from_np(v.dtype), kind="ExternalInput").ap()
    out = nc.dram_tensor("out_0_dram", inputs["x"].shape, _mybir.dt.float32, kind="ExternalOutput").ap()
    gnn_kernel(nc, args, out)
    r = _run(nc, [arrays], core_ids=[0])
    return r.results[0]["out_0_dram"]
```

```python
import math
from contextlib import ExitStack

import concourse.bass as bass
from concourse import mybir

F32 = mybir.dt.float32
I32 = mybir.dt.int32
BF16 = mybir.dt.bfloat16
ALU = mybir.AluOpType
ACT = mybir.ActivationFunctionType
AX = mybir.AxisListType

P = 128
T = 4
GR = P * T
EPS = 1e-5
FAR = 1 << 20
PAD = 1 << 16

SRC, DST, WEIGHT, END_DST, START_DST, SLOT, FIRST, INV_DEG, IS_END, HALF_INV = range(10)
NF = 10

DEPTH = 4

ENGINE_SIGNALS = {
    "A": dict(x_turned=1, x_cols=1, loop1_done=1, own_part=1, h_rows=1, h_turned=1, h_cols=1, loop2_done=1,
              half=1, y1=1, ln1_dve=6, ln1_act=2, ln2_dve=6, ln2_act=3),
    "B": dict(weighted=1, ids_made=2, scanned=1, src_turned=1, conv_done=1, summed=1, conv_out=1, h_turned=1,
              h_cols=1, loop2_done=1, own_part=1, x2_turned=1, x2_cols=1, mlp1_done=1, mlp_hidden=1,
              mlp2_done=1, y2=1, ln2_dve=6, ln2_act=3, ln1_dve=6, ln1_act=3),
    "C": dict(weighted=1, end_kept=1, scanned=1, src_turned=1, edge_turned=1, edge_cols=1, e_done=1, e_cols=1,
              conv_done=1, summed=1, half=1, y1=1, ln1_dve=7, ln1_act=3),
    "D": dict(src_turned=1, own_turned=1, src_cols=1, filled=1, k_done=1, q_done=1, v_done=1, score=2,
              sum_done=1, exped=1, clipped=1, msg=1, scanned=1, z_scanned=1, z_guarded=1, attn=2, y_turned=1,
              divided=3, ln1_dve=6, ln1_act=3),
    "E": dict(src_turned=1, own_turned=1, scanned=1, rst=1, mlp1_done=1, mlp_hidden=1, mlp2_done=1,
              y2=1, ln1_dve=6, ln1_act=3),
    "F": dict(src_turned=1, scanned=1, y_turned=1, conv_out=1),
    "G": dict(src_turned=1, scanned=1, y_turned=1, y1=1, y2=1, ln1_dve=6, ln1_act=3),
}
DMA_SIGNALS = {
    "A": dict(meta_in=1, x_in=1, ids_out=4, node_stored=1, h_stored=1, x1_stored=1, x2_stored=1),
    "B": dict(meta_in=1, flags_in=1, x_in=1, src_in=4, own_in=4, own_out=1, conv_stored=1, own_part_stored=1,
              x2_stored=1, ids_stored=1, x1_stored=1),
    "C": dict(source_in=1, meta_in=1, flags_in=1, x_in=2, edge_in=1, src_in=4, e_stored=1, x1_stored=1),
    "D": dict(source_in=1, meta_in=1, x_in=1, edge_in=1, src_in=4, x1_stored=1),
    "E": dict(source_in=1, meta_in=1, x_in=1, src_in=4, x1_stored=1),
    "F": dict(source_in=1, meta_in=2, src_in=4, x1_stored=1),
    "G": dict(source_in=1, meta_in=1, index_in=1, x_in=2, src_in=4, ids_out=4),
}
PHASES = "ABCDEFG"


class Step:

    def __init__(self, g, s, h, groups):
        self.g, self.s, self.h, self.groups = g, s, h, groups
        self.s2 = s % 2

    def back(self, n):
        if isinstance(self.g, int) and self.g < n:
            return None
        s = (self.s - n) % DEPTH
        return Step(self.g - n, s, self.h + (self.s - n - s) // DEPTH, self.groups)

    def ahead(self, n):
        if isinstance(self.g, int):
            n = min(n, self.groups - 1 - self.g)
        s = (self.s + n) % DEPTH
        return Step(self.g + n, s, self.h + (self.s + n - s) // DEPTH, self.groups)


class Signal:

    def __init__(self, sem, base, per):
        self.sem, self.base, self.per = sem, base, per

    def of(self, st, part=None):
        return self.sem, self.base + self.per * st.g + (self.per if part is None else part)


class DmaSignal:

    def __init__(self, sems, bases, per):
        self.sems, self.bases, self.per = sems, bases, per

    def of(self, st):
        return self.sems[st.s], self.bases[st.s] + 16 * self.per * (st.h + 1)


def ticks(eng, groups, delay, body):
    warm = -(-(delay + DEPTH) // DEPTH)

    def tick(n, u, j):
        def at(k):
            s = (u - k) % DEPTH
            g = n - k
            if isinstance(g, int) and not 0 <= g < groups:
                return None
            return Step(g, s, j + (u - k - s) // DEPTH, groups)

        body(at)

    for n in range(DEPTH * warm):
        tick(n, n % DEPTH, n // DEPTH)
    rounds = (groups - 1) // DEPTH
    assert rounds > warm
    with eng.Fori(warm, rounds) as j:
        for u in range(DEPTH):
            tick(DEPTH * j + u, u, j)
    for n in range(DEPTH * rounds, groups + delay):
        tick(n, n % DEPTH, n // DEPTH)


def gnn_kernel(nc, a, out):
    N, D = a["x"].shape
    E = a["src"].shape[0]
    NG = -(-E // GR)
    NG += NG % 2
    EP = NG * GR
    C = EP // P
    NLAST = N - (NG - 1) * GR
    ROW = 2 * (2 + D)
    X_PART, OWN_PART = slice(2, 2 + D), slice(2 + D, 2 + 2 * D)
    HEADS = 8
    HD = D // HEADS
    CHUNKS = 32
    CH = EP // CHUNKS
    assert N == E and 0 < NLAST <= GR and NLAST % T == 0 and D < P

    def dram(name, shape, dt=F32):
        return nc.dram_tensor(name, shape, dt, kind="Internal").ap()

    edges = dram("edges", (EP + 2, 4), I32)
    dst_list = dram("dst_list", (EP,), I32)
    edges2 = dram("edges2", (EP + 1, D))
    edge_rows = dram("edge_rows", (EP, D))
    meta_t = dram("meta_t", (EP, NF), I32)
    flags_f = dram("flags_f", (EP,), BF16)
    flags_b = dram("flags_b", (EP,), BF16)
    node_t = dram("node_t", (EP, ROW))
    node_sources = node_t.rearrange("n (h w) -> (n h) w", h=2)
    node_places = node_t.rearrange("n (h w) -> (n h) w", w=2)
    source = dram("source", (EP, 4), I32)
    x_own = dram("x_own", (EP, D))
    own_part = dram("own_part", (EP, D))
    e_t = dram("e_t", (NG, D, GR))
    h_t = dram("h_t", (2 * EP, D))
    x1_t = dram("x1_t", (2 * EP, D))
    x2_t = dram("x2_t", (2 * EP, D))
    x3_t = dram("x3_t", (2 * EP, D))
    mean_t = dram("mean_t", (EP + 1, D))

    def groups(t):
        return t.rearrange("(g p t) d -> g p (t d)", p=P, t=T)

    nodes_in = a["x"][0:(NG - 1) * GR, :]
    nodes_out = out[0:(NG - 1) * GR, :]

    with ExitStack() as ctx:
        def sb(name, shape, dt=F32):
            return ctx.enter_context(nc.sbuf_tensor(name, shape, dt))

        def sem(name):
            return ctx.enter_context(nc.semaphore(name))

        deep_rows = [sb(f"deep_rows{i}", [P, DEPTH, T, D]) for i in range(4)]
        wide_rows = sb("wide_rows", [P, DEPTH, T, ROW])
        src_rows = sb("src_rows", [P, DEPTH, T, 2 + D])
        end_mask = sb("end_mask", [P, DEPTH, T])
        row_tiles = [sb(f"rows{i}", [P, 2, T, D]) for i in range(7)]
        deep_cols = [sb(f"deep_cols{i}", [D + 1, DEPTH, GR]) for i in range(3)]
        col_tiles = [sb(f"cols{i}", [D + 1, 2, GR]) for i in range(6)]
        meta = sb("meta", [P, DEPTH, T, NF], I32)
        srcs = sb("srcs", [P, DEPTH, T, 4], I32)
        flag = sb("flag", [D, DEPTH, GR], BF16)
        ln_tiles = [(sb(f"ln_st{i}", [P, 2, T, 6]), sb(f"ln_mv{i}", [P, 2, T, 2]), sb(f"ln_s{i}", [P, 2, 7, T]))
                    for i in range(2)]
        z_r = sb("z_rows", [P, 2, 2, T, HEADS])
        eps_col = sb("eps_col", [P, 1])
        ident = sb("ident", [P, P])
        ones = sb("ones", [P, P])
        head_sum = sb("head_sum", [D, D])
        w = {n: sb(n, [D, D]) for n in ("L0_gnn_W1", "L0_gnn_W2")}
        for n in ("L0_gnn_W1_loop", "L0_gnn_W2_loop", "L1_gnn_Wq", "L1_gnn_Wk", "L1_gnn_We", "L1_gnn_Wv",
                  "L2_gnn_W1", "L2_gnn_W2"):
            w[n] = sb(n, [D + 1, D])
        bias_of = {"L0_gnn_W1_loop": "L0_gnn_b1", "L0_gnn_W2_loop": "L0_gnn_b2", "L1_gnn_Wq": "L1_gnn_bq",
                   "L1_gnn_Wk": "L1_gnn_bk", "L1_gnn_We": "L1_gnn_be", "L1_gnn_Wv": "L1_gnn_bv",
                   "L2_gnn_W1": "L2_gnn_b1", "L2_gnn_W2": "L2_gnn_b2"}
        psum = [ctx.enter_context(nc.psum_tensor(f"bank{i}", [P, GR], F32)) for i in range(8)]

        raw = [sb(f"raw{i}", [P, C], I32) for i in range(3)]
        rec = sb("rec", [P, C, 4], I32)
        halo = sb("halo", [P, C + 2, 4], I32)
        slot_no = sb("slot_no", [P, C], I32)
        node_row = sb("node_row", [P, C, 2], I32)
        work = [sb(f"work{i}", [P, C]) for i in range(4)]
        flag_tile = sb("flag_tile", [P, 2, C], BF16)
        meta_all = sb("meta_all", [P, C, NF], I32)
        small = sb("small", [P, 16])
        row1 = sb("row1", [1, 4, P])
        ends = sb("ends", [1, 2, 4], I32)
        zero_row = sb("zero_row", [1, D])
        unsorted = sb("unsorted", [P, 1], I32)
        rank_dst = sb("rank_dst", [P, CH], I32)
        rank_tmp = sb("rank_tmp", [P, CH])
        rank_neg = sb("rank_neg", [P, CH])
        rank_no = sb("rank_no_row", [P, CH])
        rank_sum = sb("rank_sum_col", [P, 1])
        rank_idx = sb("rank_idx", [P, 1], I32)
        rank_rec = sb("rank_rec", [P, 4], I32)
        rank_row = sb("rank_row", [P, D])

        names = []
        for table in (ENGINE_SIGNALS, DMA_SIGNALS):
            for uses in table.values():
                names += [n for n in uses if n not in names]
        engine_sems = {n: sem(n) for n in names if any(n in u for u in ENGINE_SIGNALS.values())}
        dma_sems = {n: [sem(f"{n}{s}") for s in range(DEPTH)] for n in names
                    if any(n in u for u in DMA_SIGNALS.values())}
        in_slot = [len(range(s, NG, DEPTH)) for s in range(DEPTH)]

        def signals(phase):
            found = {}
            earlier = PHASES[:PHASES.index(phase)]
            for n, per in ENGINE_SIGNALS[phase].items():
                found[n] = Signal(engine_sems[n], sum(ENGINE_SIGNALS[p].get(n, 0) for p in earlier) * NG, per)
            for n, per in DMA_SIGNALS[phase].items():
                dmas = sum(DMA_SIGNALS[p].get(n, 0) for p in earlier)
                found[n] = DmaSignal(dma_sems[n], [16 * dmas * c for c in in_slot], per)
            return found

        s_settled = sem("settled")
        s_phase = sem("phase_done")
        s_weights = sem("weights_in")
        s_raw = sem("raw_in")
        s_edge_copy = sem("edge_copy")
        s_pool_const = sem("pool_const")
        s_pads = sem("pads_set")
        s_prep = sem("prep_dve")
        s_prep_pe = sem("prep_pe")
        s_rec_out = sem("rec_out")
        s_halo = sem("halo_in")
        s_sorted = sem("list_sorted")
        s_tables_out = sem("tables_out")
        s_rank = sem("rank_dve")
        s_disorder = sem("disorder")
        s_rank_no = sem("rank_no")
        s_rank_sum = sem("rank_sum")
        s_rank_in = sem("rank_in")
        s_rank_copy = sem("rank_copy")
        s_rank_row = sem("rank_row_in")
        s_rank_out = sem("rank_out")
        s_rank_done = sem("rank_done")

        block = ctx.enter_context(nc.Block())

        def settle(eng):
            eng.sem_inc(s_settled, 1)

        def f32(tile):
            return tile.bitcast(F32)

        def word(st, f):
            return meta[:, st.s, :, f]

        def backwards(ap):
            (ps, pn), (fs, fn) = ap.ap
            return bass.AP(ap.tensor, ap.offset + fs * (fn - 1), [[ps, pn], [-fs, fn]])

        def lanes(tile):
            return tile.rearrange("d (p t) -> d p t", t=T)

        def rows_of(bank):
            return psum[bank][:, 0:T * D].rearrange("p (t d) -> p t d", t=T)

        def head_rows(bank):
            return psum[bank][:, T * D:T * D + T * HEADS].rearrange("p (t h) -> p t h", t=T)

        def flat(tile):
            return tile.rearrange("p t d -> p (t d)")

        def turn(pe, bank, rows):
            for t in range(T):
                last = pe.transpose(lanes(psum[bank][0:D, :])[:, :, t], rows[:, t, :], ident[:, :])
            return last

        def turn_back(pe, bank, cols):
            for t in range(T):
                last = pe.transpose(rows_of(bank)[:, t, :], lanes(cols)[:, :, t], ident[0:D, 0:D])
            return last

        def times(pe, bank, *products):
            for t in range(T):
                for i, (cols, weight) in enumerate(products):
                    last = pe.matmul(rows_of(bank)[:, t, :], lanes(cols)[:, :, t], weight,
                                     start=(i == 0), stop=(i == len(products) - 1))
            return last

        def times_cols(pe, bank, cols, weight):
            return pe.matmul(psum[bank][0:D, :], weight, cols, start=True, stop=True)

        def ln_stats(dve, sg, n, st, y):
            for t in range(T):
                last = dve.bn_stats(ln_tiles[n - 1][0][:, st.s2, t, :], y[:, t, :])
            last.then_inc(sg[f"ln{n}_dve"].sem, 1)

        def ln_aggr(dve, sg, n, st):
            stats, mv, _ = ln_tiles[n - 1]
            d, ac = sg[f"ln{n}_dve"], sg[f"ln{n}_act"]
            dve.wait_ge(*d.of(st, 1))
            if old := st.back(2):
                dve.wait_ge(*ac.of(old))
            settle(dve)
            for t in range(T):
                last = dve.bn_aggr(mv[:, st.s2, t, :], stats[:, st.s2, t, :])
            last.then_inc(d.sem, 1)

        def ln_root(act, sg, n, st):
            _, mv, sc = ln_tiles[n - 1]
            d, ac = sg[f"ln{n}_dve"], sg[f"ln{n}_act"]
            act.wait_ge(*d.of(st, 2))
            act.activation(sc[:, st.s2, 1, :], mv[:, st.s2, :, 1], ACT.Ln, bias=eps_col[:, 0:1]).then_inc(ac.sem, 1)
            act.wait_ge(*ac.of(st, 1))
            act.activation(sc[:, st.s2, 2, :], sc[:, st.s2, 1, :], ACT.Exp, scale=-0.5).then_inc(ac.sem, 1)

        def ln_newton(dve, sg, n, st, i, mask=None):
            _, mv, sc = ln_tiles[n - 1]
            d, ac = sg[f"ln{n}_dve"], sg[f"ln{n}_act"]
            r0, t1, t2, r, nb = (sc[:, st.s2, k, :] for k in (2, 3, 4, 5, 6))
            if i == 0:
                dve.wait_ge(*ac.of(st, 2))
                dve.scalar_tensor_tensor(t1, mv[:, st.s2, :, 1], EPS, r0, ALU.add, ALU.mult).then_inc(d.sem, 1)
            elif i == 1:
                dve.wait_ge(*d.of(st, 3))
                dve.scalar_tensor_tensor(t2, t1, -0.5, r0, ALU.mult, ALU.mult).then_inc(d.sem, 1)
            elif i == 2:
                dve.wait_ge(*d.of(st, 4))
                dve.scalar_tensor_tensor(r, t2, 1.5, r0, ALU.add, ALU.mult).then_inc(d.sem, 1)
                if mask is not None:
                    dve.wait_ge(*d.of(st, 5))
                    dve.tensor_tensor(r, r, mask, ALU.mult).then_inc(d.sem, 1)
            elif ac.per == 3:
                dve.wait_ge(*d.of(st, d.per - 1))
                dve.scalar_tensor_tensor(nb, mv[:, st.s2, :, 0], -1.0, r, ALU.mult, ALU.mult).then_inc(d.sem, 1)

        def ln_apply_dve(dve, sg, n, st, y, result):
            _, mv, sc = ln_tiles[n - 1]
            dve.wait_ge(*sg[f"ln{n}_dve"].of(st, 5))
            settle(dve)
            for t in range(T):
                last = dve.tensor_scalar(result[:, t, :], y[:, t, :], mv[:, st.s2, t, 0:1],
                                         sc[:, st.s2, 5, t:t + 1], ALU.subtract, ALU.mult)
            last.then_inc(sg[f"ln{n}_dve"].sem, 1)

        def ln_apply_act(act, sg, n, st, y, result):
            _, _, sc = ln_tiles[n - 1]
            act.wait_ge(*sg[f"ln{n}_dve"].of(st))
            for t in range(T):
                last = act.activation(result[:, t, :], y[:, t, :], ACT.Identity,
                                      bias=sc[:, st.s2, 6, t:t + 1], scale=sc[:, st.s2, 5, t:t + 1])
            last.then_inc(sg[f"ln{n}_act"].sem, 1)

        @block.sync
        def _(sp):
            for n, tile in w.items():
                sp.dma_start(tile[0:D, :], a[n]).then_inc(s_weights, 16)
                if n in bias_of:
                    sp.dma_start(tile[D:D + 1, :], a[bias_of[n]].unsqueeze(0)).then_inc(s_weights, 16)
            sp.wait_ge(s_pads, 5)
            full = E // C
            for i, name in enumerate(("src", "dst", "edge_weight")):
                v = a[name] if name != "edge_weight" else a[name].bitcast(I32)
                sp.dma_start(raw[i][0:full, :], v[0:full * C].rearrange("(p c) -> p c", c=C)).then_inc(s_raw, 16)
                sp.dma_start(raw[i][full:full + 1, 0:E - full * C], v[full * C:E].unsqueeze(0)).then_inc(s_raw, 16)
            sp.dma_start(mean_t[EP:EP + 1, :], zero_row[:, :]).then_inc(s_edge_copy, 16)

            sp.wait_ge(s_prep, 4)
            sp.dma_start(edges[0:1, :], ends[:, 0, :]).then_inc(s_rec_out, 16)
            sp.dma_start(edges[EP + 1:EP + 2, :], ends[:, 1, :]).then_inc(s_rec_out, 16)
            sp.dma_start(edges[1:EP + 1, :].rearrange("(p c) f -> p (c f)", p=P),
                         rec[:, :, :].rearrange("p c f -> p (c f)")).then_inc(s_rec_out, 16)
            sp.wait_ge(s_rec_out, 48)
            halo_view = bass.AP(edges.tensor, 0, [[4 * C, P], [1, 4 * (C + 2)]])
            sp.dma_start(halo[:, :, :].rearrange("p c f -> p (c f)"), halo_view).then_inc(s_halo, 16)
            sp.wait_ge(s_prep, 7)
            disorder = sp.value_load(unsorted[0:1, 0:1])
            with sp.If(disorder > 0):
                body = E // GR * GR
                sp.dma_start(edge_rows[0:body, :].rearrange("(p r) d -> p (r d)", p=P),
                             a["edge_attr_96"][0:body, :].rearrange("(p r) d -> p (r d)", p=P)).then_inc(s_edge_copy, 16)
                sp.dma_start(edge_rows[body:E, :], a["edge_attr_96"][body:E, :]).then_inc(s_edge_copy, 16)
                sp.dma_start(edge_rows[E:EP, :], a["edge_attr_96"][0:EP - E, :]).then_inc(s_edge_copy, 16)
                sp.dma_start(dst_list.rearrange("(p c) -> p c", p=P), raw[1][:, :]).then_inc(s_rec_out, 16)
                sp.wait_ge(s_rec_out, 64)
                for c in range(CHUNKS):
                    if c:
                        sp.wait_ge(s_rank, 3 * C * c + c)
                    chunk = dst_list[c * CH:(c + 1) * CH]
                    sp.dma_start(rank_dst[:, :], chunk.unsqueeze(0).to_broadcast([P, CH])).then_inc(s_rank_in, 16)
                sp.wait_ge(s_edge_copy, 64)
                sp.wait_ge(s_rank_done, 1)
                sp.dma_start(edge_rows.rearrange("(p r) d -> p (r d)", p=P),
                             edges2[1:EP + 1, :].rearrange("(p r) d -> p (r d)", p=P)).then_inc(s_edge_copy, 16)
                sp.wait_ge(s_edge_copy, 80)
                sp.dma_start(halo[:, :, :].rearrange("p c f -> p (c f)"), halo_view).then_inc(s_halo, 16)
                sp.wait_ge(s_halo, 32)
            sp.sem_inc(s_sorted, 1)

            sp.wait_ge(s_pool_const, 6)
            sp.dma_start(node_t[:, 0:2].rearrange("(p c) f -> p c f", p=P), f32(node_row)[:, :, :])\
                .then_inc(s_tables_out, 16)
            sp.wait_ge(s_prep, PREP_ALL)
            sp.dma_start(meta_t.rearrange("(p c) f -> p (c f)", p=P),
                         meta_all[:, :, :].rearrange("p c f -> p (c f)")).then_inc(s_tables_out, 16)
            sp.dma_start(flags_f.rearrange("(p c) -> p c", p=P), flag_tile[:, 0, :]).then_inc(s_tables_out, 16)
            sp.dma_start(flags_b.rearrange("(p c) -> p c", p=P), flag_tile[:, 1, :]).then_inc(s_tables_out, 16)
            sp.wait_ge(s_tables_out, 64)
            sp.wait_ge(s_edge_copy, 16)
            sp.sem_inc(s_phase, 1)

            meta_g = meta_t.rearrange("(g p t) f -> g p t f", p=P, t=T)
            source_g = source.rearrange("(g p t) f -> g p t f", p=P, t=T)

            def free(*signals_of_old):
                for sig, old in signals_of_old:
                    if old:
                        sp.wait_ge(*sig.of(old))
                        settle(sp)

            def load_meta(st, sig, g):
                sp.dma_start(meta[:, st.s, :, :], meta_g[g]).then_inc(sig.sems[st.s], 16)

            def load_flags(st, sig, table, g):
                sp.dma_start(flag[:, st.s, :], table[bass.ds(g * GR, GR)].unsqueeze(0).to_broadcast([D, GR]))\
                    .then_inc(sig.sems[st.s], 16)

            def save(st, sig, made, tile, table, g=None):
                sp.wait_ge(*made.of(st))
                settle(sp)
                sp.dma_start(groups(table)[st.g if g is None else g], tile).then_inc(sig.sems[st.s], 16)

            def load_rows(st, sig, tile, table, g):
                sp.dma_start(flat(tile[:, st.s]), groups(table)[g]).then_inc(sig.sems[st.s], 16)

            def load_source(st, sig, g):
                sp.dma_start(srcs[:, st.s, :, :], source_g[g]).then_inc(sig.sems[st.s], 16)

            def finish(sg, *names):
                for n in names:
                    for s in range(DEPTH):
                        sp.wait_ge(sg[n].sems[s], sg[n].bases[s] + 16 * sg[n].per * in_slot[s])
                sp.sem_inc(s_phase, 1)

            sg = signals("A")
            nodes = wide_rows
            half, h, y1, x1, x2 = row_tiles[:5]

            def phase_a(at):
                if st := at(0):
                    free((sg["ids_out"], st.back(DEPTH)))
                    load_meta(st, sg["meta_in"], st.g)
                if st := at(1):
                    old = st.back(DEPTH)
                    free((sg["node_stored"], old), (sg["y1"], old))
                    if isinstance(st.g, int) and st.g == NG - 1:
                        sp.dma_start(nodes[0:NLAST // T, st.s, :, X_PART],
                                     a["x"][(NG - 1) * GR:N, :].rearrange("(p t) d -> p t d", t=T))\
                            .then_inc(sg["x_in"].sems[st.s], 16)
                    else:
                        sp.dma_start(nodes[:, st.s, :, X_PART],
                                     nodes_in.rearrange("(g p t) d -> g p t d", p=P, t=T)[st.g])\
                            .then_inc(sg["x_in"].sems[st.s], 16)

                if st := at(3):
                    sp.wait_ge(*sg["own_part"].of(st))
                    settle(sp)
                    sp.dma_start(node_t[:, 2:ROW].rearrange("(g p t) d -> g p t d", p=P, t=T)[st.g],
                                 nodes[:, st.s, :, 2:ROW]).then_inc(sg["node_stored"].sems[st.s], 16)
                    save(st, sg["h_stored"], sg["h_rows"], flat(h[:, st.s2]), h_t, NG + st.g)
                if st := at(5):
                    save(st, sg["x1_stored"], sg["ln1_dve"], flat(x1[:, st.s2]), x1_t, NG + st.g)
                if st := at(6):
                    save(st, sg["x2_stored"], sg["ln2_act"], flat(x2[:, st.s2]), x2_t, NG + st.g)

            ticks(sp, NG, 6, phase_a)
            finish(sg, "node_stored", "h_stored", "x1_stored", "x2_stored", "ids_out")

            sb_ = signals("B")
            x2 = deep_rows[0]
            xw, hsum, h, y2, x3, res, own2 = row_tiles

            def phase_b(at):
                if st := at(0):
                    old = st.back(DEPTH)
                    free((sb_["weighted"], old), (sb_["own_in"], old))
                    load_meta(st, sb_["meta_in"], st.g)
                if st := at(2):
                    old = st.back(DEPTH)
                    free((sb_["scanned"], old))
                    load_flags(st, sb_["flags_in"], flags_f, st.g)
                    free((sb_["y2"], old))
                    load_rows(st, sb_["x_in"], x2, x2_t, NG + st.g)

                if st := at(3):
                    sp.wait_ge(*sb_["ids_made"].of(st))
                    settle(sp)
                    sp.dma_start(source_g[st.g], srcs[:, st.s, :, :]).then_inc(sb_["ids_stored"].sems[st.s], 16)
                    sp.wait_ge(*sb_["own_in"].of(st))
                    settle(sp)
                    sp.dma_start(x_own.rearrange("(g p t) d -> g p t d", p=P, t=T)[st.g],
                                 wide_rows[:, st.s, :, X_PART]).then_inc(sb_["own_out"].sems[st.s], 16)
                if st := at(4):
                    save(st, sb_["conv_stored"], sb_["conv_out"], flat(h[:, st.s2]), h_t)
                if st := at(5):
                    save(st, sb_["x2_stored"], sb_["ln2_act"], flat(x3[:, st.s2]), x3_t, NG + st.g)
                if st := at(6):
                    save(st, sb_["own_part_stored"], sb_["own_part"], flat(own2[:, st.s2]), own_part)
                if st := at(7):
                    sp.wait_ge(*sb_["ln1_act"].of(st))
                    settle(sp)
                    if isinstance(st.g, int) and st.g == NG - 1:
                        sp.dma_start(out[(NG - 1) * GR:N, :].rearrange("(p t) d -> p (t d)", t=T),
                                     flat(res[0:NLAST // T, st.s2])).then_inc(sb_["x1_stored"].sems[st.s], 16)
                    else:
                        sp.dma_start(groups(nodes_out)[st.g], flat(res[:, st.s2]))\
                            .then_inc(sb_["x1_stored"].sems[st.s], 16)

            ticks(sp, NG, 7, phase_b)
            finish(sb_, "own_out", "conv_stored", "own_part_stored", "x2_stored", "ids_stored", "x1_stored")

            sc = signals("C")
            hs, own2, x, ea = deep_rows
            x1, e_c = row_tiles[4], col_tiles[2]

            def phase_c_from(edge_table):
                def phase_c(at):
                    if st := at(0):
                        free((sc["src_in"], st.back(DEPTH)))
                        load_source(st, sc["source_in"], st.g)
                    if st := at(2):
                        old = st.back(DEPTH)
                        free((sc["end_kept"], old))
                        load_meta(st, sc["meta_in"], st.g)
                        free((sc["edge_turned"], old))
                        if edge_table is edge_rows:
                            load_rows(st, sc["edge_in"], ea, edge_rows, st.g)
                        elif isinstance(st.g, int) and st.g == NG - 1:
                            sp.dma_start(flat(ea[0:NLAST // T, st.s]),
                                         edge_table[(NG - 1) * GR:E, :].rearrange("(p t) d -> p (t d)", t=T))\
                                .then_inc(sc["edge_in"].sems[st.s], 16)
                        else:
                            load_rows(st, sc["edge_in"], ea, edge_table[0:(NG - 1) * GR, :], st.g)
                        free((sc["scanned"], old))
                        load_flags(st, sc["flags_in"], flags_f, st.g)
                        free((sc["y1"], old))
                        load_rows(st, sc["x_in"], own2, own_part, st.g)
                        load_rows(st, sc["x_in"], x, x_own, st.g)

                    if st := at(4):
                        sp.wait_ge(*sc["e_cols"].of(st))
                        settle(sp)
                        sp.dma_start(e_t[st.g], e_c[0:D, st.s2, :]).then_inc(sc["e_stored"].sems[st.s], 16)
                    if st := at(7):
                        save(st, sc["x1_stored"], sc["ln1_act"], flat(x1[:, st.s2]), x1_t)

                ticks(sp, NG, 7, phase_c)

            disorder = sp.value_load(unsorted[0:1, 0:1])
            with sp.If(disorder > 0):
                phase_c_from(edge_rows)
            with sp.If(disorder < 1):
                phase_c_from(a["edge_attr_96"])
            finish(sc, "x1_stored", "e_stored")

            sd = signals("D")
            xs, xo = deep_rows[:2]
            e_c = deep_cols[2]

            def phase_d(at):
                if st := at(0):
                    free((sd["src_in"], st.back(DEPTH)))
                    load_source(st, sd["source_in"], NG - 1 - st.g)
                if st := at(2):
                    g = NG - 1 - st.g
                    old = st.back(DEPTH)
                    free((sd["own_turned"], old))
                    load_rows(st, sd["x_in"], xo, x1_t, g)
                    free((sd["score"], old))
                    sp.dma_start(e_c[0:D, st.s, :], e_t[g]).then_inc(sd["edge_in"].sems[st.s], 16)
                    free((sd["scanned"], old))
                    load_flags(st, sd["meta_in"], flags_b, g)

            ticks(sp, NG, 2, phase_d)
            finish(sd, "x1_stored")

            se = signals("E")
            xs, xo = deep_rows[:2]

            def phase_e(at):
                if st := at(0):
                    free((se["src_in"], st.back(DEPTH)))
                    load_source(st, se["source_in"], NG - 1 - st.g)
                if st := at(2):
                    g = NG - 1 - st.g
                    old = st.back(DEPTH)
                    free((se["scanned"], old))
                    load_flags(st, se["meta_in"], flags_b, g)
                    free((se["y2"], old))
                    load_rows(st, se["x_in"], xo, x2_t, g)

            ticks(sp, NG, 2, phase_e)
            finish(se, "x1_stored")

            sf = signals("F")

            def phase_f(at):
                if st := at(0):
                    free((sf["src_in"], st.back(DEPTH)))
                    load_source(st, sf["source_in"], NG - 1 - st.g)
                if st := at(2):
                    g = NG - 1 - st.g
                    old = st.back(DEPTH)
                    free((sf["scanned"], old), (sf["conv_out"], old))
                    load_flags(st, sf["meta_in"], flags_b, g)
                    load_meta(st, sf["meta_in"], g)

            ticks(sp, NG, 2, phase_f)
            finish(sf, "x1_stored")

            sh = signals("G")
            xs, xo, mo = deep_rows[:3]

            def phase_g(at):
                if st := at(0):
                    free((sh["src_in"], st.back(DEPTH)))
                    load_source(st, sh["source_in"], NG - 1 - st.g)
                if st := at(2):
                    g = NG - 1 - st.g
                    old = st.back(DEPTH)
                    free((sh["scanned"], old))
                    load_flags(st, sh["meta_in"], flags_b, g)
                    free((sh["y1"], old))
                    load_rows(st, sh["x_in"], xo, x3_t, g)
                    load_rows(st, sh["x_in"], mo, mean_t[0:EP, :], g)
                    free((sh["ids_out"], old))
                    load_meta(st, sh["index_in"], g)

            ticks(sp, NG, 2, phase_g)
            finish(sh, "ids_out")

        def gather(pool, tile, table, index, sig, st):
            pool.indirect_dma_start(out=tile, out_offset=None, in_=table,
                                    in_offset=bass.IndirectOffsetOnAxis(ap=index, axis=0),
                                    bounds_check=table.shape[0] - 1, oob_is_err=False).then_inc(sig.sems[st.s], 16)

        def scatter(pool, table, index, tile, sig, st, scale=1):
            pool.indirect_dma_start(out=table, out_offset=bass.IndirectOffsetOnAxis(ap=index, axis=0), in_=tile,
                                    in_offset=None, bounds_check=scale * (N - 1), oob_is_err=False)\
                .then_inc(sig.sems[st.s], 16)

        @block.gpsimd
        def _(pool):
            pool.iota(slot_no[:, :], [[1, C]], base=0, channel_multiplier=C).then_inc(s_pool_const, 1)
            pool.iota(node_row[:, :, :], [[1, C], [0, 2]], base=EP, channel_multiplier=C).then_inc(s_pool_const, 1)
            pool.memset(ident[:, :], 0.0).then_inc(s_pool_const, 1)
            pool.memset(head_sum[:, :], float(HD) ** -0.5).then_inc(s_pool_const, 1)
            pool.wait_ge(s_pool_const, 4)
            pool.affine_select(out=ident[:, :], in_=ident[:, :], compare_op=ALU.not_equal, fill=1.0, base=0,
                               pattern=[[-1, P]], channel_multiplier=1).then_inc(s_pool_const, 1)
            blocks = head_sum[:, :].rearrange("p (h c) -> p h c", c=HD)
            pool.affine_select(out=blocks, in_=blocks, compare_op=ALU.is_ge, fill=0.0, base=0,
                               pattern=[[-HD, HEADS], [0, HD]], channel_multiplier=1).then_inc(s_pool_const, 1)
            pool.wait_ge(s_pool_const, 6)
            pool.affine_select(out=blocks, in_=blocks, compare_op=ALU.is_ge, fill=0.0, base=HD - 1,
                               pattern=[[HD, HEADS], [0, HD]], channel_multiplier=-1).then_inc(s_pool_const, 1)

            pool.wait_ge(s_prep, 7)
            disorder = pool.value_load(unsorted[0:1, 0:1])
            with pool.If(disorder > 0):
                pool.wait_ge(s_rank, CHUNKS * (3 * C + 1))
                pool.wait_ge(s_edge_copy, 64)
                unsorted_rows = edge_rows.rearrange("(p c) d -> p c d", p=P)

                def move(c, first):
                    if not first:
                        pool.wait_ge(s_rank_out, 32 * c)
                    pool.dma_start(rank_row[:, :], unsorted_rows[:, bass.ds(c, 1), :].rearrange("p c d -> p (c d)"))\
                        .then_inc(s_rank_row, 16)
                    pool.tensor_copy(rank_idx[:, :], work[0][:, bass.ds(c, 1)]).then_inc(s_rank_copy, 1)
                    pool.tensor_copy(rank_rec[:, :], rec[:, bass.ds(c, 1), :].rearrange("p c f -> p (c f)"))\
                        .then_inc(s_rank_copy, 1)
                    pool.wait_ge(s_rank_copy, 2 * c + 2)
                    pool.wait_ge(s_rank_row, 16 * c + 16)
                    settle(pool)
                    for table, tile in ((edges2, rank_row), (edges, rank_rec)):
                        pool.indirect_dma_start(out=table, out_offset=bass.IndirectOffsetOnAxis(
                            ap=rank_idx[:, 0:1], axis=0), in_=tile[:, :], in_offset=None,
                            bounds_check=EP, oob_is_err=False).then_inc(s_rank_out, 16)

                move(0, True)
                with pool.Fori(1, C) as c:
                    move(c, False)
                pool.wait_ge(s_rank_out, 32 * C)
                pool.sem_inc(s_rank_done, 1)

            sg = signals("A")
            pool.wait_ge(s_phase, 1)

            def phase_a(at):
                st = at(0)
                pool.wait_ge(*sg["meta_in"].of(st))
                settle(pool)
                for t in range(T):
                    scatter(pool, node_places, meta[:, st.s, t, END_DST:END_DST + 1],
                            f32(meta[:, st.s, t, SLOT:SLOT + 2]), sg["ids_out"], st, ROW // 2)

            ticks(pool, NG, 0, phase_a)

            sb_ = signals("B")
            pool.wait_ge(s_phase, 2)

            def phase_b(at):
                st = at(0)
                old = st.back(DEPTH)
                pool.wait_ge(*sb_["meta_in"].of(st))
                if old:
                    pool.wait_ge(*sb_["weighted"].of(old))
                    pool.wait_ge(*sb_["ids_made"].of(old))
                settle(pool)
                for t in range(T):
                    gather(pool, src_rows[:, st.s, t, :], node_sources, meta[:, st.s, t, SRC:SRC + 1],
                           sb_["src_in"], st)
                if old:
                    pool.wait_ge(*sb_["summed"].of(old))
                    pool.wait_ge(*sb_["own_out"].of(old))
                    settle(pool)
                for t in range(T):
                    gather(pool, wide_rows[:, st.s, t, :], node_t, meta[:, st.s, t, DST:DST + 1],
                           sb_["own_in"], st)

            ticks(pool, NG, 0, phase_b)

            def sources(phase, table, field, reader, extra=0, more=None):
                s = signals(phase)
                xs = deep_rows[0]
                pool.wait_ge(s_phase, PHASES.index(phase) + 1)

                def body(at):
                    if st := at(0):
                        pool.wait_ge(*s["source_in"].of(st))
                        if old := st.back(DEPTH):
                            pool.wait_ge(*s[reader].of(old))
                        settle(pool)
                        for t in range(T):
                            gather(pool, xs[:, st.s, t, :], table, srcs[:, st.s, t, field:field + 1],
                                   s["src_in"], st)
                    if more:
                        more(s, at)

                ticks(pool, NG, extra, body)

            def attend(s, at):
                sc_c, ex_c, wv_c, z_c, y_c, zg_c = col_tiles
                if st := at(4):
                    pool.wait_ge(*s["z_guarded"].of(st))
                    if old := st.back(2):
                        pool.wait_ge(*s["y_turned"].of(old))
                    y = y_c[0:D, st.s2, :]
                    pool.tensor_tensor(y, zg_c[0:D, st.s2, :], deep_cols[0][0:D, st.s, :], ALU.mult)\
                        .then_inc(s["attn"].sem, 1)
                    pool.wait_ge(*s["attn"].of(st, 1))
                    pool.wait_ge(*s["scanned"].of(st))
                    pool.tensor_tensor(y, y, wv_c[0:D, st.s2, :], ALU.add).then_inc(s["attn"].sem, 1)

            def results(s, at):
                if st := at(3):
                    pool.wait_ge(*s["ln1_act"].of(st))
                    pool.wait_ge(*s["index_in"].of(st))
                    settle(pool)
                    for t in range(T):
                        scatter(pool, out, meta[:, st.s, t, START_DST:START_DST + 1], row_tiles[2][:, st.s2, t, :],
                                s["ids_out"], st)

            sources("C", h_t, 0, "weighted")
            sources("D", x1_t, 0, "src_turned", 4, attend)
            sources("E", x2_t, 1, "src_turned")
            sources("F", x3_t, 1, "src_turned")
            sources("G", mean_t, 2, "src_turned", 3, results)

        @block.tensor
        def _(pe):
            pe.wait_ge(s_pads, 5)
            pe.wait_ge(s_prep, 5)
            pe.matmul(psum[0][:, 0:1], ones[:, :], small[:, 0:1], start=True, stop=True).then_inc(s_prep_pe, 1)
            pe.wait_ge(s_pool_const, 7)
            pe.wait_ge(s_prep, 16)
            pe.transpose(psum[1][0:1, 0:P], small[:, 2:3], ident[:, :]).then_inc(s_prep_pe, 1)
            pe.transpose(psum[2][0:1, 0:P], small[:, 3:4], ident[:, :]).then_inc(s_prep_pe, 1)
            pe.wait_ge(s_prep, 20)
            pe.matmul(psum[3][:, 0:1], row1[0:1, 2, :], ones[0:1, 0:1], start=True, stop=True).then_inc(s_prep_pe, 1)
            pe.matmul(psum[4][:, 0:1], row1[0:1, 3, :], ones[0:1, 0:1], start=True, stop=True).then_inc(s_prep_pe, 1)
            pe.wait_ge(s_weights, 16 * (len(w) + len(bias_of)))

            sg = signals("A")
            nodes = wide_rows
            h = row_tiles[1]
            x_c, h_c = col_tiles[:2]
            pe.wait_ge(s_phase, 1)

            def phase_a(at):
                if st := at(1):
                    pe.wait_ge(*sg["x_cols"].of(st))
                    if old := st.back(2):
                        pe.wait_ge(*sg["h_rows"].of(old))
                    times(pe, 2 + st.s2, (x_c[:, st.s2], w["L0_gnn_W1_loop"][:, :]))\
                        .then_inc(sg["loop1_done"].sem, 1)
                if st := at(0):
                    pe.wait_ge(*sg["x_in"].of(st))
                    if old := st.back(2):
                        pe.wait_ge(*sg["x_cols"].of(old))
                    turn(pe, st.s2, nodes[:, st.s, :, X_PART]).then_inc(sg["x_turned"].sem, 1)
                if st := at(2):
                    pe.wait_ge(*sg["h_cols"].of(st))
                    if old := st.back(2):
                        pe.wait_ge(*sg["half"].of(old))
                    times(pe, 6 + st.s2, (h_c[:, st.s2], w["L0_gnn_W2_loop"][:, :]))\
                        .then_inc(sg["loop2_done"].sem, 1)
                if st := at(1):
                    pe.wait_ge(*sg["h_rows"].of(st))
                    if old := st.back(2):
                        pe.wait_ge(*sg["h_cols"].of(old))
                    turn(pe, 4 + st.s2, h[:, st.s2]).then_inc(sg["h_turned"].sem, 1)

            ticks(pe, NG, 2, phase_a)

            sb_ = signals("B")
            xw, hsum, h, y2, x3, res, own2 = row_tiles
            x2 = deep_rows[0]
            seg, x2_c, g_c, h_c = col_tiles[:4]
            pe.wait_ge(s_phase, 2)

            def phase_b(at):
                if st := at(4):
                    pe.wait_ge(*sb_["h_cols"].of(st))
                    if old := st.back(1):
                        pe.wait_ge(*sb_["own_part"].of(old))
                    times(pe, 6, (h_c[:, st.s2], w["L0_gnn_W2_loop"][:, :])).then_inc(sb_["loop2_done"].sem, 1)
                if st := at(3):
                    pe.wait_ge(*sb_["conv_out"].of(st))
                    if old := st.back(1):
                        pe.wait_ge(*sb_["h_cols"].of(old))
                    turn(pe, 5, h[:, st.s2]).then_inc(sb_["h_turned"].sem, 1)
                if st := at(2):
                    pe.wait_ge(*sb_["mlp_hidden"].of(st))
                    if old := st.back(1):
                        pe.wait_ge(*sb_["y2"].of(old))
                    times(pe, 4, (g_c[:, st.s2], w["L2_gnn_W2"][:, :])).then_inc(sb_["mlp2_done"].sem, 1)
                    pe.wait_ge(*sb_["scanned"].of(st))
                    if old := st.back(1):
                        pe.wait_ge(*sb_["summed"].of(old))
                    times(pe, 3, (seg[0:D, st.s2], w["L0_gnn_W1"][:, :])).then_inc(sb_["conv_done"].sem, 1)
                if st := at(1):
                    pe.wait_ge(*sb_["x2_cols"].of(st))
                    if old := st.back(1):
                        pe.wait_ge(*sb_["mlp_hidden"].of(old))
                    times_cols(pe, 2, x2_c[:, st.s2], w["L2_gnn_W1"][:, :]).then_inc(sb_["mlp1_done"].sem, 1)
                    pe.wait_ge(*sb_["weighted"].of(st))
                    if old := st.back(1):
                        pe.wait_ge(*sb_["scanned"].of(old))
                    turn(pe, 1, xw[:, st.s2]).then_inc(sb_["src_turned"].sem, 1)
                if st := at(0):
                    pe.wait_ge(*sb_["x_in"].of(st))
                    if old := st.back(1):
                        pe.wait_ge(*sb_["x2_cols"].of(old))
                    turn(pe, 0, x2[:, st.s]).then_inc(sb_["x2_turned"].sem, 1)

            ticks(pe, NG, 4, phase_b)

            sc = signals("C")
            ea = deep_rows[3]
            xw = row_tiles[0]
            seg, ea_c, e_c = col_tiles[:3]
            pe.wait_ge(s_phase, 3)

            def phase_c(at):
                if st := at(2):
                    pe.wait_ge(*sc["scanned"].of(st))
                    if old := st.back(2):
                        pe.wait_ge(*sc["summed"].of(old))
                    times(pe, 6 + st.s2, (seg[0:D, st.s2], w["L0_gnn_W2"][:, :])).then_inc(sc["conv_done"].sem, 1)
                if st := at(1):
                    pe.wait_ge(*sc["edge_cols"].of(st))
                    if old := st.back(2):
                        pe.wait_ge(*sc["e_cols"].of(old))
                    times_cols(pe, 4 + st.s2, ea_c[:, st.s2], w["L1_gnn_We"][:, :]).then_inc(sc["e_done"].sem, 1)
                    pe.wait_ge(*sc["weighted"].of(st))
                    if old := st.back(2):
                        pe.wait_ge(*sc["scanned"].of(old))
                    turn(pe, 2 + st.s2, xw[:, st.s2]).then_inc(sc["src_turned"].sem, 1)
                if st := at(0):
                    pe.wait_ge(*sc["edge_in"].of(st))
                    if old := st.back(2):
                        pe.wait_ge(*sc["edge_cols"].of(old))
                    turn(pe, st.s2, ea[:, st.s]).then_inc(sc["edge_turned"].sem, 1)

            ticks(pe, NG, 2, phase_c)

            sd = signals("D")
            xs, xo = deep_rows[:2]
            xf_c, xs_c, e_c = deep_cols
            sc_c, ex_c, wv_c, z_c, y_c, zg_c = col_tiles
            pe.wait_ge(s_phase, 4)

            def phase_d(at):
                if st := at(5):
                    bank = 6 + st.s2
                    pe.wait_ge(*sd["attn"].of(st))
                    if old := st.back(2):
                        pe.wait_ge(*sd["divided"].of(old))
                    for t in range(T):
                        pe.matmul(head_rows(bank)[:, t, :], lanes(z_c[0:D, st.s2])[:, :, t],
                                  ident[0:D, 0:D].rearrange("p (h c) -> p h c", c=HD)[:, :, 0],
                                  start=True, stop=True)
                    turn_back(pe, bank, y_c[0:D, st.s2]).then_inc(sd["y_turned"].sem, 1)
                if st := at(3):
                    pe.wait_ge(*sd["score"].of(st))
                    if old := st.back(1):
                        pe.wait_ge(*sd["exped"].of(old))
                    times_cols(pe, 5, sc_c[0:D, st.s2], head_sum[:, :]).then_inc(sd["sum_done"].sem, 1)
                    if old := st.back(1):
                        pe.wait_ge(*sd["msg"].of(old))
                    times_cols(pe, 4, xs_c[:, st.s], w["L1_gnn_Wv"][:, :]).then_inc(sd["v_done"].sem, 1)
                if st := at(1):
                    pe.wait_ge(*sd["src_cols"].of(st))
                    if old := st.back(1):
                        pe.wait_ge(*sd["score"].of(old))
                    times_cols(pe, 2, xs_c[:, st.s], w["L1_gnn_Wk"][:, :]).then_inc(sd["k_done"].sem, 1)
                    pe.wait_ge(*sd["filled"].of(st))
                    times_cols(pe, 3, xf_c[:, st.s], w["L1_gnn_Wq"][:, :]).then_inc(sd["q_done"].sem, 1)
                if st := at(0):
                    pe.wait_ge(*sd["x_in"].of(st))
                    if old := st.back(1):
                        pe.wait_ge(*sd["filled"].of(old))
                    turn(pe, 1, xo[:, st.s]).then_inc(sd["own_turned"].sem, 1)
                    pe.wait_ge(*sd["src_in"].of(st))
                    if old := st.back(1):
                        pe.wait_ge(*sd["src_cols"].of(old))
                    turn(pe, 0, xs[:, st.s]).then_inc(sd["src_turned"].sem, 1)

            ticks(pe, NG, 5, phase_d)

            se = signals("E")
            xs, xo = deep_rows[:2]
            seg, rst, g_c = col_tiles[:3]
            pe.wait_ge(s_phase, 5)

            def phase_e(at):
                if st := at(2):
                    pe.wait_ge(*se["mlp_hidden"].of(st))
                    if old := st.back(2):
                        pe.wait_ge(*se["y2"].of(old))
                    times(pe, 6 + st.s2, (g_c[:, st.s2], w["L2_gnn_W2"][:, :])).then_inc(se["mlp2_done"].sem, 1)
                if st := at(0):
                    pe.wait_ge(*se["x_in"].of(st))
                    if old := st.back(2):
                        pe.wait_ge(*se["rst"].of(old))
                    turn(pe, 2 + st.s2, xo[:, st.s]).then_inc(se["own_turned"].sem, 1)
                    pe.wait_ge(*se["src_in"].of(st))
                    turn(pe, st.s2, xs[:, st.s]).then_inc(se["src_turned"].sem, 1)
                if st := at(1):
                    pe.wait_ge(*se["rst"].of(st))
                    if old := st.back(2):
                        pe.wait_ge(*se["mlp_hidden"].of(old))
                    times_cols(pe, 4 + st.s2, rst[:, st.s2], w["L2_gnn_W1"][:, :]).then_inc(se["mlp1_done"].sem, 1)

            ticks(pe, NG, 2, phase_e)

            for phase, reader in (("F", "conv_out"), ("G", "y2")):
                s = signals(phase)
                xs, seg = deep_rows[0], col_tiles[0]
                pe.wait_ge(s_phase, PHASES.index(phase) + 1)

                def phase_fg(at):
                    if st := at(0):
                        pe.wait_ge(*s["src_in"].of(st))
                        if old := st.back(2):
                            pe.wait_ge(*s["scanned"].of(old))
                        turn(pe, st.s2, xs[:, st.s]).then_inc(s["src_turned"].sem, 1)
                    if st := at(1):
                        pe.wait_ge(*s["scanned"].of(st))
                        if old := st.back(2):
                            pe.wait_ge(*s[reader].of(old))
                        turn_back(pe, 2 + st.s2, seg[0:D, st.s2]).then_inc(s["y_turned"].sem, 1)

                ticks(pe, NG, 1, phase_fg)

        @block.scalar
        def _(act):
            act.preload_act_table_set("natural_log_exp_and_others")

            def store(st, sig, made, tile, table, g):
                act.wait_ge(*made.of(st))
                act.dma_start(groups(table)[g], tile).then_inc(sig.sems[st.s], 16)

            sg = signals("A")
            nodes = wide_rows
            half, h, y1, x1, x2 = row_tiles[:5]
            x_c, h_c = col_tiles[:2]
            act.wait_ge(s_phase, 1)
            act.wait_ge(s_pads, 5)

            def phase_a(at):
                if st := at(1):
                    act.wait_ge(*sg["loop1_done"].of(st))
                    act.activation(nodes[:, st.s, :, OWN_PART], rows_of(2 + st.s2), ACT.Copy)\
                        .then_inc(sg["own_part"].sem, 1)
                    if old := st.back(2):
                        act.wait_ge(*sg["h_turned"].of(old))
                        act.wait_ge(*sg["h_stored"].of(old))
                    act.activation(h[:, st.s2], rows_of(2 + st.s2), ACT.Relu).then_inc(sg["h_rows"].sem, 1)
                if st := at(0):
                    act.wait_ge(*sg["x_turned"].of(st))
                    if old := st.back(2):
                        act.wait_ge(*sg["loop1_done"].of(old))
                    act.activation(x_c[0:D, st.s2], psum[st.s2][0:D, :], ACT.Copy).then_inc(sg["x_cols"].sem, 1)
                if st := at(2):
                    act.wait_ge(*sg["loop2_done"].of(st))
                    if old := st.back(2):
                        act.wait_ge(*sg["y1"].of(old))
                    act.activation(half[:, st.s2], rows_of(6 + st.s2), ACT.Relu, scale=0.5)\
                        .then_inc(sg["half"].sem, 1)
                if st := at(4):
                    if old := st.back(2):
                        act.wait_ge(*sg["x2_stored"].of(old))
                    ln_apply_act(act, sg, 2, st, x1[:, st.s2], x2[:, st.s2])
                if st := at(1):
                    act.wait_ge(*sg["h_turned"].of(st))
                    if old := st.back(2):
                        act.wait_ge(*sg["loop2_done"].of(old))
                    act.activation(h_c[0:D, st.s2], psum[4 + st.s2][0:D, :], ACT.Copy)\
                        .then_inc(sg["h_cols"].sem, 1)
                if st := at(3):
                    ln_root(act, sg, 2, st)
                if st := at(2):
                    ln_root(act, sg, 1, st)

            ticks(act, NG, 4, phase_a)

            sb_ = signals("B")
            xw, hsum, h, y2, x3, res, own2 = row_tiles
            seg, x2_c, g_c, h_c = col_tiles[:4]
            act.wait_ge(s_phase, 2)

            def phase_b(at):
                if st := at(4):
                    act.wait_ge(*sb_["loop2_done"].of(st))
                    if old := st.back(2):
                        act.wait_ge(*sb_["own_part_stored"].of(old))
                    act.activation(own2[:, st.s2], rows_of(6), ACT.Copy).then_inc(sb_["own_part"].sem, 1)
                if st := at(3):
                    act.wait_ge(*sb_["h_turned"].of(st))
                    if old := st.back(2):
                        act.wait_ge(*sb_["loop2_done"].of(old))
                    act.activation(h_c[0:D, st.s2], psum[5][0:D, :], ACT.Copy).then_inc(sb_["h_cols"].sem, 1)
                if st := at(5):
                    if old := st.back(2):
                        act.wait_ge(*sb_["x1_stored"].of(old))
                    ln_apply_act(act, sb_, 1, st, x3[:, st.s2], res[:, st.s2])
                if st := at(3):
                    if old := st.back(2):
                        act.wait_ge(*sb_["ln1_act"].of(old))
                        act.wait_ge(*sb_["x2_stored"].of(old))
                    ln_apply_act(act, sb_, 2, st, y2[:, st.s2], x3[:, st.s2])
                if st := at(4):
                    ln_root(act, sb_, 1, st)
                if st := at(2):
                    act.wait_ge(*sb_["summed"].of(st))
                    if old := st.back(2):
                        act.wait_ge(*sb_["h_turned"].of(old))
                        act.wait_ge(*sb_["conv_stored"].of(old))
                    act.activation(h[:, st.s2], hsum[:, st.s2], ACT.Relu).then_inc(sb_["conv_out"].sem, 1)
                if st := at(1):
                    act.wait_ge(*sb_["mlp1_done"].of(st))
                    if old := st.back(2):
                        act.wait_ge(*sb_["mlp2_done"].of(old))
                    act.activation(g_c[0:D, st.s2], psum[2][0:D, :], ACT.Relu).then_inc(sb_["mlp_hidden"].sem, 1)
                if st := at(0):
                    act.wait_ge(*sb_["x2_turned"].of(st))
                    if old := st.back(2):
                        act.wait_ge(*sb_["mlp1_done"].of(old))
                    act.activation(x2_c[0:D, st.s2], psum[0][0:D, :], ACT.Copy).then_inc(sb_["x2_cols"].sem, 1)
                if st := at(2):
                    ln_root(act, sb_, 2, st)

            ticks(act, NG, 5, phase_b)

            sc = signals("C")
            xw, hsum, half, y1, x1 = row_tiles[:5]
            seg, ea_c, e_c = col_tiles[:3]
            act.wait_ge(s_phase, 3)

            def phase_c(at):
                if st := at(4):
                    if old := st.back(2):
                        act.wait_ge(*sc["x1_stored"].of(old))
                    ln_apply_act(act, sc, 1, st, y1[:, st.s2], x1[:, st.s2])
                if st := at(2):
                    act.wait_ge(*sc["summed"].of(st))
                    if old := st.back(2):
                        act.wait_ge(*sc["y1"].of(old))
                    act.activation(half[:, st.s2], hsum[:, st.s2], ACT.Relu, scale=0.5).then_inc(sc["half"].sem, 1)
                if st := at(1):
                    act.wait_ge(*sc["e_done"].of(st))
                    if old := st.back(2):
                        act.wait_ge(*sc["e_stored"].of(old))
                    act.activation(e_c[0:D, st.s2], psum[4 + st.s2][0:D, :], ACT.Copy)\
                        .then_inc(sc["e_cols"].sem, 1)
                if st := at(3):
                    ln_root(act, sc, 1, st)
                if st := at(0):
                    act.wait_ge(*sc["edge_turned"].of(st))
                    if old := st.back(2):
                        act.wait_ge(*sc["e_done"].of(old))
                    act.activation(ea_c[0:D, st.s2], psum[st.s2][0:D, :], ACT.Copy)\
                        .then_inc(sc["edge_cols"].sem, 1)

            ticks(act, NG, 4, phase_c)

            sd = signals("D")
            x2, y_r = row_tiles[:2]
            xf_c, xs_c, e_c = deep_cols
            sc_c, ex_c, wv_c, z_c, y_c, zg_c = col_tiles
            act.wait_ge(s_phase, 4)

            def phase_d(at):
                if st := at(8):
                    store(st, sd["x1_stored"], sd["ln1_act"], flat(x2[:, st.s2]), x2_t, NG - 1 - st.g)
                if st := at(3):
                    act.wait_ge(*sd["sum_done"].of(st))
                    if old := st.back(2):
                        act.wait_ge(*sd["z_scanned"].of(old))
                        act.wait_ge(*sd["msg"].of(old))
                    act.activation(ex_c[0:D, st.s2], psum[5][0:D, :], ACT.Exp).then_inc(sd["exped"].sem, 1)
                if st := at(7):
                    if old := st.back(2):
                        act.wait_ge(*sd["x1_stored"].of(old))
                    ln_apply_act(act, sd, 1, st, y_r[:, st.s2], x2[:, st.s2])
                if st := at(6):
                    ln_root(act, sd, 1, st)
                if st := at(3):
                    act.wait_ge(*sd["z_scanned"].of(st))
                    if old := st.back(2):
                        act.wait_ge(*sd["attn"].of(old))
                    act.activation(zg_c[0:D, st.s2], z_c[0:D, st.s2], ACT.Copy, bias=1e-6)\
                        .then_inc(sd["z_guarded"].sem, 1)
                if st := at(0):
                    act.wait_ge(*sd["src_turned"].of(st))
                    if old := st.back(DEPTH):
                        act.wait_ge(*sd["v_done"].of(old))
                    act.activation(xs_c[0:D, st.s], psum[0][0:D, :], ACT.Copy).then_inc(sd["src_cols"].sem, 1)

            ticks(act, NG, 8, phase_d)

            se = signals("E")
            y2, x3 = row_tiles[:2]
            seg, rst, g_c = col_tiles[:3]
            act.wait_ge(s_phase, 5)

            def phase_e(at):
                if st := at(5):
                    store(st, se["x1_stored"], se["ln1_act"], flat(x3[:, st.s2]), x3_t, NG - 1 - st.g)
                if st := at(4):
                    if old := st.back(2):
                        act.wait_ge(*se["x1_stored"].of(old))
                    ln_apply_act(act, se, 1, st, y2[:, st.s2], x3[:, st.s2])
                if st := at(3):
                    ln_root(act, se, 1, st)
                if st := at(1):
                    act.wait_ge(*se["mlp1_done"].of(st))
                    if old := st.back(2):
                        act.wait_ge(*se["mlp2_done"].of(old))
                    act.activation(g_c[0:D, st.s2], psum[4 + st.s2][0:D, :], ACT.Relu)\
                        .then_inc(se["mlp_hidden"].sem, 1)

            ticks(act, NG, 5, phase_e)

            sf = signals("F")
            mean = row_tiles[0]
            act.wait_ge(s_phase, 6)

            def phase_f(at):
                if st := at(2):
                    store(st, sf["x1_stored"], sf["conv_out"], flat(mean[:, st.s2]), mean_t[0:EP, :],
                          NG - 1 - st.g)
                if st := at(1):
                    act.wait_ge(*sf["y_turned"].of(st))
                    if old := st.back(2):
                        act.wait_ge(*sf["x1_stored"].of(old))
                    for t in range(T):
                        last = act.activation(mean[:, st.s2, t, :], rows_of(2 + st.s2)[:, t, :], ACT.Copy,
                                              scale=f32(meta[:, st.s, t, INV_DEG:INV_DEG + 1]))
                    last.then_inc(sf["conv_out"].sem, 1)

            ticks(act, NG, 2, phase_f)

            sh = signals("G")
            t1, y2, res = row_tiles[:3]
            act.wait_ge(s_phase, 7)

            def phase_g(at):
                if st := at(2):
                    ln_root(act, sh, 1, st)
                    if old := st.back(2):
                        act.wait_ge(*sh["ids_out"].of(old))
                    ln_apply_act(act, sh, 1, st, y2[:, st.s2], res[:, st.s2])

            ticks(act, NG, 2, phase_g)

        @block.vector
        def _(dve):
            dve.memset(ones[:, :], 1.0).then_inc(s_pads, 1)
            dve.memset(raw[0][:, :], 0).then_inc(s_pads, 1)
            dve.memset(raw[1][:, :], PAD).then_inc(s_pads, 1)
            dve.memset(raw[2][:, :], 0).then_inc(s_pads, 1)
            dve.memset(zero_row[:, :], 0.0)
            dve.memset(eps_col[:, :], EPS)
            dve.memset(ends[:, 0, :], -1)
            dve.memset(ends[:, 1, :], FAR)
            dve.memset(wide_rows[:, :, :, 2 + 2 * D:ROW], 0.0)
            for tile in (*deep_cols, *col_tiles):
                last = dve.memset(tile[D:D + 1, :, :], 1.0)
            last.then_inc(s_pads, 1)

            done = [0]

            def step(ins):
                done[0] += 1
                ins.then_inc(s_prep, 1)
                dve.wait_ge(s_prep, done[0])

            dve.wait_ge(s_raw, 96)
            dve.wait_ge(s_pool_const, 2)
            for i in range(3):
                step(dve.tensor_copy(rec[:, :, i], raw[i][:, :]))
            step(dve.tensor_copy(rec[:, :, 3], slot_no[:, :]))
            cur, before, behind = halo[:, 1:C + 1, 1], halo[:, 0:C, 1], halo[:, 2:C + 2, 1]
            dve.wait_ge(s_halo, 16)
            dve.tensor_tensor(work[0][:, :], cur, before, ALU.is_lt).then_inc(s_disorder, 1)
            dve.wait_ge(s_disorder, 1)
            step(dve.tensor_reduce(small[:, 0:1], work[0][:, :], AX.X, ALU.add))
            dve.wait_ge(s_prep_pe, 1)
            step(dve.tensor_copy(small[:, 1:2], psum[0][:, 0:1]))
            step(dve.tensor_copy(unsorted[:, :], small[:, 1:2]))

            disorder = dve.value_load(unsorted[0:1, 0:1])
            with dve.If(disorder > 0):
                dve.tensor_copy(work[1][:, :], slot_no[:, :])
                dve.memset(work[0][:, :], 1.0)
                dve.tensor_copy(work[2][:, :], raw[1][:, :])
                for chunk in range(CHUNKS):
                    dve.wait_ge(s_rank_in, 16 * (chunk + 1))
                    base = (3 * C + 1) * chunk
                    dve.memset(rank_neg[:, :], -1.0)
                    dve.memset(rank_tmp[:, :], 1.0).then_inc(s_rank, 1)
                    dve.wait_ge(s_rank, base + 1)
                    dve.tensor_tensor_scan(rank_no[:, :], rank_tmp[:, :], rank_neg[:, :],
                                           initial=float(1 - chunk * CH), op0=ALU.mult, op1=ALU.add)\
                        .then_inc(s_rank_no, 1)
                    dve.wait_ge(s_rank_no, chunk + 1)

                    def rank_column(c):
                        k = base + 1 + 3 * c
                        dve.tensor_scalar(rank_tmp[:, :], rank_dst[:, :], work[2][:, bass.ds(c, 1)], float(PAD),
                                          ALU.subtract, ALU.mult).then_inc(s_rank, 1)
                        dve.wait_ge(s_rank, k + 1)
                        dve.scalar_tensor_tensor(rank_tmp[:, :], rank_tmp[:, :], work[1][:, bass.ds(c, 1)],
                                                 rank_no[:, :], ALU.subtract, ALU.is_lt).then_inc(s_rank, 1)
                        dve.wait_ge(s_rank, k + 2)
                        dve.tensor_reduce(rank_sum[:, :], rank_tmp[:, :], AX.X, ALU.add).then_inc(s_rank_sum, 1)
                        dve.wait_ge(s_rank_sum, C * chunk + c + 1)
                        dve.tensor_tensor(work[0][:, bass.ds(c, 1)], work[0][:, bass.ds(c, 1)], rank_sum[:, :],
                                          ALU.add).then_inc(s_rank, 1)
                        dve.wait_ge(s_rank, k + 3)

                    with dve.Fori(0, C) as c:
                        rank_column(c)
                dve.wait_ge(s_rank_done, 1)

            dve.wait_ge(s_sorted, 1)
            same_before, same_behind, first_slot, last_slot = (t[:, :] for t in work)
            m = meta_all
            mf = f32(m[:, :, :])
            no = slot_no[:, :]
            dve.tensor_scalar(m[:, :, SRC], halo[:, 1:C + 1, 0], 2.0, None, ALU.mult)
            dve.tensor_copy(m[:, :, WEIGHT], halo[:, 1:C + 1, 2])
            dve.tensor_scalar(m[:, :, DST], cur, float(N - 1), None, ALU.min)
            dve.tensor_copy(m[:, :, SLOT], no)
            dve.tensor_tensor(mf[:, :, IS_END], cur, behind, ALU.not_equal)
            dve.tensor_tensor(same_before, cur, before, ALU.is_equal)
            step(dve.tensor_tensor(same_behind, cur, behind, ALU.is_equal))
            dve.tensor_copy(flag_tile[:, 0, :], same_before)
            dve.tensor_copy(flag_tile[:, 1, :], same_behind)
            dve.tensor_scalar(first_slot, same_before, -1.0, 1.0, ALU.mult, ALU.add)
            step(dve.tensor_scalar(last_slot, same_behind, -1.0, 1.0, ALU.mult, ALU.add))
            dve.scalar_tensor_tensor(m[:, :, START_DST], cur, float(-FAR), first_slot, ALU.add, ALU.mult)
            step(dve.scalar_tensor_tensor(m[:, :, END_DST], cur, float(-FAR), last_slot, ALU.add, ALU.mult))
            dve.tensor_scalar(m[:, :, START_DST], m[:, :, START_DST], float(FAR), None, ALU.add)
            step(dve.tensor_scalar(m[:, :, END_DST], m[:, :, END_DST], float(FAR), float(ROW // 2), ALU.add, ALU.mult))
            dve.tensor_tensor(same_before, first_slot, no, ALU.mult)
            step(dve.scalar_tensor_tensor(same_behind, no, float(-FAR), last_slot, ALU.add, ALU.mult))
            step(dve.tensor_scalar(same_behind, same_behind, float(FAR), None, ALU.add))
            dve.tensor_tensor_scan(first_slot, same_before, same_before, initial=0.0, op0=ALU.max, op1=ALU.max)
            step(dve.tensor_tensor_scan(backwards(last_slot), backwards(same_behind), backwards(same_behind),
                                        initial=float(FAR), op0=ALU.min, op1=ALU.min))
            step(dve.tensor_copy(small[:, 2:3], first_slot[:, C - 1:C]))
            step(dve.tensor_copy(small[:, 3:4], last_slot[:, 0:1]))
            dve.wait_ge(s_prep_pe, 3)
            dve.tensor_copy(row1[0:1, 0, :], psum[1][0:1, 0:P])
            dve.memset(row1[0:1, 2, 0:1], 0.0)
            dve.memset(row1[0:1, 3, P - 1:P], float(FAR))
            step(dve.tensor_copy(row1[0:1, 1, :], psum[2][0:1, 0:P]))
            step(dve.tensor_tensor_scan(row1[0:1, 2, 1:P], row1[0:1, 0, 0:P - 1], row1[0:1, 0, 0:P - 1],
                                        initial=0.0, op0=ALU.max, op1=ALU.max))
            step(dve.tensor_tensor_scan(backwards(row1[0:1, 3, 0:P - 1]), backwards(row1[0:1, 1, 1:P]),
                                        backwards(row1[0:1, 1, 1:P]), initial=float(FAR), op0=ALU.min,
                                        op1=ALU.min))
            step(dve.memset(small[:, 6:7], 0.0))
            dve.wait_ge(s_prep_pe, 5)
            dve.tensor_copy(small[:, 4:5], psum[3][:, 0:1])
            step(dve.tensor_copy(small[:, 5:6], psum[4][:, 0:1]))
            dve.tensor_scalar(first_slot, first_slot, small[:, 4:5], None, ALU.max)
            step(dve.tensor_scalar(last_slot, last_slot, small[:, 5:6], None, ALU.min))
            dve.tensor_copy(m[:, :, FIRST], first_slot)
            step(dve.scalar_tensor_tensor(same_before, last_slot, 1.0, no, ALU.add, ALU.subtract))
            step(dve.reciprocal(mf[:, :, INV_DEG], same_before))
            step(dve.tensor_scalar(mf[:, :, HALF_INV], mf[:, :, INV_DEG], 0.5, None, ALU.mult))
            assert done[0] == PREP_ALL

            def weigh(s, st, rows, result):
                dve.wait_ge(*s["src_in"].of(st))
                if old := st.back(2):
                    dve.wait_ge(*s["src_turned"].of(old))
                weight = f32(meta[:, st.s, :, WEIGHT:WEIGHT + 1]).to_broadcast([P, T, D])
                dve.tensor_tensor(result[:, st.s2], rows, weight, ALU.mult).then_inc(s["weighted"].sem, 1)

            def scan(s, st, name, result, slot, data, backward, used=None):
                order = backwards if backward else (lambda ap: ap)
                carry = 0 if backward else GR - 1
                initial = 0.0
                if old := st.back(1):
                    dve.wait_ge(*s[name].of(old))
                    initial = result[0:D, slot(old), carry:carry + 1]
                if used:
                    dve.wait_ge(*used)
                dve.tensor_tensor_scan(order(result[0:D, slot(st), :]), order(flag[:, st.s, :]), order(data),
                                       initial=initial, op0=ALU.mult, op1=ALU.add).then_inc(s[name].sem, 1)

            def s2(st):
                return st.s2

            def mix(s, st, own, half, y):
                dve.wait_ge(*s["half"].of(st))
                if old := st.back(2):
                    dve.wait_ge(*(s["ln1_dve"] if s["ln1_act"].per == 2 else s["ln1_act"]).of(old))
                dve.scalar_tensor_tensor(y[:, st.s2], own, 1.5, half[:, st.s2], ALU.mult, ALU.add)\
                    .then_inc(s["y1"].sem, 1)

            sg = signals("A")
            nodes = wide_rows
            half, h, y1, x1, x2 = row_tiles[:5]
            dve.wait_ge(s_phase, 1)

            def phase_a(at):
                for i in range(4):
                    if st := at(4):
                        ln_newton(dve, sg, 2, st, i)
                    if st := at(3):
                        ln_newton(dve, sg, 1, st, i)
                if st := at(3):
                    if old := st.back(2):
                        dve.wait_ge(*sg["x1_stored"].of(old))
                        dve.wait_ge(*sg["ln2_act"].of(old))
                    ln_apply_dve(dve, sg, 1, st, y1[:, st.s2], x1[:, st.s2])
                if st := at(2):
                    mix(sg, st, nodes[:, st.s, :, X_PART], half, y1)
                if st := at(3):
                    dve.wait_ge(*sg["ln1_dve"].of(st))
                    ln_stats(dve, sg, 2, st, x1[:, st.s2])
                if st := at(2):
                    dve.wait_ge(*sg["y1"].of(st))
                    ln_stats(dve, sg, 1, st, y1[:, st.s2])
                if st := at(3):
                    ln_aggr(dve, sg, 2, st)
                if st := at(2):
                    ln_aggr(dve, sg, 1, st)

            ticks(dve, NG, 4, phase_a)

            sb_ = signals("B")
            xw, hsum, h, y2, x3, res, own2 = row_tiles
            x2 = deep_rows[0]
            seg = col_tiles[0]
            dve.wait_ge(s_phase, 2)

            def phase_b(at):
                for i in range(4):
                    if st := at(3):
                        ln_newton(dve, sb_, 2, st, i)
                    if st := at(5):
                        ln_newton(dve, sb_, 1, st, i)
                if st := at(4):
                    dve.wait_ge(*sb_["ln2_act"].of(st))
                    ln_stats(dve, sb_, 1, st, x3[:, st.s2])
                if st := at(2):
                    dve.wait_ge(*sb_["mlp2_done"].of(st))
                    if old := st.back(2):
                        dve.wait_ge(*sb_["ln2_act"].of(old))
                    dve.tensor_tensor(y2[:, st.s2], rows_of(4), x2[:, st.s], ALU.add).then_inc(sb_["y2"].sem, 1)
                if st := at(4):
                    ln_aggr(dve, sb_, 1, st)
                if st := at(2):
                    dve.wait_ge(*sb_["y2"].of(st))
                    ln_stats(dve, sb_, 2, st, y2[:, st.s2])
                    dve.wait_ge(*sb_["own_in"].of(st))
                    dve.wait_ge(*sb_["conv_done"].of(st))
                    if old := st.back(2):
                        dve.wait_ge(*sb_["conv_out"].of(old))
                    dve.tensor_tensor(hsum[:, st.s2], rows_of(3), wide_rows[:, st.s, :, OWN_PART], ALU.add)\
                        .then_inc(sb_["summed"].sem, 1)
                    ln_aggr(dve, sb_, 2, st)
                if st := at(1):
                    dve.wait_ge(*sb_["src_turned"].of(st))
                    dve.wait_ge(*sb_["flags_in"].of(st))
                    old = st.back(2)
                    scan(sb_, st, "scanned", seg, s2, psum[1][0:D, :], False, old and sb_["conv_done"].of(old))
                if st := at(0):
                    q = sb_["ids_made"]
                    dve.wait_ge(*sb_["meta_in"].of(st))
                    weigh(sb_, st, src_rows[:, st.s, :, X_PART], xw)
                    if old := st.back(DEPTH):
                        dve.wait_ge(*sb_["ids_stored"].of(old))
                    places = src_rows[:, st.s, :, 0:2].bitcast(I32)
                    dve.tensor_copy(srcs[:, st.s, :, 0:2], places).then_inc(q.sem, 1)
                    dve.tensor_scalar(srcs[:, st.s, :, 2:4], places[:, :, 1:2].to_broadcast([P, T, 2]),
                                      float(EP), None, ALU.min).then_inc(q.sem, 1)

            ticks(dve, NG, 5, phase_b)

            sc = signals("C")
            hs, own2, x, ea = deep_rows
            xw, hsum, half, y1, x1 = row_tiles[:5]
            dve.wait_ge(s_phase, 3)

            def phase_c(at):
                if st := at(3):
                    mix(sc, st, x[:, st.s], half, y1)
                if st := at(4):
                    for i in range(4):
                        ln_newton(dve, sc, 1, st, i, end_mask[:, st.s, :])
                if st := at(2):
                    dve.wait_ge(*sc["conv_done"].of(st))
                    dve.wait_ge(*sc["x_in"].of(st))
                    if old := st.back(2):
                        dve.wait_ge(*sc["half"].of(old))
                    dve.tensor_tensor(hsum[:, st.s2], rows_of(6 + st.s2), own2[:, st.s], ALU.add)\
                        .then_inc(sc["summed"].sem, 1)
                if st := at(3):
                    dve.wait_ge(*sc["y1"].of(st))
                    ln_stats(dve, sc, 1, st, y1[:, st.s2])
                if st := at(3):
                    ln_aggr(dve, sc, 1, st)
                if st := at(1):
                    dve.wait_ge(*sc["src_turned"].of(st))
                    dve.wait_ge(*sc["flags_in"].of(st))
                    old = st.back(2)
                    scan(sc, st, "scanned", seg, s2, psum[2 + st.s2][0:D, :], False, old and sc["conv_done"].of(old))
                if st := at(0):
                    dve.wait_ge(*sc["meta_in"].of(st))
                    weigh(sc, st, hs[:, st.s], xw)
                    if old := st.back(DEPTH):
                        dve.wait_ge(*sc["ln1_dve"].of(old))
                    dve.tensor_copy(end_mask[:, st.s, :], f32(word(st, IS_END))).then_inc(sc["end_kept"].sem, 1)

            ticks(dve, NG, 4, phase_c)

            sd = signals("D")
            xf_c, xs_c, e_c = deep_cols
            sc_c, ex_c, wv_c, z_c, y_c, zg_c = col_tiles
            y_r = row_tiles[1]
            dve.wait_ge(s_phase, 4)

            def phase_d(at):
                norm, last, sums, score, fill = at(7), at(6), at(3), at(2), at(1)
                if st := last:
                    q = sd["divided"]
                    bank = 6 + st.s2
                    dve.wait_ge(*sd["y_turned"].of(st))
                    dve.tensor_scalar(z_r[:, st.s2, 0], head_rows(bank), 1e-6, None, ALU.add).then_inc(q.sem, 1)
                if st := norm:
                    ln_newton(dve, sd, 1, st, 0)
                if st := fill:
                    dve.wait_ge(*sd["meta_in"].of(st))
                    dve.wait_ge(*sd["own_turned"].of(st))
                    old = st.back(DEPTH)
                    if old:
                        dve.wait_ge(*sd["q_done"].of(old))
                    scan(sd, st, "filled", xf_c, lambda q: q.s, psum[1][0:D, :], True, old and sd["attn"].of(old))
                if st := norm:
                    ln_newton(dve, sd, 1, st, 1)
                if st := last:
                    dve.wait_ge(*q.of(st, 1))
                    dve.reciprocal(z_r[:, st.s2, 1], z_r[:, st.s2, 0]).then_inc(q.sem, 1)
                if st := norm:
                    ln_newton(dve, sd, 1, st, 2)
                if st := score:
                    dve.wait_ge(*sd["edge_in"].of(st))
                    dve.wait_ge(*sd["k_done"].of(st))
                    if old := st.back(2):
                        dve.wait_ge(*sd["scanned"].of(old))
                    dve.tensor_tensor(sc_c[0:D, st.s2], psum[2][0:D, :], e_c[0:D, st.s], ALU.mult)\
                        .then_inc(sd["score"].sem, 1)
                if st := norm:
                    ln_newton(dve, sd, 1, st, 3)
                if st := last:
                    dve.wait_ge(*q.of(st, 2))
                    if old := st.back(2):
                        dve.wait_ge(*sd["ln1_act"].of(old))
                    dve.tensor_tensor(y_r[:, st.s2].rearrange("p t (h c) -> p (t h) c", c=HD),
                                      psum[bank][:, 0:T * D].rearrange("p (n c) -> p n c", c=HD),
                                      z_r[:, st.s2, 1].rearrange("p t h -> p (t h)").unsqueeze(2)
                                      .to_broadcast([P, T * HEADS, HD]), ALU.mult).then_inc(q.sem, 1)
                if st := score:
                    dve.wait_ge(*sd["score"].of(st, 1))
                    dve.wait_ge(*sd["q_done"].of(st))
                    dve.tensor_tensor(sc_c[0:D, st.s2], sc_c[0:D, st.s2], psum[3][0:D, :], ALU.mult)\
                        .then_inc(sd["score"].sem, 1)
                if st := last:
                    dve.wait_ge(*q.of(st))
                    ln_stats(dve, sd, 1, st, y_r[:, st.s2])
                if st := sums:
                    dve.wait_ge(*sd["exped"].of(st))
                    dve.tensor_scalar(ex_c[0:D, st.s2], ex_c[0:D, st.s2], math.exp(-5.0), math.exp(5.0), ALU.max,
                                      ALU.min).then_inc(sd["clipped"].sem, 1)
                if st := last:
                    ln_aggr(dve, sd, 1, st)
                if st := sums:
                    dve.wait_ge(*sd["v_done"].of(st))
                    dve.wait_ge(*sd["clipped"].of(st))
                    dve.wait_ge(*sd["sum_done"].of(st))
                    dve.tensor_tensor(sc_c[0:D, st.s2], psum[4][0:D, :], ex_c[0:D, st.s2], ALU.mult)\
                        .then_inc(sd["msg"].sem, 1)
                    old = st.back(2)
                    scan(sd, st, "z_scanned", z_c, s2, ex_c[0:D, st.s2], True, old and sd["y_turned"].of(old))
                if st := sums:
                    dve.wait_ge(*sd["msg"].of(st))
                    old = st.back(2)
                    scan(sd, st, "scanned", wv_c, s2, sc_c[0:D, st.s2], True, old and sd["attn"].of(old))

            ticks(dve, NG, 7, phase_d)

            se = signals("E")
            xs, xo = deep_rows[:2]
            y2, x3 = row_tiles[:2]
            seg, rst, g_c = col_tiles[:3]
            dve.wait_ge(s_phase, 5)

            def phase_e(at):
                if st := at(3):
                    dve.wait_ge(*se["mlp2_done"].of(st))
                    if old := st.back(2):
                        dve.wait_ge(*se["ln1_act"].of(old))
                    dve.tensor_tensor(y2[:, st.s2], rows_of(6 + st.s2), xo[:, st.s], ALU.add)\
                        .then_inc(se["y2"].sem, 1)
                if st := at(4):
                    for i in (0, 1):
                        ln_newton(dve, se, 1, st, i)
                if st := at(1):
                    dve.wait_ge(*se["meta_in"].of(st))
                    dve.wait_ge(*se["src_turned"].of(st))
                    old = st.back(2)
                    scan(se, st, "scanned", seg, s2, psum[st.s2][0:D, :], True, old and se["rst"].of(old))
                if st := at(4):
                    for i in (2, 3):
                        ln_newton(dve, se, 1, st, i)
                if st := at(3):
                    dve.wait_ge(*se["y2"].of(st))
                    ln_stats(dve, se, 1, st, y2[:, st.s2])
                if st := at(1):
                    dve.wait_ge(*se["scanned"].of(st))
                    if old := st.back(2):
                        dve.wait_ge(*se["mlp1_done"].of(old))
                    dve.tensor_tensor(rst[0:D, st.s2], psum[2 + st.s2][0:D, :], seg[0:D, st.s2], ALU.add)\
                        .then_inc(se["rst"].sem, 1)
                if st := at(3):
                    ln_aggr(dve, se, 1, st)

            ticks(dve, NG, 4, phase_e)

            sf = signals("F")
            dve.wait_ge(s_phase, 6)

            def phase_f(at):
                st = at(0)
                dve.wait_ge(*sf["meta_in"].of(st))
                dve.wait_ge(*sf["src_turned"].of(st))
                old = st.back(2)
                scan(sf, st, "scanned", seg, s2, psum[st.s2][0:D, :], True, old and sf["y_turned"].of(old))

            ticks(dve, NG, 0, phase_f)

            sh = signals("G")
            xs, xo, mo = deep_rows[:3]
            t1, y2, res = row_tiles[:3]
            dve.wait_ge(s_phase, 7)

            def phase_g(at):
                if st := at(2):
                    dve.wait_ge(*sh["y_turned"].of(st))
                    dve.wait_ge(*sh["index_in"].of(st))
                    if old := st.back(2):
                        dve.wait_ge(*sh["ln1_act"].of(old))
                    dve.wait_ge(*sh["x_in"].of(st))
                    dve.scalar_tensor_tensor(t1[:, st.s2], mo[:, st.s], 0.5, xo[:, st.s], ALU.mult, ALU.add)\
                        .then_inc(sh["y1"].sem, 1)
                    dve.wait_ge(*sh["y1"].of(st))
                    for t in range(T):
                        last = dve.scalar_tensor_tensor(y2[:, st.s2, t, :], rows_of(2 + st.s2)[:, t, :],
                                                        f32(meta[:, st.s, t, HALF_INV:HALF_INV + 1]),
                                                        t1[:, st.s2, t, :], ALU.mult, ALU.add)
                    last.then_inc(sh["y2"].sem, 1)
                    dve.wait_ge(*sh["y2"].of(st))
                    ln_stats(dve, sh, 1, st, y2[:, st.s2])
                    ln_aggr(dve, sh, 1, st)
                if st := at(0):
                    dve.wait_ge(*sh["meta_in"].of(st))
                    dve.wait_ge(*sh["src_turned"].of(st))
                    old = st.back(2)
                    scan(sh, st, "scanned", seg, s2, psum[st.s2][0:D, :], True, old and sh["y_turned"].of(old))
                if st := at(2):
                    for i in range(4):
                        ln_newton(dve, sh, 1, st, i)

            ticks(dve, NG, 2, phase_g)


PREP_ALL = 25

_INS = ["x", "src", "dst", "edge_attr_96", "edge_weight", "L0_gnn_W1", "L0_gnn_W1_loop", "L0_gnn_b1", "L0_gnn_W2",
        "L0_gnn_W2_loop", "L0_gnn_b2", "L1_gnn_Wq", "L1_gnn_bq", "L1_gnn_Wk", "L1_gnn_bk", "L1_gnn_We",
        "L1_gnn_be", "L1_gnn_Wv", "L1_gnn_bv", "L2_gnn_W1", "L2_gnn_b1", "L2_gnn_W2", "L2_gnn_b2"]


def kernel(**inputs):
    import numpy as _np
    import concourse.bacc as _bacc
    from concourse import mybir as _mybir
    from concourse.bass_utils import run_bass_kernel_spmd as _run

    nc = _bacc.Bacc("TRN2", target_bir_lowering=False, num_devices=1)
    arrays, args = {}, {}
    for name in _INS:
        v = _np.ascontiguousarray(inputs[name])
        arrays[f"in_{name}_dram"] = v
        args[name] = nc.dram_tensor(f"in_{name}_dram", v.shape, _mybir.dt.from_np(v.dtype), kind="ExternalInput").ap()
    out = nc.dram_tensor("out_0_dram", inputs["x"].shape, _mybir.dt.float32, kind="ExternalOutput").ap()
    gnn_kernel(nc, args, out)
    r = _run(nc, [arrays], core_ids=[0])
    return r.results[0]["out_0_dram"]
```
